# Optimizing a Trainium2 kernel written in Bass

```python
import numpy as np
import jax
import jax.numpy as jnp

def _softmax(x, axis=-1):
    return jax.nn.softmax(x, axis=axis)

def _gelu(x):
    return jax.nn.gelu(x, approximate=True)

def _silu(x):
    return jax.nn.silu(x)

def _sigmoid(x):
    return jax.nn.sigmoid(x)

def _layernorm(x, axis=-1, eps=1e-05):
    m = jnp.mean(x, axis=axis, keepdims=True)
    v = jnp.var(x, axis=axis, keepdims=True)
    return (x - m) / jnp.sqrt(v + eps)

def _scatter_add(tgt, idx, src, axis=0):
    return tgt.at[idx].add(src)

def _segment_sum(src, seg, n):
    return jax.ops.segment_sum(src, seg, n)
kernel_name = 'mk_macaron_d1_jaxref_r4_e87e2b'

def setup_inputs(seed: int=0):
    np.random.seed(seed)
    _w = jnp.asarray

    def _L0_attn_setup():
        import jax, jax.numpy as jnp
        import numpy as np
        B, S, E = (2, 1024, 256)
        H, DQK, DV = (16, 64, 64)
        ROPE_BASE = 10000.0

        def _rope(t):
            D = t.shape[-1]
            inv_freq = 1.0 / ROPE_BASE ** (jnp.arange(0, D, 2, dtype=jnp.float32) / D)
            pos = jnp.arange(t.shape[2], dtype=jnp.float32)
            ang = pos[:, None] * inv_freq[None, :]
            cos = jnp.cos(ang)[None, None]
            sin = jnp.sin(ang)[None, None]
            t1, t2 = (t[..., :D // 2], t[..., D // 2:])
            return jnp.concatenate([t1 * cos - t2 * sin, t1 * sin + t2 * cos], axis=-1)
        key = jax.random.key(seed)
        ks = jax.random.split(key, 4)
        sE = 1.0 / np.sqrt(E)
        sV = 1.0 / np.sqrt(H * DV)
        return {'x': jax.random.normal(ks[0], (B, S, E), jnp.float32), 'Wq': jax.random.normal(ks[1], (E, H * DQK), jnp.float32) * sE, 'bq': jnp.zeros((H * DQK,), jnp.float32), 'Wkv': jax.random.normal(ks[2], (E, H * (DQK + DV)), jnp.float32) * sE, 'bkv': jnp.zeros((H * (DQK + DV),), jnp.float32), 'Wo': jax.random.normal(ks[3], (H * DV, E), jnp.float32) * sV, 'bo': jnp.zeros((E,), jnp.float32)}
    _L0_attn_in = _L0_attn_setup()

    def _L0_ffn_setup():
        import jax, jax.numpy as jnp
        import numpy as np
        B, L, D = (4, 512, 256)
        H = 16
        E = 16
        NS = 16
        S = NS // E
        F = 1024
        EPS = 1e-05

        def _layernorm(x, g, b):
            mu = jnp.mean(x, axis=-1, keepdims=True)
            var = jnp.mean(jnp.square(x - mu), axis=-1, keepdims=True)
            return (x - mu) * jax.lax.rsqrt(var + EPS) * g + b

        def _mha(q, k, v, Wq, bq, Wk, bk, Wv, bv, Wo, bo):
            Bq, Lq, Dm = q.shape
            dh = Dm // H
            qh = (q @ Wq + bq).reshape(Bq, Lq, H, dh)
            kh = (k @ Wk + bk).reshape(Bq, -1, H, dh)
            vh = (v @ Wv + bv).reshape(Bq, -1, H, dh)
            scores = jnp.einsum('bqhd,bkhd->bhqk', qh, kh) / jnp.asarray(np.sqrt(dh), q.dtype)
            attn = jax.nn.softmax(scores, axis=-1)
            out = jnp.einsum('bhqk,bkhd->bqhd', attn, vh).reshape(Bq, Lq, Dm)
            return out @ Wo + bo
        key = jax.random.key(seed)
        ks = jax.random.split(key, 32)
        s = 0.02
        d = {}
        d['x'] = jax.random.normal(ks[0], (B, L, D), jnp.float32)
        d['slot_query'] = jax.random.normal(ks[1], (1, NS, D), jnp.float32) * 0.01
        for i, nm in enumerate(['d_Wq', 'd_Wk', 'd_Wv', 'd_Wo']):
            d[nm] = jax.random.normal(ks[2 + i], (D, D), jnp.float32) * s
        for nm in ['d_bq', 'd_bk', 'd_bv', 'd_bo']:
            d[nm] = jnp.zeros((D,), jnp.float32)
        for i, nm in enumerate(['c_Wq', 'c_Wk', 'c_Wv', 'c_Wo']):
            d[nm] = jax.random.normal(ks[6 + i], (D, D), jnp.float32) * s
        for nm in ['c_bq', 'c_bk', 'c_bv', 'c_bo']:
            d[nm] = jnp.zeros((D,), jnp.float32)
        d['e_ln_g'] = jnp.ones((E, D), jnp.float32)
        d['e_ln_b'] = jnp.zeros((E, D), jnp.float32)
        d['e_W1'] = jax.random.normal(ks[10], (E, D, F), jnp.float32) * s
        d['e_b1'] = jnp.zeros((E, F), jnp.float32)
        d['e_Wg'] = jax.random.normal(ks[11], (E, D, F), jnp.float32) * s
        d['e_bg'] = jnp.zeros((E, F), jnp.float32)
        d['e_W2'] = jax.random.normal(ks[12], (E, F, D), jnp.float32) * s
        d['e_b2'] = jnp.zeros((E, D), jnp.float32)
        return d
    _L0_ffn_in = _L0_ffn_setup()
    _d = {'L0_attn_x': _L0_attn_in['x'], 'L0_attn_Wq': _L0_attn_in['Wq'], 'L0_attn_bq': _L0_attn_in['bq'], 'L0_attn_Wkv': _L0_attn_in['Wkv'], 'L0_attn_bkv': _L0_attn_in['bkv'], 'L0_attn_Wo': _L0_attn_in['Wo'], 'L0_attn_bo': _L0_attn_in['bo'], 'L0_ffn_slot_query': _L0_ffn_in['slot_query'], 'L0_ffn_d_Wq': _L0_ffn_in['d_Wq'], 'L0_ffn_d_Wk': _L0_ffn_in['d_Wk'], 'L0_ffn_d_Wv': _L0_ffn_in['d_Wv'], 'L0_ffn_d_Wo': _L0_ffn_in['d_Wo'], 'L0_ffn_d_bq': _L0_ffn_in['d_bq'], 'L0_ffn_d_bk': _L0_ffn_in['d_bk'], 'L0_ffn_d_bv': _L0_ffn_in['d_bv'], 'L0_ffn_d_bo': _L0_ffn_in['d_bo'], 'L0_ffn_c_Wq': _L0_ffn_in['c_Wq'], 'L0_ffn_c_Wk': _L0_ffn_in['c_Wk'], 'L0_ffn_c_Wv': _L0_ffn_in['c_Wv'], 'L0_ffn_c_Wo': _L0_ffn_in['c_Wo'], 'L0_ffn_c_bq': _L0_ffn_in['c_bq'], 'L0_ffn_c_bk': _L0_ffn_in['c_bk'], 'L0_ffn_c_bv': _L0_ffn_in['c_bv'], 'L0_ffn_c_bo': _L0_ffn_in['c_bo'], 'L0_ffn_e_ln_g': _L0_ffn_in['e_ln_g'], 'L0_ffn_e_ln_b': _L0_ffn_in['e_ln_b'], 'L0_ffn_e_W1': _L0_ffn_in['e_W1'], 'L0_ffn_e_b1': _L0_ffn_in['e_b1'], 'L0_ffn_e_Wg': _L0_ffn_in['e_Wg'], 'L0_ffn_e_bg': _L0_ffn_in['e_bg'], 'L0_ffn_e_W2': _L0_ffn_in['e_W2'], 'L0_ffn_e_b2': _L0_ffn_in['e_b2']}
    _x0 = _d['L0_attn_x']
    _d['L0_attn_x'] = jax.random.normal(jax.random.fold_in(jax.random.key(seed), 1), (16, 512, 256), dtype=_x0.dtype)
    del _x0
    return _d

def reference(L0_attn_x, L0_attn_Wq, L0_attn_bq, L0_attn_Wkv, L0_attn_bkv, L0_attn_Wo, L0_attn_bo, L0_ffn_slot_query, L0_ffn_d_Wq, L0_ffn_d_Wk, L0_ffn_d_Wv, L0_ffn_d_Wo, L0_ffn_d_bq, L0_ffn_d_bk, L0_ffn_d_bv, L0_ffn_d_bo, L0_ffn_c_Wq, L0_ffn_c_Wk, L0_ffn_c_Wv, L0_ffn_c_Wo, L0_ffn_c_bq, L0_ffn_c_bk, L0_ffn_c_bv, L0_ffn_c_bo, L0_ffn_e_ln_g, L0_ffn_e_ln_b, L0_ffn_e_W1, L0_ffn_e_b1, L0_ffn_e_Wg, L0_ffn_e_bg, L0_ffn_e_W2, L0_ffn_e_b2):

    def _L0_attn_ref(x, Wq, bq, Wkv, bkv, Wo, bo):
        import jax, jax.numpy as jnp
        import numpy as np
        B, S, E = (2, 1024, 256)
        H, DQK, DV = (16, 64, 64)
        ROPE_BASE = 10000.0

        def _rope(t):
            D = t.shape[-1]
            inv_freq = 1.0 / ROPE_BASE ** (jnp.arange(0, D, 2, dtype=jnp.float32) / D)
            pos = jnp.arange(t.shape[2], dtype=jnp.float32)
            ang = pos[:, None] * inv_freq[None, :]
            cos = jnp.cos(ang)[None, None]
            sin = jnp.sin(ang)[None, None]
            t1, t2 = (t[..., :D // 2], t[..., D // 2:])
            return jnp.concatenate([t1 * cos - t2 * sin, t1 * sin + t2 * cos], axis=-1)
        b, s, e = x.shape
        q = x @ Wq + bq
        kv = x @ Wkv + bkv
        k, v = jnp.split(kv, [H * DQK], axis=-1)
        q = _rope(q.reshape(b, s, H, DQK).transpose(0, 2, 1, 3))
        k = _rope(k.reshape(b, s, H, DQK).transpose(0, 2, 1, 3))
        v = v.reshape(b, s, H, DV).transpose(0, 2, 1, 3)
        scores = jnp.einsum('bhqd,bhkd->bhqk', q, k) * (1.0 / np.sqrt(DQK))
        causal = jnp.tril(jnp.ones((s, s), dtype=bool))
        scores = jnp.where(causal[None, None], scores, -jnp.inf)
        probs = jax.nn.softmax(scores, axis=-1)
        out = jnp.einsum('bhqk,bhkd->bhqd', probs, v)
        out = out.transpose(0, 2, 1, 3).reshape(b, s, H * DV)
        return out @ Wo + bo

    def _L0_ffn_ref(x, slot_query, d_Wq, d_Wk, d_Wv, d_Wo, d_bq, d_bk, d_bv, d_bo, c_Wq, c_Wk, c_Wv, c_Wo, c_bq, c_bk, c_bv, c_bo, e_ln_g, e_ln_b, e_W1, e_b1, e_Wg, e_bg, e_W2, e_b2):
        import jax, jax.numpy as jnp
        import numpy as np
        B, L, D = (4, 512, 256)
        H = 16
        E = 16
        NS = 16
        S = NS // E
        F = 1024
        EPS = 1e-05

        def _layernorm(x, g, b):
            mu = jnp.mean(x, axis=-1, keepdims=True)
            var = jnp.mean(jnp.square(x - mu), axis=-1, keepdims=True)
            return (x - mu) * jax.lax.rsqrt(var + EPS) * g + b

        def _mha(q, k, v, Wq, bq, Wk, bk, Wv, bv, Wo, bo):
            Bq, Lq, Dm = q.shape
            dh = Dm // H
            qh = (q @ Wq + bq).reshape(Bq, Lq, H, dh)
            kh = (k @ Wk + bk).reshape(Bq, -1, H, dh)
            vh = (v @ Wv + bv).reshape(Bq, -1, H, dh)
            scores = jnp.einsum('bqhd,bkhd->bhqk', qh, kh) / jnp.asarray(np.sqrt(dh), q.dtype)
            attn = jax.nn.softmax(scores, axis=-1)
            out = jnp.einsum('bhqk,bkhd->bqhd', attn, vh).reshape(Bq, Lq, Dm)
            return out @ Wo + bo
        Bx = x.shape[0]
        q = jnp.broadcast_to(slot_query, (Bx, NS, D))
        o = q + _mha(q, x, x, d_Wq, d_bq, d_Wk, d_bk, d_Wv, d_bv, d_Wo, d_bo)
        os = o.reshape(Bx, E, S, D)
        h = _layernorm(os, e_ln_g[None, :, None, :], e_ln_b[None, :, None, :])
        u = jax.nn.silu(jnp.einsum('besd,edf->besf', h, e_W1) + e_b1[None, :, None, :])
        g = jax.nn.silu(jnp.einsum('besd,edf->besf', h, e_Wg) + e_bg[None, :, None, :])
        y = jnp.einsum('besf,efd->besd', u * g, e_W2) + e_b2[None, :, None, :]
        o = o + y.reshape(Bx, NS, D)
        out = _mha(x, o, o, c_Wq, c_bq, c_Wk, c_bk, c_Wv, c_bv, c_Wo, c_bo)
        return out
    x = L0_attn_x
    x = x + 0.5 * _L0_ffn_ref(_layernorm(x, axis=-1), L0_ffn_slot_query, L0_ffn_d_Wq, L0_ffn_d_Wk, L0_ffn_d_Wv, L0_ffn_d_Wo, L0_ffn_d_bq, L0_ffn_d_bk, L0_ffn_d_bv, L0_ffn_d_bo, L0_ffn_c_Wq, L0_ffn_c_Wk, L0_ffn_c_Wv, L0_ffn_c_Wo, L0_ffn_c_bq, L0_ffn_c_bk, L0_ffn_c_bv, L0_ffn_c_bo, L0_ffn_e_ln_g, L0_ffn_e_ln_b, L0_ffn_e_W1, L0_ffn_e_b1, L0_ffn_e_Wg, L0_ffn_e_bg, L0_ffn_e_W2, L0_ffn_e_b2)
    x = x + _L0_attn_ref(_layernorm(x, axis=-1), L0_attn_Wq, L0_attn_bq, L0_attn_Wkv, L0_attn_bkv, L0_attn_Wo, L0_attn_bo)
    x = x + 0.5 * _L0_ffn_ref(_layernorm(x, axis=-1), L0_ffn_slot_query, L0_ffn_d_Wq, L0_ffn_d_Wk, L0_ffn_d_Wv, L0_ffn_d_Wo, L0_ffn_d_bq, L0_ffn_d_bk, L0_ffn_d_bv, L0_ffn_d_bo, L0_ffn_c_Wq, L0_ffn_c_Wk, L0_ffn_c_Wv, L0_ffn_c_Wo, L0_ffn_c_bq, L0_ffn_c_bk, L0_ffn_c_bv, L0_ffn_c_bo, L0_ffn_e_ln_g, L0_ffn_e_ln_b, L0_ffn_e_W1, L0_ffn_e_b1, L0_ffn_e_Wg, L0_ffn_e_bg, L0_ffn_e_W2, L0_ffn_e_b2)
    return x

_drawn_inputs = setup_inputs


def setup_inputs(seed=0):
    import zlib

    import numpy as np

    out = dict(_drawn_inputs(seed))
    spreads = {'L0_attn_bq': (0.0, 0.59),
     'L0_attn_bkv': (0.0, 0.1),
     'L0_attn_bo': (0.0, 0.1),
     'L0_ffn_d_bq': (0.0, 0.8),
     'L0_ffn_d_bk': (0.0, 0.8),
     'L0_ffn_d_bv': (0.0, 0.8),
     'L0_ffn_d_bo': (0.0, 0.72),
     'L0_ffn_c_bq': (0.0, 0.8),
     'L0_ffn_c_bk': (0.0, 0.8),
     'L0_ffn_c_bv': (0.0, 0.1),
     'L0_ffn_c_bo': (0.0, 0.1),
     'L0_ffn_e_ln_g': (1.0, 0.6),
     'L0_ffn_e_ln_b': (0.0, 0.8),
     'L0_ffn_e_b1': (0.0, 0.8),
     'L0_ffn_e_bg': (0.0, 0.8),
     'L0_ffn_e_b2': (0.0, 0.8)}
    factors = {'L0_ffn_slot_query': 8.0,
     'L0_ffn_d_Wq': 8.0,
     'L0_ffn_d_Wk': 8.0,
     'L0_ffn_d_Wv': 8.0,
     'L0_ffn_d_Wo': 8.0,
     'L0_ffn_c_Wq': 8.0,
     'L0_ffn_c_Wk': 8.0,
     'L0_ffn_c_Wv': 4.481,
     'L0_ffn_e_W1': 8.0,
     'L0_ffn_e_Wg': 8.0,
     'L0_ffn_e_W2': 8.0}
    for name, (base, spread) in spreads.items():
        noise = np.random.default_rng([zlib.crc32(name.encode()), seed]).standard_normal(out[name].shape)
        drawn = base * np.exp(spread * noise) if base else spread * noise
        out[name] = jnp.asarray(drawn.astype(out[name].dtype))
    for name, factor in factors.items():
        out[name] = (out[name] * factor).astype(out[name].dtype)
    return out
```

```python
from contextlib import ExitStack

import numpy as np

import concourse.bass as bass
from concourse import mybir

F32 = mybir.dt.float32
F32R = mybir.dt.float32r
BF16 = mybir.dt.bfloat16
ALU = mybir.AluOpType
ACT = mybir.ActivationFunctionType
AX = mybir.AxisListType

P = 128
B, S, D = 16, 512, 256
TT = S // P
DC = D // P
FH, FDH = 16, 16
NS = 16
HS = FH * NS
HPC = P // FDH
NE, F = 16, 1024
FK = F // P
AH, ADH = 16, 64
AW = AH * ADH
PAIRS = AH // 2
QUAD = 32
EPS = 1e-5
MASKED = -3.0e38


class Count:

    def __init__(self, sem, per, credit=0):
        self.sem, self.per, self.credit = sem, per, credit

    def at(self, j, n):
        assert n + self.credit >= 1 or not isinstance(j, int) or j * self.per + n + self.credit >= 1
        return j * self.per + (n + self.credit)


def hold(g, eng, sem, value):
    eng.wait_ge(sem, value)
    eng.sem_inc(g.held, 1)


def bcast(ap, axis, n):
    shape = list(ap.shape)
    return ap.unsqueeze(axis).broadcast_to(shape[:axis] + [n] + shape[axis:])


def setup_phase(nc, io, g, sem):
    loaded = sem("setup_loaded")
    q_mm, q_done, blk_done, g_mm, g_done, zeroed, scaled = (
        sem(f"setup_{n}") for n in ("q_mm", "q_done", "blk_done", "g_mm", "g_done", "zeroed", "scaled"))
    LOADS = 12 + 4
    with ExitStack() as s:
        sb = lambda n, sh: s.enter_context(nc.sbuf_tensor(n, sh, F32))
        wq, wkT = sb("su_wq", [P, DC, D]), sb("su_wkT", [P, DC, D])
        sqT, bq, bk = sb("su_sqT", [P, DC, NS]), sb("su_bq", [P, DC]), sb("su_bk", [P, DC])
        qT, qblk = sb("su_qT", [P, DC, NS]), sb("su_qblk", [P, DC, HPC, NS])
        ps_q = s.enter_context(nc.psum_tensor("su_psq", [P, DC, NS], F32))
        ps_g = s.enter_context(nc.psum_tensor("su_psg", [P, DC, HS], F32))
        ps_c = s.enter_context(nc.psum_tensor("su_psc", [P, DC, 2], F32))
        block = s.enter_context(nc.Block())

        @block.sync
        def _(sp):
            sp.wait_ge(zeroed, 2)
            for dst, src in (
                (g.ident[:], io["ident"]), (g.blkmask[:], io["blkmask"]),
                (wq[:], io["d_Wq"].rearrange("(c p) n -> p c n", p=P)),
                (wkT[:], io["d_WkT"].rearrange("(c p) n -> p c n", p=P)),
                (sqT[:], io["sqT"]), (bq[:], io["d_bq"]), (bk[:], io["d_bk"]),
                *((g.wv_pad[:, c, :, 0:FDH], io["d_Wv"].rearrange("(c p) (h e) -> c p h e", p=P, e=FDH)[c]) for c in range(DC)),
                (g.bv_pad[:], io["d_bv_pad"]),
                (g.cwqT[:], io["c_WqT"].rearrange("(c p) n -> p c n", p=P)),
                (g.cwo[:], io["c_Wo"].rearrange("(c p) n -> p c n", p=P)),
            ):
                sp.dma_start(dst, src).then_inc(loaded, 16)
            for q in range(4):
                sp.dma_start(g.wo_pad[q * QUAD:q * QUAD + FDH, :, :],
                             io["d_Wo"].rearrange("(t q e) n -> q e t n", q=4, e=FDH)[q]).then_inc(loaded, 16)

        @block.vector
        def _(dve):
            nc.vector.memset(g.wv_pad[:], 0.0).then_inc(zeroed, 1)
            nc.vector.memset(g.wo_pad[:], 0.0).then_inc(zeroed, 1)
            dve.wait_ge(q_mm, 1)
            for c in range(DC):
                nc.vector.tensor_scalar(qT[:, c, :], ps_q[:, c, :], bq[:, c:c + 1], FDH ** -0.5,
                                        ALU.add, ALU.mult).then_inc(q_done, 1)
            dve.wait_ge(q_done, DC)
            for c in range(DC):
                nc.vector.tensor_tensor(qblk[:, c], g.blkmask[:].rearrange("p (h s) -> p h s", s=NS),
                                        bcast(qT[:, c, :], 1, HPC), ALU.mult).then_inc(blk_done, 1)
            dve.wait_ge(g_mm, 1)
            nc.vector.tensor_copy(g.G[:], ps_g[:]).then_inc(g_done, 1)
            nc.vector.tensor_copy(g.cb[:], ps_c[:, :, 0]).then_inc(g_done, 1)

        @block.tensor
        def _(pe):
            pe.wait_ge(loaded, 16 * LOADS)
            for m in range(DC):
                for c in range(DC):
                    last = nc.tensor.matmul(ps_q[:, m, :], wq[:, c, m * P:(m + 1) * P], sqT[:, c, :],
                                            start=(c == 0), stop=(c == DC - 1))
            last.then_inc(q_mm, 1)
            pe.wait_ge(blk_done, DC)
            for m in range(DC):
                for c in range(DC):
                    nc.tensor.matmul(ps_g[:, m, c * P:(c + 1) * P], wkT[:, c, m * P:(m + 1) * P],
                                     qblk[:, c].rearrange("p h s -> p (h s)"), start=True, stop=True)
            for c in range(DC):
                last = nc.tensor.matmul(ps_c[:, c, 0:1], qblk[:, c].rearrange("p h s -> p (h s)"),
                                        bk[:, c:c + 1], start=True, stop=True)
            last.then_inc(g_mm, 1)


def layernorm_stats(nc, g, dve, x, stats, mv, tiles, stats_sem, mom_sem, j):
    for i in range(tiles):
        nc.vector.bn_stats(stats[:, i, :], x[:, i, :]).then_inc(stats_sem.sem, 1)
    hold(g, dve, stats_sem.sem, stats_sem.at(j, tiles))
    for i in range(tiles):
        nc.vector.bn_aggr(mv[:, i, :], stats[:, i, :]).then_inc(mom_sem.sem, 1)


def layernorm_rstd(nc, g, pool, mv, veps, rstd, tiles, mom_sem, veps_sem, rstd_sem, j):
    hold(g, pool, mom_sem.sem, mom_sem.at(j, tiles))
    nc.gpsimd.tensor_scalar(veps[:, 0:tiles], mv[:, 0:tiles, 1], EPS, None, ALU.add).then_inc(veps_sem.sem, 1)
    pool.wait_ge(veps_sem.sem, veps_sem.at(j, 1))
    nc.gpsimd.tensor_tensor(rstd[:, 0:tiles], veps[:, 0:tiles], g.mhalf[:, 0:tiles], ALU.pow).then_inc(rstd_sem.sem, 1)


def dispatch_phase(nc, g, sem, f, x_dram, at_all):
    n = lambda x: f"dis_{x}"
    name = lambda x: f"dis{f}_{x}"
    x_in = [sem(n(f"x_in{i}")) for i in range(2)]
    c = lambda x, per: Count(sem(n(x)), per)
    stats_s, mom_s, veps_s, rstd_s, xn_s = c("stats", TT), c("moments", TT), c("veps", 1), c("rstd", 1), c("xn", TT)
    xt_mm, xt_s = c("xt_mm", DC), c("xt", DC)
    score_mm, max_s, bias_s, exp_s, recip_s, p_s = (
        c("score_mm", DC), c("max", DC), c("bias", DC), c("exp", DC), c("recip", 1), c("p", DC))
    pt_mm, pt_s, at_mm, at_s = c("pt_mm", 2), c("pt", 2), c("at_mm", 1), c("at", 1)
    with ExitStack() as s:
        sb = lambda nm, sh: s.enter_context(nc.sbuf_tensor(name(nm), sh, F32))
        pb = lambda nm, sh: s.enter_context(nc.psum_tensor(name(nm), sh, F32))
        xin, xn = sb("b_x", [P, 2, TT, D]), sb("b_xn", [P, 2, TT, D])
        stats, mv = sb("b_stats", [P, TT, 6]), sb("b_mv", [P, TT, 2])
        veps, rstd = sb("b_veps", [P, TT]), sb("b_rstd", [P, TT])
        xnT = sb("b_xnT", [P, DC, S])
        nmax, ebias, sums, rinv = (sb(x, [P, DC]) for x in ("b_nmax", "b_ebias", "b_sums", "b_rinv"))
        prob, probT = sb("b_prob", [P, 2, DC, S]), sb("b_probT", [P, TT, HS])
        ps_xt, ps_s = pb("ps_xt", [P, DC, S]), pb("ps_s", [P, DC, S])
        ps_pt, ps_at = pb("ps_pt", [P, TT, HS]), pb("ps_at", [P, DC, HS])
        block = s.enter_context(nc.Block())

        @block.sync
        def _(sp):
            def load(j, par):
                sp.dma_start(xin[:, par], x_dram[j].rearrange("(i p) d -> p i d", p=P)).then_inc(x_in[par], 16)

            load(0, 0)
            load(1, 1)
            with sp.Fori(0, B // 2 - 1) as k:
                for par in range(2):
                    hold(g, sp, xn_s.sem, xn_s.at(2 * k + par, TT))
                    load(2 * k + 2 + par, par)

        @block.vector
        def _(dve):
            def moments(j, h, par, first=False):
                dve.wait_ge(x_in[par], (h + 1) * 16)
                if not first:
                    dve.wait_ge(xn_s.sem, xn_s.at(j, 0))
                layernorm_stats(nc, g, dve, xin[:, par], stats, mv, TT, stats_s, mom_s, j)

            def normalise(j, par, first=False):
                dve.wait_ge(rstd_s.sem, rstd_s.at(j, 1))
                if not first:
                    dve.wait_ge(at_mm.sem, at_mm.at(j, -1))
                for i in range(TT):
                    nc.vector.tensor_scalar(xn[:, par, i, :], xin[:, par, i, :], mv[:, i, 0:1], rstd[:, i:i + 1],
                                            ALU.subtract, ALU.mult).then_inc(xn_s.sem, 1)

            def shift(j):
                for m in range(DC):
                    dve.wait_ge(score_mm.sem, score_mm.at(j, m + 1))
                    nc.vector.tensor_reduce(nmax[:, m:m + 1], ps_s[:, m, :], AX.X, ALU.max, negate=True)\
                        .then_inc(max_s.sem, 1)
                    dve.wait_ge(max_s.sem, max_s.at(j, m + 1))
                    nc.vector.scalar_tensor_tensor(ebias[:, m:m + 1], nmax[:, m:m + 1], g.cb[:, m:m + 1],
                                                   g.cb[:, m:m + 1], ALU.subtract, ALU.add).then_inc(bias_s.sem, 1)

            def scale(j, par):
                dve.wait_ge(exp_s.sem, exp_s.at(j, DC))
                nc.vector.reciprocal(rinv[:], sums[:]).then_inc(recip_s.sem, 1)
                dve.wait_ge(recip_s.sem, recip_s.at(j, 1))
                for m in range(DC):
                    nc.vector.tensor_scalar(prob[:, par, m, :], prob[:, par, m, :], rinv[:, m:m + 1], None,
                                            ALU.mult).then_inc(p_s.sem, 1)

            def keep(j):
                dve.wait_ge(at_mm.sem, at_mm.at(j, 1))
                nc.vector.tensor_copy(at_all[:, :, :, j], ps_at[:]).then_inc(at_s.sem, 1)

            def step(j, h, par, first=False, last=False):
                if not last:
                    moments(j + 1, h + par, 1 - par)
                shift(j)
                scale(j, par)
                if not first:
                    keep(j - 1)
                if not last:
                    normalise(j + 1, 1 - par, first)

            moments(0, 0, 0, True)
            normalise(0, 0, True)
            step(0, 0, 0, first=True)
            with dve.Fori(0, B // 2 - 1) as k:
                step(2 * k + 1, k, 1)
                step(2 * k + 2, k + 1, 0)
            step(B - 1, B // 2 - 1, 1, last=True)
            keep(B - 1)

        @block.gpsimd
        def _(pool):
            layernorm_rstd(nc, g, pool, mv, veps, rstd, TT, mom_s, veps_s, rstd_s, 0)
            with pool.Fori(1, B) as j:
                pool.wait_ge(xn_s.sem, xn_s.at(j, 0))
                layernorm_rstd(nc, g, pool, mv, veps, rstd, TT, mom_s, veps_s, rstd_s, j)

        @block.tensor
        def _(pe):
            def transpose_x(j, par, first=False):
                pe.wait_ge(xn_s.sem, xn_s.at(j, TT))
                if not first:
                    pe.wait_ge(xt_s.sem, xt_s.at(j, 0))
                for c in range(DC):
                    for i in range(TT):
                        last = nc.tensor.transpose(ps_xt[:, c, i * P:(i + 1) * P],
                                                   xn[:, par, i, c * P:(c + 1) * P], g.ident[:])
                    last.then_inc(xt_mm.sem, 1)

            def scores(j, first):
                pe.wait_ge(xt_s.sem, xt_s.at(j, DC))
                if not first:
                    pe.wait_ge(exp_s.sem, exp_s.at(j, 0))
                for m in range(DC):
                    for c in range(DC):
                        last = nc.tensor.matmul(ps_s[:, m, :], g.G[:, c, m * P:(m + 1) * P], xnT[:, c, :],
                                                start=(c == 0), stop=(c == DC - 1))
                    last.then_inc(score_mm.sem, 1)

            def transpose_p(j, par, first=False):
                pe.wait_ge(p_s.sem, p_s.at(j, DC))
                if not first:
                    pe.wait_ge(pt_s.sem, pt_s.at(j, 0))
                for half in range(2):
                    for i in range(2 * half, 2 * half + 2):
                        for m in range(DC):
                            last = nc.tensor.transpose(ps_pt[:, i, m * P:(m + 1) * P],
                                                       prob[:, par, m, i * P:(i + 1) * P], g.ident[:])
                    last.then_inc(pt_mm.sem, 1)

            def gather(j, par, first=False):
                pe.wait_ge(pt_s.sem, pt_s.at(j, 2))
                if not first:
                    pe.wait_ge(at_s.sem, at_s.at(j, 0))
                for c in range(DC):
                    for i in range(TT):
                        last = nc.tensor.matmul(ps_at[:, c, :], xn[:, par, i, c * P:(c + 1) * P], probT[:, i, :],
                                                start=(i == 0), stop=(i == TT - 1))
                last.then_inc(at_mm.sem, 1)

            def step(j, par, first=False, second=False, last=False):
                if not first:
                    transpose_p(j - 1, 1 - par, second)
                scores(j, first)
                if not first:
                    gather(j - 1, 1 - par, second)
                if not last:
                    transpose_x(j + 1, 1 - par)

            transpose_x(0, 0, True)
            step(0, 0, first=True)
            step(1, 1, second=True)
            step(2, 0)
            with pe.Fori(1, B // 2 - 1) as k:
                step(2 * k + 1, 1)
                step(2 * k + 2, 0)
            step(B - 1, 1, last=True)
            transpose_p(B - 1, 1)
            gather(B - 1, 1)

        @block.scalar
        def _(act):
            def copy_x(j, first=False):
                if not first:
                    act.wait_ge(score_mm.sem, score_mm.at(j, 0))
                for c in range(DC):
                    act.wait_ge(xt_mm.sem, xt_mm.at(j, c + 1))
                    nc.scalar.copy(xnT[:, c, :], ps_xt[:, c, :]).then_inc(xt_s.sem, 1)

            def exps(j, par, early=False):
                if not early:
                    act.wait_ge(pt_mm.sem, pt_mm.at(j, -2))
                for m in range(DC):
                    act.wait_ge(bias_s.sem, bias_s.at(j, m + 1))
                    nc.scalar.activation(prob[:, par, m, :], ps_s[:, m, :], ACT.Exp, bias=ebias[:, m:m + 1],
                                         accum_out=sums[:, m:m + 1]).then_inc(exp_s.sem, 1)

            def copy_p(j, first=False):
                if not first:
                    act.wait_ge(at_mm.sem, at_mm.at(j, 0))
                for half in range(2):
                    act.wait_ge(pt_mm.sem, pt_mm.at(j, half + 1))
                    nc.scalar.copy(probT[:, 2 * half:2 * half + 2, :], ps_pt[:, 2 * half:2 * half + 2, :])\
                        .then_inc(pt_s.sem, 1)

            def step(j, par, first=False, second=False, last=False):
                if not first:
                    copy_p(j - 1, second)
                exps(j, par, first or second)
                if not last:
                    copy_x(j + 1)

            copy_x(0, True)
            step(0, 0, first=True)
            step(1, 1, second=True)
            step(2, 0)
            with act.Fori(1, B // 2 - 1) as k:
                step(2 * k + 1, 1)
                step(2 * k + 2, 0)
            step(B - 1, 1, last=True)
            copy_p(B - 1)


def expert_phase(nc, io, g, sem, f, at_all, kT, vT):
    n = lambda x: f"ex_{x}"
    name = lambda x: f"ex{f}_{x}"
    one = lambda x: sem(n(x))
    c = lambda x, per: Count(sem(n(x)), per)
    NP = NE // 2
    R = 2 * QUAD
    tab_in, padded, rows_s, v_mm, v_s, o_mm, o_s = (one(x) for x in ("tab", "pad", "rows", "v_mm", "v", "o_mm", "o"))
    stats_s, mom_s, veps_s, rstd_s = c("stats", 2), c("moments", 2), c("veps", 1), c("rstd", 1)
    h0_s, hT_mm, hg_s, hb_s, oT_s = one("h0"), one("hT_mm"), one("hg"), one("hb"), one("oT")
    w_in = [[one(f"{w}_in{i}") for i in range(2)] for w in ("w1", "wg", "w2")]
    stage_s, up_mm, pre_s, silu_s, ug_s = c("stage", 1), c("up_mm", 2), c("pre", 2), c("silu", 2), c("ug", 1)
    ugT_mm, ugT_s, y_mm, y_s, yT_mm, on_s = c("ugT_mm", 1), c("ugT", 1), c("y_mm", 1), c("y", 1), c("yT_mm", 1), c("on", 1)
    kv_mm, kv_s, bk_s = one("kv_mm"), one("kv"), one("bk")
    with ExitStack() as s:
        sb = lambda nm, sh: s.enter_context(nc.sbuf_tensor(name(nm), sh, F32))
        pb = lambda nm, sh: s.enter_context(nc.psum_tensor(name(nm), sh, F32))
        sq, bo = sb("t_sq", [P, 2, D]), sb("t_bo", [P, D])
        gT, bT, b2T = (sb(x, [P, DC, NE]) for x in ("t_gT", "t_bT", "t_b2T"))
        cwk, cwv = sb("t_cwk", [P, DC, D]), sb("t_cwv", [P, DC, D])
        bk, bv, bk4 = sb("t_bk", [P, DC]), sb("t_bv", [P, DC]), sb("t_bk4", [P, DC])
        attnT = sb("t_attnT", [P, 4, HS])
        o, h0 = sb("t_o", [P, 2, D]), sb("t_h0", [P, 2, D])
        stats, mv, veps, rstd = sb("t_st", [P, 2, 6]), sb("t_mv", [P, 2, 2]), sb("t_ve", [P, 2]), sb("t_rs", [P, 2])
        hg = sb("t_hg", [P, DC, NE, B])
        hP = sb("t_hP", [P, DC, NE, QUAD])
        oT, onT = sb("t_oT", [P, DC, NE, B]), sb("t_onT", [P, DC, NE, B])
        w1, wg = sb("t_w1", [P, 2, 2, DC, F]), sb("t_wg", [P, 2, 2, DC, F])
        w2 = sb("t_w2", [P, 2, 2, FK, D])
        b1, bg = sb("t_b1", [R, 2, F]), sb("t_bg", [R, 2, F])
        stage = sb("t_stage", [P, 2, DC, 2, QUAD])
        ub, gb = sb("t_ub", [R, F]), sb("t_gb", [R, F])
        ugT, y = sb("t_ugT", [P, FK, R]), sb("t_y", [R, D])
        ps_u, ps_g = pb("ps_u", [P, F]), pb("ps_g", [P, F])
        ps_ugT, ps_y, ps_yT, ps_kv = pb("ps_ugT", [P, FK, R]), pb("ps_y", [P, 512]), pb("ps_yT", [P, DC, R]), pb("ps_kv", [P, 2, 256])
        ps_v = ps_u[:].rearrange("p (t r) -> p t r", t=4)
        ps_o = ps_g[:, 0:2 * D].rearrange("p (m d) -> p m d", m=2)
        ps_hT = ps_ugT[:].rearrange("p k r -> p (k r)").rearrange("p (c r) -> p c r", c=DC)
        ps_oT = ps_y[:].rearrange("p (c r) -> p c r", c=DC)
        TABS = 9
        block = s.enter_context(nc.Block())

        @block.sync
        def _(sp):
            def load(pr, par):
                for (w, src, bias, bsrc), at in zip((
                        (w1, io["e_W1"], b1, io["e_b1"]), (wg, io["e_Wg"], bg, io["e_bg"])), w_in):
                    for e in range(2):
                        sp.dma_start(w[:, par, e], src[2 * pr + e].rearrange("(c p) f -> p c f", p=P)).then_inc(at[par], 16)
                    sp.dma_start(bias[:, par, :], bsrc[pr]).then_inc(at[par], 16)
                for e in range(2):
                    sp.dma_start(w2[:, par, e], io["e_W2"][2 * pr + e].rearrange("(p k) d -> p k d", k=FK))\
                        .then_inc(w_in[2][par], 16)

            for dst, src in ((sq[:], io["sq_rows"].rearrange("(m p) d -> p m d", p=P)), (bo[:], io["d_bo"]),
                             (gT[:], io["e_gT"]), (bT[:], io["e_bT"]), (b2T[:], io["e_b2T"]),
                             (cwk[:], io["c_Wk"].rearrange("(c p) n -> p c n", p=P)),
                             (cwv[:], io["c_Wv"].rearrange("(c p) n -> p c n", p=P)),
                             (bk[:], io["c_bk"]), (bv[:], io["c_bv"])):
                sp.dma_start(dst, src).then_inc(tab_in, 16)
            load(0, 0)
            load(1, 1)
            with sp.Fori(0, NP // 2 - 1) as k:
                for par in range(2):
                    hold(g, sp, pre_s.sem, pre_s.at(2 * k + par, 2))
                    hold(g, sp, y_mm.sem, y_mm.at(2 * k + par, 1))
                    load(2 * k + 2 + par, par)

        @block.vector
        def _(dve):
            nc.vector.memset(hP[:], 0.0).then_inc(padded, 1)
            dve.wait_ge(tab_in, 16 * TABS)
            nc.vector.tensor_scalar(bk4[:], bk[:], FDH ** -0.5, None, ALU.mult).then_inc(bk_s, 1)
            for m in range(2):
                nc.vector.tensor_tensor(sq[:, m, :], sq[:, m, :], bo[:], ALU.add).then_inc(rows_s, 1)
            dve.wait_ge(o_mm, 1)
            dve.wait_ge(rows_s, 2)
            nc.vector.tensor_tensor(o[:], ps_o, sq[:], ALU.add).then_inc(o_s, 1)
            dve.wait_ge(o_s, 1)
            layernorm_stats(nc, g, dve, o, stats, mv, 2, stats_s, mom_s, 0)
            dve.wait_ge(rstd_s.sem, rstd_s.at(0, 1))
            for m in range(2):
                nc.vector.tensor_scalar(h0[:, m, :], o[:, m, :], mv[:, m, 0:1], rstd[:, m:m + 1],
                                        ALU.subtract, ALU.mult).then_inc(h0_s, 1)
            dve.wait_ge(hT_mm, 2)
            for ch in range(DC):
                nc.vector.tensor_tensor(hg[:, ch], ps_hT[:, ch].rearrange("p (e b) -> p e b", b=B),
                                        bcast(gT[:, ch, :], 2, B), ALU.mult).then_inc(hg_s, 1)
                nc.vector.tensor_tensor(oT[:, ch], ps_oT[:, ch].rearrange("p (e b) -> p e b", b=B),
                                        bcast(b2T[:, ch, :], 2, B), ALU.add).then_inc(oT_s, 1)
            dve.wait_ge(hg_s, DC)
            dve.wait_ge(padded, 1)
            for ch in range(DC):
                nc.vector.tensor_tensor(hP[:, ch, :, 0:B], hg[:, ch], bcast(bT[:, ch, :], 2, B), ALU.add).then_inc(hb_s, 1)
            dve.wait_ge(hb_s, DC)
            dve.wait_ge(oT_s, DC)

            def hidden(pr, par, first=False):
                if not first:
                    dve.wait_ge(up_mm.sem, up_mm.at(pr, -2))
                nc.vector.tensor_copy(stage[:, par], hP[:, :, bass.ds(2 * pr, 2), :]).then_inc(stage_s.sem, 1)

            def step(pr, par, h, first=False, second=False, last=False):
                if not last:
                    hidden(pr + 1, 1 - par, first)
                for i, (bias, ps, pre) in enumerate(((b1, ps_u, ub), (bg, ps_g, gb))):
                    dve.wait_ge(up_mm.sem, up_mm.at(pr, i + 1))
                    if not first and i == 0:
                        dve.wait_ge(ugT_mm.sem, ugT_mm.at(pr, 0))
                    nc.vector.tensor_tensor(pre[:], ps[0:R, :], bias[:, par, :], ALU.add).then_inc(pre_s.sem, 1)
                dve.wait_ge(silu_s.sem, silu_s.at(pr, 2))
                nc.vector.tensor_tensor(ub[:], ub[:], gb[:], ALU.mult).then_inc(ug_s.sem, 1)
                dve.wait_ge(yT_mm.sem, yT_mm.at(pr, 1))
                nc.vector.tensor_tensor(onT[:, :, bass.ds(2 * pr, 2), :],
                                        ps_yT[:].rearrange("p c (e r) -> p c e r", e=2)[:, :, :, 0:B],
                                        oT[:, :, bass.ds(2 * pr, 2), :], ALU.add).then_inc(on_s.sem, 1)

            hidden(0, 0, True)
            step(0, 0, 0, first=True)
            with dve.Fori(0, NP // 2 - 1) as k:
                step(2 * k + 1, 1, k)
                step(2 * k + 2, 0, k + 1)
            step(NP - 1, 1, NP // 2 - 1, last=True)

        @block.gpsimd
        def _(pool):
            layernorm_rstd(nc, g, pool, mv, veps, rstd, 2, mom_s, veps_s, rstd_s, 0)

        @block.tensor
        def _(pe):
            for t in range(4):
                for ch in range(DC):
                    for q in range(4):
                        h = 4 * t + q
                        last = nc.tensor.matmul(
                            ps_v[q * QUAD:(q + 1) * QUAD, t, :], g.wv_pad[:, ch, h, :],
                            at_all[:, ch, h * NS:(h + 1) * NS, :].rearrange("p s b -> p (s b)"),
                            start=(ch == 0), stop=(ch == DC - 1))
            last.then_inc(v_mm, 1)
            pe.wait_ge(v_s, 4)
            for m in range(2):
                for t in range(4):
                    last = nc.tensor.matmul(ps_o[:, m, :], attnT[:, t, m * P:(m + 1) * P], g.wo_pad[:, t, :],
                                            start=(t == 0), stop=(t == 3))
            last.then_inc(o_mm, 1)
            pe.wait_ge(h0_s, 2)
            for src, dst in ((h0, ps_hT), (o, ps_oT)):
                for ch in range(DC):
                    for m in range(2):
                        last = nc.tensor.transpose(dst[:, ch, m * P:(m + 1) * P], src[:, m, ch * P:(ch + 1) * P], g.ident[:])
                last.then_inc(hT_mm, 1)

            def up(pr, par, h, first=False):
                pe.wait_ge(stage_s.sem, stage_s.at(pr, 1))
                for i, (w, ps) in enumerate(((w1, ps_u), (wg, ps_g))):
                    pe.wait_ge(w_in[i][par], (h + 1) * 48)
                    if not first:
                        pe.wait_ge(pre_s.sem, pre_s.at(pr, i - 1))
                    for half in range(2):
                        for ch in range(DC):
                            for e in range(2):
                                last = nc.tensor.matmul(ps[e * QUAD:(e + 1) * QUAD, half * 512:(half + 1) * 512],
                                                        stage[:, par, ch, e, :], w[:, par, e, ch, half * 512:(half + 1) * 512],
                                                        start=(ch == 0), stop=(ch == DC - 1))
                    last.then_inc(up_mm.sem, 1)

            def down(pr, par, h, first=False):
                pe.wait_ge(ug_s.sem, ug_s.at(pr, 1))
                if not first:
                    hold(g, pe, ugT_s.sem, ugT_s.at(pr, 0))
                for k in range(FK):
                    last = nc.tensor.transpose(ps_ugT[:, k, :], ub[:].rearrange("r (p k) -> r k p", k=FK)[:, k, :],
                                               g.ident[0:R, 0:R])
                last.then_inc(ugT_mm.sem, 1)
                pe.wait_ge(ugT_s.sem, ugT_s.at(pr, 1))
                pe.wait_ge(w_in[2][par], (h + 1) * 32)
                if not first:
                    pe.wait_ge(y_s.sem, y_s.at(pr, 0))
                for k in range(FK):
                    for e in range(2):
                        last = nc.tensor.matmul(ps_y[e * QUAD:(e + 1) * QUAD, 0:D], ugT[:, k, e * QUAD:(e + 1) * QUAD],
                                                w2[:, par, e, k, :], start=(k == 0), stop=(k == FK - 1))
                last.then_inc(y_mm.sem, 1)
                pe.wait_ge(y_s.sem, y_s.at(pr, 1))
                if not first:
                    hold(g, pe, on_s.sem, on_s.at(pr, 0))
                for ch in range(DC):
                    last = nc.tensor.transpose(ps_yT[:, ch, :], y[:, ch * P:(ch + 1) * P], g.ident[0:R, 0:R])
                last.then_inc(yT_mm.sem, 1)

            up(0, 0, 0, True)
            down(0, 0, 0, True)
            with pe.Fori(0, NP // 2 - 1) as k:
                for par in range(2):
                    up(2 * k + 1 + par, 1 - par, k + par)
                    down(2 * k + 1 + par, 1 - par, k + par)
            up(NP - 1, 1, NP // 2 - 1)
            down(NP - 1, 1, NP // 2 - 1)
            pe.wait_ge(on_s.sem, on_s.at(NP - 1, 1))
            for i, (w, ps) in enumerate(((cwk, ps_kv), (cwv, ps_o))):
                for m in range(2):
                    for ch in range(DC):
                        last = nc.tensor.matmul(ps[:, m, :], w[:, ch, m * P:(m + 1) * P],
                                                onT[:, ch].rearrange("p e b -> p (e b)"),
                                                start=(ch == 0), stop=(ch == DC - 1))
                last.then_inc(kv_mm, 1)

        @block.scalar
        def _(act):
            act.wait_ge(v_mm, 1)
            for t in range(4):
                nc.scalar.activation(attnT[:, t, :], ps_v[:, t, :], ACT.Identity, bias=g.bv_pad[:, t:t + 1]).then_inc(v_s, 1)

            def step(pr, first=False):
                for i, pre in enumerate((ub, gb)):
                    act.wait_ge(pre_s.sem, pre_s.at(pr, i + 1))
                    nc.scalar.activation(pre[:], pre[:], ACT.Silu).then_inc(silu_s.sem, 1)
                act.wait_ge(ugT_mm.sem, ugT_mm.at(pr, 1))
                if not first:
                    act.wait_ge(y_mm.sem, y_mm.at(pr, 0))
                nc.scalar.copy(ugT[:], ps_ugT[:]).then_inc(ugT_s.sem, 1)
                act.wait_ge(y_mm.sem, y_mm.at(pr, 1))
                if not first:
                    act.wait_ge(yT_mm.sem, yT_mm.at(pr, 0))
                nc.scalar.copy(y[:], ps_y[0:R, 0:D]).then_inc(y_s.sem, 1)

            step(0, True)
            with act.Fori(1, NP) as pr:
                step(pr)
            act.wait_ge(bk_s, 1)
            act.wait_ge(kv_mm, 1)
            for m in range(DC):
                nc.scalar.activation(kT[:, m].rearrange("p s b -> p (s b)"), ps_kv[:, m, :], ACT.Identity,
                                     bias=bk4[:, m:m + 1], scale=FDH ** -0.5).then_inc(kv_s, 1)
            act.wait_ge(kv_mm, 2)
            for m in range(DC):
                nc.scalar.activation(vT[:, m].rearrange("p s b -> p (s b)"), ps_o[:, m, :], ACT.Identity,
                                     bias=bv[:, m:m + 1]).then_inc(kv_s, 1)


def combine_phase(nc, io, g, sem, f, x_dram, out_dram, kT, vT):
    n = lambda x: f"com_{x}"
    name = lambda x: f"com{f}_{x}"
    c = lambda x, per, credit=0: Count(sem(n(x)), per, credit)
    NU = 2 * B
    W = 2
    tab_in = sem(n("tab"))
    x_in = [sem(n(f"x_in{i}")) for i in range(2)]
    out_s = [sem(n(f"out{i}")) for i in range(2)]
    stats_s, mom_s, veps_s, rstd_s, xn_s = c("stats", W), c("moments", W), c("veps", 1), c("rstd", 1), c("xn", W)
    xb_s, half_s = c("xb", 1), sem(n("half"))
    blk_s, gu_mm, g_s, cb_mm, cb_s = c("blk", 4), c("gu_mm", 2), c("gu", 2), c("cb_mm", 1), c("cb", 1)
    xt_mm, xt_s, s_mm, s1_s, max_s, sub_s, exp_s, sum_s, rec_s, p_s = (
        c(x, 1) for x in ("xt_mm", "xt", "s_mm", "s1", "max", "sub", "exp", "sum", "rec", "p"))
    pt_mm, pt_s, o_mm, o_s = c("pt_mm", 1), c("pt", 1), c("o_mm", 1), c("o", 1)
    with ExitStack() as s:
        sb = lambda nm, sh: s.enter_context(nc.sbuf_tensor(name(nm), sh, F32))
        pb = lambda nm, sh: s.enter_context(nc.psum_tensor(name(nm), sh, F32))
        bq, bo, boh = sb("t_bq", [P, DC, P]), sb("t_bo", [P, W, D]), sb("t_boh", [P, W, D])
        xin, xb, xo = sb("b_x", [P, 2, W, D]), sb("b_xb", [P, 2, W, D]), sb("b_xo", [P, 2, W, D])
        stats, mv, veps, rstd = sb("b_st", [P, W, 6]), sb("b_mv", [P, W, 2]), sb("b_ve", [P, W]), sb("b_rs", [P, W])
        xn, xnT = sb("b_xn", [P, W, D]), sb("b_xnT", [P, DC, W * P])
        kblk, vblk = sb("b_kblk", [P, DC, HPC, NS]), sb("b_vblk", [P, DC, HPC, NS])
        G, U, cb = sb("b_G", [P, 2, DC, HS]), sb("b_U", [P, 2, DC, D]), sb("b_cb", [P, 2, HS])
        s1, prob = sb("b_s1", [P, W, HS]), sb("b_prob", [P, 2, W, HS])
        mx, sm, rc = (sb(x, [P, W * FH]) for x in ("b_mx", "b_sm", "b_rc"))
        pT = sb("b_pT", [P, DC, W * P])
        ps_xt, ps_g, ps_u, ps_c = pb("ps_xt", [P, DC, W * P]), pb("ps_g", [P, DC, HS]), pb("ps_u", [P, DC, D]), pb("ps_c", [P, 512])
        ps_s, ps_pt, ps_o = pb("ps_s", [P, W, HS]), pb("ps_pt", [P, DC, W * P]), pb("ps_o", [P, W, D])
        heads = lambda ap: ap.rearrange("p w (h s) -> p (w h) s", s=NS)
        block = s.enter_context(nc.Block())

        def rows(dram, j, p):
            return dram[j].rearrange("(u i p) d -> u p i d", u=2, p=P)[p]

        @block.sync
        def _(sp):
            sp.dma_start(bq[:], io["c_bq"]).then_inc(tab_in, 16)
            sp.dma_start(bo[:], io["c_bo"]).then_inc(tab_in, 16)

            def load(j, p):
                sp.dma_start(xin[:, p], rows(x_dram, j, p)).then_inc(x_in[p], 16)

            for p in range(2):
                load(0, p)
            with sp.Fori(0, B - 1) as j:
                for p in range(2):
                    hold(g, sp, xn_s.sem, xn_s.at(2 * j + p, W))
                    hold(g, sp, xb_s.sem, xb_s.at(2 * j + p, 1))
                    load(j + 1, p)
                for p in range(2):
                    hold(g, sp, o_s.sem, o_s.at(2 * j + p, 1))
                    sp.dma_start(rows(out_dram, j, p), xo[:, p]).then_inc(out_s[p], 16)
            for p in range(2):
                sp.wait_ge(o_s.sem, o_s.at(2 * (B - 1) + p, 1))
                sp.dma_start(rows(out_dram, B - 1, p), xo[:, p]).then_inc(out_s[p], 16)
            for p in range(2):
                sp.wait_ge(out_s[p], 16 * B)

        @block.vector
        def _(dve):
            dve.wait_ge(tab_in, 32)
            nc.vector.tensor_scalar(boh[:], bo[:], 0.5, None, ALU.mult).then_inc(half_s, 1)

            def blocks(j, first=False):
                if not first:
                    dve.wait_ge(cb_mm.sem, cb_mm.at(j, 0))
                for src, dst in ((kT, kblk), (vT, vblk)):
                    for ch in range(DC):
                        nc.vector.tensor_tensor(dst[:, ch], g.blkmask[:].rearrange("p (h s) -> p h s", s=NS),
                                                bcast(src[:, ch, :, j], 1, HPC), ALU.mult).then_inc(blk_s.sem, 1)

            def copies(j, jp):
                dve.wait_ge(cb_mm.sem, cb_mm.at(j, 1))
                nc.vector.tensor_copy(cb[:, jp, :], ps_c[:, 0:HS]).then_inc(cb_s.sem, 1)

            def normalise(u, j, p, first=False):
                dve.wait_ge(x_in[p], j * 16 + 16)
                layernorm_stats(nc, g, dve, xin[:, p], stats, mv, W, stats_s, mom_s, u)
                dve.wait_ge(rstd_s.sem, rstd_s.at(u, 1))
                if not first:
                    dve.wait_ge(xt_mm.sem, xt_mm.at(u, 0))
                for i in range(W):
                    nc.vector.tensor_scalar(xn[:, i, :], xin[:, p, i, :], mv[:, i, 0:1], rstd[:, i:i + 1],
                                            ALU.subtract, ALU.mult).then_inc(xn_s.sem, 1)

            def shift(u, j, jp, first=False):
                dve.wait_ge(cb_s.sem, cb_s.at(j, 1))
                dve.wait_ge(s_mm.sem, s_mm.at(u, 1))
                if not first:
                    dve.wait_ge(exp_s.sem, exp_s.at(u, 0))
                nc.vector.tensor_tensor(s1[:], ps_s[:], bcast(cb[:, jp, :], 1, W), ALU.add).then_inc(s1_s.sem, 1)
                dve.wait_ge(s1_s.sem, s1_s.at(u, 1))
                nc.vector.tensor_reduce(mx[:], heads(s1[:]), AX.X, ALU.max).then_inc(max_s.sem, 1)
                dve.wait_ge(max_s.sem, max_s.at(u, 1))
                nc.vector.tensor_tensor(heads(s1[:]), heads(s1[:]), bcast(mx[:], 2, NS), ALU.subtract).then_inc(sub_s.sem, 1)

            def scale(u, p):
                dve.wait_ge(exp_s.sem, exp_s.at(u, 1))
                nc.vector.tensor_reduce(sm[:], heads(prob[:, p]), AX.X, ALU.add).then_inc(sum_s.sem, 1)
                dve.wait_ge(sum_s.sem, sum_s.at(u, 1))
                nc.vector.reciprocal(rc[:], sm[:]).then_inc(rec_s.sem, 1)
                dve.wait_ge(rec_s.sem, rec_s.at(u, 1))
                nc.vector.tensor_tensor(heads(prob[:, p]), heads(prob[:, p]), bcast(rc[:], 2, NS), ALU.mult).then_inc(p_s.sem, 1)

            def result(u, j, p, early=False):
                dve.wait_ge(o_mm.sem, o_mm.at(u, 1))
                dve.wait_ge(xb_s.sem, xb_s.at(u, 1))
                if not early:
                    dve.wait_ge(out_s[p], j * 16)
                nc.vector.scalar_tensor_tensor(xo[:, p], ps_o[:], 0.5, xb[:, p], ALU.mult, ALU.add).then_inc(o_s.sem, 1)

            def body(j, jp, first=False, second=False, last=False):
                shift(2 * j, j, jp, first)
                normalise(2 * j + 1, j, 1)
                scale(2 * j, 0)
                if not first:
                    result(2 * j - 1, j - 1, 1, second)
                if not last:
                    blocks(j + 1)
                shift(2 * j + 1, j, jp)
                if not last:
                    normalise(2 * j + 2, j + 1, 0)
                    copies(j + 1, 1 - jp)
                scale(2 * j + 1, 1)
                result(2 * j, j, 0, first)

            blocks(0, True)
            normalise(0, 0, 0, True)
            copies(0, 0)
            body(0, 0, first=True)
            body(1, 1, second=True)
            with dve.Fori(1, B // 2 - 1) as k:
                body(2 * k, 0)
                body(2 * k + 1, 1)
            body(B - 2, 0)
            body(B - 1, 1, last=True)
            result(2 * B - 1, B - 1, 1)

        @block.gpsimd
        def _(pool):
            pool.wait_ge(half_s, 1)

            def unit(u, j, p, first=False, early=False):
                if not first:
                    pool.wait_ge(xn_s.sem, xn_s.at(u, 0))
                layernorm_rstd(nc, g, pool, mv, veps, rstd, W, mom_s, veps_s, rstd_s, u)
                if not early:
                    pool.wait_ge(o_s.sem, o_s.at(u, -1))
                nc.gpsimd.tensor_tensor(xb[:, p], xin[:, p], boh[:], ALU.add).then_inc(xb_s.sem, 1)

            unit(0, 0, 0, True, True)
            unit(1, 0, 1, False, True)
            with pool.Fori(1, B) as j:
                for p in range(2):
                    unit(2 * j + p, j, p)

        @block.tensor
        def _(pe):
            def fold(j, jp, first=False):
                pe.wait_ge(blk_s.sem, blk_s.at(j, 4))
                if not first:
                    pe.wait_ge(g_s.sem, g_s.at(j, 0))
                    pe.wait_ge(cb_s.sem, cb_s.at(j, 0))
                for m in range(DC):
                    for ch in range(DC):
                        last = nc.tensor.matmul(ps_g[:, m, ch * P:(ch + 1) * P], g.cwqT[:, ch, m * P:(m + 1) * P],
                                                kblk[:, ch].rearrange("p h s -> p (h s)"), start=True, stop=True)
                last.then_inc(gu_mm.sem, 1)
                for ch in range(DC):
                    last = nc.tensor.matmul(ps_u[:, ch, :], vblk[:, ch].rearrange("p h s -> p (h s)"), g.cwo[:, ch, :],
                                            start=True, stop=True)
                last.then_inc(gu_mm.sem, 1)
                for ch in range(DC):
                    last = nc.tensor.matmul(ps_c[:, ch * P:(ch + 1) * P], bq[:, ch, :],
                                            kblk[:, ch].rearrange("p h s -> p (h s)"), start=True, stop=True)
                last.then_inc(cb_mm.sem, 1)

            def transpose_x(u, first=False):
                pe.wait_ge(xn_s.sem, xn_s.at(u, W))
                if not first:
                    pe.wait_ge(xt_s.sem, xt_s.at(u, 0))
                for ch in range(DC):
                    for i in range(W):
                        last = nc.tensor.transpose(ps_xt[:, ch, i * P:(i + 1) * P], xn[:, i, ch * P:(ch + 1) * P], g.ident[:])
                last.then_inc(xt_mm.sem, 1)

            def scores(u, j, jp, first=False):
                pe.wait_ge(xt_s.sem, xt_s.at(u, 1))
                pe.wait_ge(g_s.sem, g_s.at(j, 1))
                if not first:
                    pe.wait_ge(s1_s.sem, s1_s.at(u, 0))
                for i in range(W):
                    for ch in range(DC):
                        last = nc.tensor.matmul(ps_s[:, i, :], xnT[:, ch, i * P:(i + 1) * P], G[:, jp, ch, :],
                                                start=(ch == 0), stop=(ch == DC - 1))
                last.then_inc(s_mm.sem, 1)

            def transpose_p(u, p, first=False):
                pe.wait_ge(p_s.sem, p_s.at(u, 1))
                if not first:
                    pe.wait_ge(pt_s.sem, pt_s.at(u, 0))
                for ch in range(DC):
                    for i in range(W):
                        last = nc.tensor.transpose(ps_pt[:, ch, i * P:(i + 1) * P], prob[:, p, i, ch * P:(ch + 1) * P], g.ident[:])
                last.then_inc(pt_mm.sem, 1)

            def mix(u, j, jp, first=False):
                pe.wait_ge(pt_s.sem, pt_s.at(u, 1))
                pe.wait_ge(g_s.sem, g_s.at(j, 2))
                if not first:
                    pe.wait_ge(o_s.sem, o_s.at(u, 0))
                for i in range(W):
                    for ch in range(DC):
                        last = nc.tensor.matmul(ps_o[:, i, :], pT[:, ch, i * P:(i + 1) * P], U[:, jp, ch, :],
                                                start=(ch == 0), stop=(ch == DC - 1))
                last.then_inc(o_mm.sem, 1)

            def body(j, jp, first=False, second=False, last=False):
                scores(2 * j, j, jp, first)
                if not first:
                    transpose_p(2 * j - 1, 1)
                transpose_x(2 * j + 1)
                if not first:
                    mix(2 * j - 1, j - 1, 1 - jp)
                scores(2 * j + 1, j, jp)
                transpose_p(2 * j, 0, first)
                if not last:
                    transpose_x(2 * j + 2)
                    fold(j + 1, 1 - jp)
                mix(2 * j, j, jp, first)

            fold(0, 0, True)
            transpose_x(0, True)
            body(0, 0, first=True)
            body(1, 1)
            with pe.Fori(1, B // 2 - 1) as k:
                body(2 * k, 0)
                body(2 * k + 1, 1)
            body(B - 2, 0)
            body(B - 1, 1, last=True)
            transpose_p(2 * B - 1, 1)
            mix(2 * B - 1, B - 1, 1)

        @block.scalar
        def _(act):
            def folds(j, jp, early=False):
                if not early:
                    act.wait_ge(o_mm.sem, o_mm.at(2 * j, -2))
                for i, (dst, src) in enumerate(((G, ps_g), (U, ps_u))):
                    act.wait_ge(gu_mm.sem, gu_mm.at(j, i + 1))
                    nc.scalar.copy(dst[:, jp], src[:]).then_inc(g_s.sem, 1)

            def copy_x(u, first=False):
                act.wait_ge(xt_mm.sem, xt_mm.at(u, 1))
                if not first:
                    act.wait_ge(s_mm.sem, s_mm.at(u, 0))
                nc.scalar.copy(xnT[:], ps_xt[:]).then_inc(xt_s.sem, 1)

            def exps(u, p, early=False):
                act.wait_ge(sub_s.sem, sub_s.at(u, 1))
                if not early:
                    act.wait_ge(pt_mm.sem, pt_mm.at(u, -1))
                nc.scalar.activation(prob[:, p], s1[:], ACT.Exp).then_inc(exp_s.sem, 1)

            def copy_p(u, first=False):
                act.wait_ge(pt_mm.sem, pt_mm.at(u, 1))
                if not first:
                    act.wait_ge(o_mm.sem, o_mm.at(u, 0))
                nc.scalar.copy(pT[:], ps_pt[:]).then_inc(pt_s.sem, 1)

            def body(j, jp, first=False, second=False, last=False):
                if not first:
                    copy_p(2 * j - 1)
                copy_x(2 * j + 1)
                exps(2 * j, 0, first)
                copy_p(2 * j, first)
                if not last:
                    copy_x(2 * j + 2)
                    folds(j + 1, 1 - jp, first)
                exps(2 * j + 1, 1, first)

            folds(0, 0, True)
            copy_x(0, True)
            body(0, 0, first=True)
            body(1, 1)
            with act.Fori(1, B // 2 - 1) as k:
                body(2 * k, 0)
                body(2 * k + 1, 1)
            body(B - 2, 0)
            body(B - 1, 1, last=True)
            copy_p(2 * B - 1)


def attention_phase(nc, io, g, sem, x_dram, out_dram):
    n = lambda x: f"att_{x}"
    c = lambda x, per, credit=0: Count(sem(n(x)), per, credit)
    one = lambda x: sem(n(x))
    tab_in, w_in, w_hi, w_lo, zero_s, bqs_s = (one(x) for x in ("tab", "w_in", "w_hi", "w_lo", "zero", "bqs"))
    x_in, xres_in, out_s = c("x_in", 16), c("xres_in", 16), c("out", 16, 16)
    stats_s, mom_s, veps_s, rstd_s, xn_s = c("stats", TT), c("moments", TT), c("veps", 1), c("rstd", 1), c("xn", TT, TT)
    xt_mm, xhi_s, xlo_s = c("xt_mm", DC, DC), c("xhi", DC), c("xlo", DC)
    v_mm, v_s = c("v_mm", 2 * TT), c("v", 2 * TT)
    z_mm, z_s, shuf_s, cos_s, sin_s, rope_s = (
        c("z_mm", 2 * PAIRS, 2 * PAIRS), c("z", 2 * PAIRS), c("shuf", 2 * PAIRS), c("cos", 2 * PAIRS), c("sin", 2 * PAIRS),
        c("rope", 3 * PAIRS, 3))
    s_mm, max_s, exp_s, rec_s, p_s = (
        c("s_mm", 4 * AH, 8), c("max", 4 * AH), c("exp", 4 * AH, 4), c("rec", AH), c("p", 4 * AH))
    pt_mm, pta_s, ptd_s, pv_mm, ohi_s, olo_s = (
        c("pt_mm", 4 * AH, 8), c("pta", 2 * AH, 2), c("ptd", 2 * AH, 2), c("pv_mm", PAIRS, 1), c("ohi", PAIRS), c("olo", PAIRS, 1))
    wo_mm, xb_s, xo_s = c("wo_mm", 2, 2), c("xb", 1), c("xo", 2, 2)
    OFF = [0, 512, 896, 1152]
    WIDTH = [S - kb * P for kb in range(TT)]
    with ExitStack() as s:
        sb = lambda nm, sh, dt=F32: s.enter_context(nc.sbuf_tensor(n(nm), sh, dt))
        pb = lambda nm, sh: s.enter_context(nc.psum_tensor(n(nm), sh, F32))
        w_parts = {w: [sb(f"w{w}_{x}", [P, 2048], F32R) for x in ("hi", "lo")] for w in ("q", "k", "v", "o")}
        split = lambda w: [t[:].rearrange("p (c n) -> p c n", c=(PAIRS if w == "o" else DC)) for t in w_parts[w]]
        wq, wk, wv, wo = (split(w) for w in ("q", "k", "v", "o"))
        cos, sin = sb("cos", [P, S]), sb("sin", [P, S])
        bq, bqs, bk = sb("bq", [P, PAIRS]), sb("bqs", [P, PAIRS]), sb("bk", [P, PAIRS])
        bv, bo = sb("bv", [P, AW]), sb("bo", [P, D])
        identb, masked = sb("identb", [P, P], BF16), sb("masked", [P, P], BF16)
        xin, xn, xres, xo = (sb(x, [P, TT, D]) for x in ("x", "xn", "xres", "xo"))
        stats, mv, veps, rstd = sb("st", [P, TT, 6]), sb("mv", [P, TT, 2]), sb("ve", [P, TT]), sb("rs", [P, TT])
        xT = [sb(f"xT_{x}", [P, DC, S], F32R) for x in ("hi", "lo")]
        v = sb("v_sb", [P, TT, AW])
        z, zs = sb("z_sb", [P, 2, S]), sb("zs", [P, 2, S])
        qz = sb("qz", [P, 2, 2, S])
        kT = sb("kT", [P, 2, S])
        prob = sb("prob", [P, 2, TT, S])
        nmax, sums, rinv = (sb(x, [P, 2, TT]) for x in ("nmax", "sums", "rinv"))
        probT = sb("probT", [P, 2, OFF[3] + WIDTH[3]])
        oT = [sb(f"oT_{x}", [P, PAIRS, S], F32R) for x in ("hi", "lo")]
        ps_s = [pb(f"ps_s{i}", [P, S]) for i in range(TT)]
        ps_z = [pb(f"ps_z{i}", [P, S]) for i in range(2)]
        ps_pt, ps_pv = pb("ps_pt", [P, S]), pb("ps_pv", [P, S])
        w_stage = prob[:].rearrange("p h i s -> p h (i s)")
        block = s.enter_context(nc.Block())

        def products(ps, lhs, rhs):
            terms = [(a, b, ch) for a, b in ((0, 0), (0, 1), (1, 0)) for ch in range(len(lhs[0]))]
            for i, (a, b, ch) in enumerate(terms):
                last = nc.tensor.matmul(ps, lhs[a][ch], rhs[b][ch], start=(i == 0), stop=(i == len(terms) - 1))
            return last

        @block.sync
        def _(sp):
            for dst, src in ((cos[:], io["cos"]), (sin[:], io["sin"]), (bq[:], io["a_bq"]), (bk[:], io["a_bk"]),
                             (bv[:], io["a_bv"]), (bo[:], io["a_bo"]), (identb[:], io["identb"]), (masked[:], io["masked"])):
                sp.dma_start(dst, src).then_inc(tab_in, 16)
            for i, (w, pitch) in enumerate((("q", 2), ("k", 2), ("v", 2), ("o", 8))):
                if i >= 2:
                    sp.wait_ge(w_lo, i - 1)
                sp.dma_start(w_stage[:, i % 2, :].rearrange("p (c n) -> p c n", c=pitch),
                             io["a_W" + w].rearrange("(c p) n -> p c n", p=P)).then_inc(w_in, 16)
                sp.wait_ge(w_in, 16 * (i + 1))
            with sp.Fori(0, B) as j:
                hold(g, sp, xn_s.sem, xn_s.at(j, 0))
                sp.dma_start(xin[:], x_dram[j].rearrange("(i p) d -> p i d", p=P)).then_inc(x_in.sem, 16)
                hold(g, sp, xo_s.sem, xo_s.at(j, 0))
                sp.dma_start(xres[:], x_dram[j].rearrange("(i p) d -> p i d", p=P)).then_inc(xres_in.sem, 16)
                hold(g, sp, xo_s.sem, xo_s.at(j, 2))
                sp.dma_start(out_dram[j].rearrange("(i p) d -> p i d", p=P), xo[:]).then_inc(out_s.sem, 16)
            sp.wait_ge(out_s.sem, out_s.at(B - 1, 16))

        @block.gpsimd
        def _(pool):
            nc.gpsimd.memset(qz[:], 0.0).then_inc(zero_s, 1)
            pool.wait_ge(tab_in, 16 * 8)
            with pool.Fori(0, B) as j:
                pool.wait_ge(xn_s.sem, xn_s.at(j, 0))
                layernorm_rstd(nc, g, pool, mv, veps, rstd, TT, mom_s, veps_s, rstd_s, j)
                pool.wait_ge(xres_in.sem, xres_in.at(j, 16))
                for i in range(TT):
                    last = nc.gpsimd.tensor_tensor(xres[:, i, :], xres[:, i, :], bo[:], ALU.add)
                last.then_inc(xb_s.sem, 1)
                for p in range(PAIRS):
                    for i in range(2):
                        m = 2 * p + i + 1
                        pool.wait_ge(shuf_s.sem, shuf_s.at(j, m))
                        nc.gpsimd.tensor_tensor(z[:, i, :], z[:, i, :], cos[:], ALU.mult).then_inc(cos_s.sem, 1)
                        nc.gpsimd.tensor_tensor(zs[:, i, :], zs[:, i, :], sin[:], ALU.mult).then_inc(sin_s.sem, 1)

        @block.vector
        def _(dve):
            dve.sem_inc(xn_s.sem, TT)
            dve.sem_inc(rope_s.sem, 3)
            dve.sem_inc(ptd_s.sem, 2)
            dve.sem_inc(olo_s.sem, 1)
            dve.sem_inc(xo_s.sem, 2)
            dve.wait_ge(tab_in, 16 * 8)
            nc.vector.tensor_scalar(bqs[:], bq[:], ADH ** -0.5, None, ALU.mult).then_inc(bqs_s, 1)
            for i, w in enumerate("qkvo"):
                dve.wait_ge(w_hi, i + 1)
                hi, lo = w_parts[w]
                nc.vector.tensor_tensor(lo[:], w_stage[:, i % 2, :], hi[:].bitcast(F32), ALU.subtract).then_inc(w_lo, 1)
            dve.wait_ge(zero_s, 1)

            def swap(j, p):
                for i in range(2):
                    hold(g, dve, z_s.sem, z_s.at(j, 2 * p + i + 1))
                    nc.vector.stream_shuffle(zs[:, i, :], z[:, i, :], mask=[k ^ 16 for k in range(32)]).then_inc(shuf_s.sem, 1)

            def rotate(j, p):
                par = p % 2
                dve.wait_ge(s_mm.sem, s_mm.at(j, 8 * (p - 1)))
                dve.wait_ge(sin_s.sem, sin_s.at(j, 2 * p + 1))
                for hh in range(2):
                    at = slice(hh * ADH, (hh + 1) * ADH)
                    nc.vector.tensor_tensor(qz[at, par, hh, :], z[at, 0, :], zs[at, 0, :], ALU.add).then_inc(rope_s.sem, 1)
                dve.wait_ge(sin_s.sem, sin_s.at(j, 2 * p + 2))
                nc.vector.tensor_tensor(kT[:, par, :], z[:, 1, :], zs[:, 1, :], ALU.add).then_inc(rope_s.sem, 1)

            def largest(j, h, i):
                qt = TT - 1 - i
                dve.wait_ge(s_mm.sem, s_mm.at(j, 4 * h + i + 1))
                nc.vector.tensor_reduce(nmax[:, h % 2, qt:qt + 1], ps_s[qt][:, 0:(qt + 1) * P], AX.X, ALU.max, negate=True)\
                    .then_inc(max_s.sem, 1)

            def copy_pt(j, h, kb):
                if h % 2 == 0 or True:
                    dve.wait_ge(pv_mm.sem, pv_mm.at(j, h // 2))
                dve.wait_ge(pt_mm.sem, pt_mm.at(j, 4 * h + kb + 1))
                nc.vector.tensor_copy(probT[:, h % 2, OFF[kb]:OFF[kb] + WIDTH[kb]], ps_pt[:, 0:WIDTH[kb]]).then_inc(ptd_s.sem, 1)

            def scale(j, h):
                dve.wait_ge(exp_s.sem, exp_s.at(j, 4 * h + 4))
                nc.vector.reciprocal(rinv[:, h % 2, :], sums[:, h % 2, :]).then_inc(rec_s.sem, 1)
                dve.wait_ge(rec_s.sem, rec_s.at(j, h + 1))
                for qt in range(TT):
                    t = prob[:, h % 2, qt, 0:(qt + 1) * P]
                    nc.vector.tensor_scalar(t, t, rinv[:, h % 2, qt:qt + 1], None, ALU.mult).then_inc(p_s.sem, 1)

            def low_part(j, p):
                dve.wait_ge(ohi_s.sem, ohi_s.at(j, p + 1))
                nc.vector.tensor_tensor(oT[1][:, p, :], ps_pv[:], oT[0][:, p, :].bitcast(F32), ALU.subtract).then_inc(olo_s.sem, 1)

            with dve.Fori(0, B) as j:
                dve.wait_ge(x_in.sem, x_in.at(j, 16))
                layernorm_stats(nc, g, dve, xin, stats, mv, TT, stats_s, mom_s, j)
                dve.wait_ge(rstd_s.sem, rstd_s.at(j, 1))
                dve.wait_ge(xt_mm.sem, xt_mm.at(j, 0))
                for i in range(TT):
                    nc.vector.tensor_scalar(xn[:, i, :], xin[:, i, :], mv[:, i, 0:1], rstd[:, i:i + 1],
                                            ALU.subtract, ALU.mult).then_inc(xn_s.sem, 1)
                for ch in range(DC):
                    dve.wait_ge(xhi_s.sem, xhi_s.at(j, ch + 1))
                    nc.vector.tensor_tensor(xT[1][:, ch, :], ps_z[ch][:], xT[0][:, ch, :].bitcast(F32), ALU.subtract)\
                        .then_inc(xlo_s.sem, 1)
                for m in range(2 * TT):
                    dve.wait_ge(v_mm.sem, v_mm.at(j, m + 1))
                    i, half = m // 2, m % 2
                    nc.vector.tensor_tensor(v[:, i, half * 512:(half + 1) * 512], ps_z[m % 2][:],
                                            bv[:, half * 512:(half + 1) * 512], ALU.add).then_inc(v_s.sem, 1)
                swap(j, 0)
                rotate(j, 0)
                for h in range(AH + 1):
                    if h < AH:
                        largest(j, h, 0)
                        largest(j, h, 1)
                    if h > 0:
                        copy_pt(j, h - 1, 2)
                    if h < AH:
                        largest(j, h, 2)
                    if h > 0:
                        copy_pt(j, h - 1, 3)
                    if h < AH:
                        largest(j, h, 3)
                        scale(j, h)
                    p = h // 2
                    if p + 1 < PAIRS:
                        (swap if h % 2 == 0 else rotate)(j, p + 1)
                    if h % 2 == 1 and h >= 3:
                        low_part(j, (h - 3) // 2)
                low_part(j, PAIRS - 1)
                dve.wait_ge(xb_s.sem, xb_s.at(j, 1))
                dve.wait_ge(out_s.sem, out_s.at(j, 0))
                for i in range(2):
                    dve.wait_ge(wo_mm.sem, wo_mm.at(j, i + 1))
                    nc.vector.tensor_tensor(xo[:, 2 * i:2 * i + 2, :], ps_z[i][:].rearrange("p (i d) -> p i d", i=2),
                                            xres[:, 2 * i:2 * i + 2, :], ALU.add).then_inc(xo_s.sem, 1)

        @block.scalar
        def _(act):
            act.sem_inc(exp_s.sem, 4)
            act.sem_inc(pta_s.sem, 2)
            act.sem_inc(out_s.sem, 16)
            for i, w in enumerate("qkvo"):
                act.wait_ge(w_in, 16 * (i + 1))
                nc.scalar.copy(w_parts[w][0][:], w_stage[:, i % 2, :]).then_inc(w_hi, 1)
            act.wait_ge(bqs_s, 1)

            def project(j, p, i):
                act.wait_ge(z_mm.sem, z_mm.at(j, 2 * p + i + 1))
                act.wait_ge(rope_s.sem, rope_s.at(j, 3 * p))
                bias, scale = ((bqs, ADH ** -0.5), (bk, 1.0))[i]
                nc.scalar.activation(z[:, i, :], ps_z[i][:], ACT.Identity, bias=bias[:, p:p + 1], scale=scale).then_inc(z_s.sem, 1)

            def exps(j, h, i):
                qt = TT - 1 - i
                act.wait_ge(max_s.sem, max_s.at(j, 4 * h + i + 1))
                act.wait_ge(pt_mm.sem, pt_mm.at(j, 4 * (h - 1)))
                nc.scalar.activation(prob[:, h % 2, qt, 0:(qt + 1) * P], ps_s[qt][:, 0:(qt + 1) * P], ACT.Exp,
                                     bias=nmax[:, h % 2, qt:qt + 1], accum_out=sums[:, h % 2, qt:qt + 1]).then_inc(exp_s.sem, 1)

            def copy_pt(j, h, kb):
                act.wait_ge(pv_mm.sem, pv_mm.at(j, h // 2))
                act.wait_ge(pt_mm.sem, pt_mm.at(j, 4 * h + kb + 1))
                nc.scalar.copy(probT[:, h % 2, OFF[kb]:OFF[kb] + WIDTH[kb]], ps_pt[:, 0:WIDTH[kb]]).then_inc(pta_s.sem, 1)

            def high_part(j, p):
                act.wait_ge(pv_mm.sem, pv_mm.at(j, p + 1))
                act.wait_ge(wo_mm.sem, wo_mm.at(j, 0))
                nc.scalar.copy(oT[0][:, p, :], ps_pv[:]).then_inc(ohi_s.sem, 1)

            with act.Fori(0, B) as j:
                act.wait_ge(z_mm.sem, z_mm.at(j, 0))
                for ch in range(DC):
                    act.wait_ge(xt_mm.sem, xt_mm.at(j, ch + 1))
                    nc.scalar.copy(xT[0][:, ch, :], ps_z[ch][:]).then_inc(xhi_s.sem, 1)
                project(j, 0, 0)
                project(j, 0, 1)
                for h in range(AH + 1):
                    if h > 0:
                        copy_pt(j, h - 1, 0)
                    if h < AH:
                        exps(j, h, 0)
                    if h > 0:
                        copy_pt(j, h - 1, 1)
                    if h < AH:
                        for i in range(1, TT):
                            exps(j, h, i)
                    if h % 2 == 0 and h // 2 + 1 < PAIRS:
                        project(j, h // 2 + 1, 0)
                        project(j, h // 2 + 1, 1)
                    if h % 2 == 1 and h >= 3:
                        high_part(j, (h - 3) // 2)
                high_part(j, PAIRS - 1)

        @block.tensor
        def _(pe):
            pe.sem_inc(xt_mm.sem, DC)
            pe.sem_inc(z_mm.sem, 2 * PAIRS)
            pe.sem_inc(s_mm.sem, 8)
            pe.sem_inc(pt_mm.sem, 8)
            pe.sem_inc(pv_mm.sem, 1)
            pe.sem_inc(wo_mm.sem, 2)
            pe.wait_ge(w_lo, 4)
            pe.wait_ge(tab_in, 16 * 8)

            def project(j, p, i, freed):
                pe.wait_ge(*freed)
                w = (wq, wk)[i]
                products(ps_z[i][:], [[part[:, ch, p * P:(p + 1) * P] for ch in range(DC)] for part in w],
                         [[part[:, ch, :] for ch in range(DC)] for part in xT]).then_inc(z_mm.sem, 1)

            def scores(j, h, i):
                qt, par, width = TT - 1 - i, (h // 2) % 2, (TT - i) * P
                if i == 0 and h % 2 == 0:
                    pe.wait_ge(rope_s.sem, rope_s.at(j, 3 * (h // 2) + 3))
                pe.wait_ge(exp_s.sem, exp_s.at(j, 4 * (h - 1) + i + 1))
                nc.tensor.matmul(ps_s[qt][:, 0:width], qz[:, par, h % 2, qt * P:(qt + 1) * P], kT[:, par, 0:width],
                                 start=True, stop=False)
                nc.tensor.matmul(ps_s[qt][:, qt * P:width], identb[:], masked[:], start=False, stop=True).then_inc(s_mm.sem, 1)

            def transposes(j, h, kb):
                if kb == 0:
                    pe.wait_ge(p_s.sem, p_s.at(j, 4 * h + 4))
                    pe.wait_ge(ptd_s.sem, ptd_s.at(j, 2 * h))
                elif kb < 3:
                    pe.wait_ge(pta_s.sem, pta_s.at(j, 2 * h + kb))
                else:
                    pe.wait_ge(ptd_s.sem, ptd_s.at(j, 2 * h + 1))
                for qt in range(kb, TT):
                    last = nc.tensor.transpose(ps_pt[:, (qt - kb) * P:(qt - kb + 1) * P],
                                               prob[:, h % 2, qt, kb * P:(kb + 1) * P], g.ident[:])
                last.then_inc(pt_mm.sem, 1)

            def mix(j, p):
                pe.wait_ge(pta_s.sem, pta_s.at(j, 4 * p + 4))
                pe.wait_ge(ptd_s.sem, ptd_s.at(j, 4 * p + 4))
                pe.wait_ge(olo_s.sem, olo_s.at(j, p))
                if p == 0:
                    pe.wait_ge(v_s.sem, v_s.at(j, 2 * TT))
                for kb in range(TT):
                    for hh in range(2):
                        h = 2 * p + hh
                        last = nc.tensor.matmul(ps_pv[hh * ADH:(hh + 1) * ADH, kb * P:S], v[:, kb, h * ADH:(h + 1) * ADH],
                                                probT[:, hh, OFF[kb]:OFF[kb] + WIDTH[kb]], start=(kb == 0), stop=(kb == TT - 1))
                last.then_inc(pv_mm.sem, 1)

            with pe.Fori(0, B) as j:
                pe.wait_ge(xn_s.sem, xn_s.at(j, TT))
                for ch in range(DC):
                    pe.wait_ge(xo_s.sem, xo_s.at(j, ch - 1))
                    for i in range(TT):
                        last = nc.tensor.transpose(ps_z[ch][:, i * P:(i + 1) * P], xn[:, i, ch * P:(ch + 1) * P], g.ident[:])
                    last.then_inc(xt_mm.sem, 1)
                pe.wait_ge(xlo_s.sem, xlo_s.at(j, DC))
                for m in range(2 * TT):
                    i, half = m // 2, m % 2
                    if m >= 2:
                        pe.wait_ge(v_s.sem, v_s.at(j, m - 1))
                    products(ps_z[m % 2][:], [[part[:, ch, i * P:(i + 1) * P] for ch in range(DC)] for part in xT],
                             [[part[:, ch, half * 512:(half + 1) * 512] for ch in range(DC)] for part in wv]).then_inc(v_mm.sem, 1)
                project(j, 0, 0, (v_s.sem, v_s.at(j, 2 * TT - 1)))
                project(j, 0, 1, (v_s.sem, v_s.at(j, 2 * TT)))
                for h in range(AH + 1):
                    p = h // 2
                    if h % 2 == 1 and h >= 3:
                        mix(j, (h - 3) // 2)
                    for i in range(TT):
                        if h > 0:
                            transposes(j, h - 1, i)
                        if h < AH:
                            scores(j, h, i)
                    if h % 2 == 0 and p + 1 < PAIRS:
                        project(j, p + 1, 0, (z_s.sem, z_s.at(j, 2 * p + 1)))
                        project(j, p + 1, 1, (z_s.sem, z_s.at(j, 2 * p + 2)))
                mix(j, PAIRS - 1)
                pe.wait_ge(olo_s.sem, olo_s.at(j, PAIRS))
                for i in range(2):
                    pe.wait_ge(z_s.sem, z_s.at(j, 2 * PAIRS - 1 + i))
                    for t in range(2):
                        at = slice((2 * i + t) * P, (2 * i + t + 1) * P)
                        last = products(ps_z[i][:, t * D:(t + 1) * D], [[part[:, p, at] for p in range(PAIRS)] for part in oT],
                                        [[part[:, p, :] for p in range(PAIRS)] for part in wo])
                    last.then_inc(wo_mm.sem, 1)


class Shared:
    pass


def macaron_block(nc, io):
    sems = ExitStack()
    with sems, ExitStack() as s:
        made = {}

        def sem(name):
            if name not in made:
                made[name] = sems.enter_context(nc.semaphore(name))
            return made[name]

        sb = lambda nm, sh: s.enter_context(nc.sbuf_tensor("sh_" + nm, sh, F32))
        g = Shared()
        g.ident, g.blkmask = sb("ident", [P, P]), sb("blkmask", [P, P])
        g.mhalf = sb("mhalf", [P, TT])
        g.G, g.cb = sb("G", [P, DC, HS]), sb("cb", [P, DC])
        g.wv_pad, g.bv_pad = sb("wv_pad", [P, DC, FH, QUAD]), sb("bv_pad", [P, 4])
        g.wo_pad = sb("wo_pad", [P, 4, D])
        g.cwqT, g.cwo = sb("cwqT", [P, DC, D]), sb("cwo", [P, DC, D])
        x1 = nc.dram_tensor("x_after_ffn", (B, S, D), F32, kind="Internal").ap()
        x2 = nc.dram_tensor("x_after_attention", (B, S, D), F32, kind="Internal").ap()
        mhalf_s = sem("mhalf")
        g.held = sem("held")
        with nc.Block() as block:
            @block.gpsimd
            def _(pool):
                nc.gpsimd.memset(g.mhalf[:], -0.5).then_inc(mhalf_s, 1)
                pool.wait_ge(mhalf_s, 1)
        setup_phase(nc, io, g, sem)

        def ffn(f, src, dst):
            with ExitStack() as t:
                kT = t.enter_context(nc.sbuf_tensor(f"ffn{f}_kT", [P, DC, NS, B], F32))
                vT = t.enter_context(nc.sbuf_tensor(f"ffn{f}_vT", [P, DC, NS, B], F32))
                with ExitStack() as u:
                    at_all = u.enter_context(nc.sbuf_tensor(f"ffn{f}_at", [P, DC, HS, B], F32))
                    dispatch_phase(nc, g, sem, f, src, at_all)
                    expert_phase(nc, io, g, sem, f, at_all, kT, vT)
                combine_phase(nc, io, g, sem, f, src, dst, kT, vT)

        ffn(0, io["x"], x1)
        ffn_sems = [h for k, h in made.items() if k.startswith(("dis_", "ex_", "com_"))]
        attention_phase(nc, io, g, sem, x1, x2)
        with nc.Block() as block:
            @block.sync
            def _(sp):
                for h in ffn_sems:
                    sp.sem_clear(h)
        ffn(1, x2, io["out"])



def _rotary_order():
    half = ADH // 2
    return np.concatenate([np.arange(0, 16), half + np.arange(0, 16), np.arange(16, 32), half + np.arange(16, 32)])


def _rotary_tables():
    inv = (np.float32(1.0) / np.float32(10000.0) ** (np.arange(0, ADH, 2, dtype=np.float32) / np.float32(ADH))).astype(np.float32)
    ang = np.arange(S, dtype=np.float32)[:, None] * inv[None, :]
    order = _rotary_order()
    freq, sign = order % (ADH // 2), np.where(order < ADH // 2, -1.0, 1.0).astype(np.float32)
    cos, sin = np.cos(ang)[:, freq].T, np.sin(ang)[:, freq].T * sign[:, None]
    return (np.ascontiguousarray(np.tile(t, (2, 1)).astype(np.float32)) for t in (cos, sin))


def kernel(**inputs):
    import concourse.bacc as bacc
    from concourse.bass_utils import run_bass_kernel_spmd
    import ml_dtypes

    a = {k.replace("L0_attn_", "a_").replace("L0_ffn_", ""): np.ascontiguousarray(v) for k, v in inputs.items()}
    cols = lambda v: np.ascontiguousarray(v.reshape(-1, P).T)
    rows = lambda v: np.ascontiguousarray(np.broadcast_to(v, (P,) + v.shape))
    byexp = lambda v: np.ascontiguousarray(v.reshape(NE, DC, P).transpose(2, 1, 0))
    pairs = lambda v: np.ascontiguousarray(np.broadcast_to(v[:, None, :], (NE, QUAD, F)).reshape(NE // 2, 2 * QUAD, F))
    order = _rotary_order()
    perm = lambda v: np.ascontiguousarray(v.reshape(-1, AH, ADH)[:, :, order].reshape(v.shape))
    cos, sin = _rotary_tables()
    bv_pad = np.zeros((4, 4, QUAD), np.float32)
    bv_pad[:, :, :FDH] = a["d_bv"].reshape(4, 4, FDH)
    wk, wv = a["a_Wkv"][:, :AW], a["a_Wkv"][:, AW:]
    arrays = {
        "x": a["a_x"], "sqT": np.ascontiguousarray(a["slot_query"].reshape(NS, DC, P).transpose(2, 1, 0)),
        "sq_rows": np.repeat(a["slot_query"][0], B, axis=0),
        "d_Wq": a["d_Wq"], "d_WkT": np.ascontiguousarray(a["d_Wk"].T), "d_Wv": a["d_Wv"], "d_Wo": a["d_Wo"],
        "d_bq": cols(a["d_bq"]), "d_bk": cols(a["d_bk"]), "d_bv_pad": np.ascontiguousarray(bv_pad.reshape(4, P).T),
        "d_bo": rows(a["d_bo"]),
        "c_WqT": np.ascontiguousarray(a["c_Wq"].T), "c_Wk": a["c_Wk"], "c_Wv": a["c_Wv"], "c_Wo": a["c_Wo"],
        "c_bq": np.ascontiguousarray(np.repeat(cols(a["c_bq"])[:, :, None], P, axis=2)),
        "c_bk": cols(a["c_bk"]), "c_bv": cols(a["c_bv"]),
        "c_bo": np.ascontiguousarray(np.broadcast_to(a["c_bo"], (P, 2, D))),
        "e_gT": byexp(a["e_ln_g"]), "e_bT": byexp(a["e_ln_b"]), "e_b2T": byexp(a["e_b2"]),
        "e_W1": a["e_W1"], "e_Wg": a["e_Wg"], "e_W2": a["e_W2"], "e_b1": pairs(a["e_b1"]), "e_bg": pairs(a["e_bg"]),
        "a_Wq": perm(a["a_Wq"]), "a_Wk": perm(np.ascontiguousarray(wk)), "a_Wv": np.ascontiguousarray(wv), "a_Wo": a["a_Wo"],
        "a_bq": cols(perm(a["a_bq"])), "a_bk": cols(perm(np.ascontiguousarray(a["a_bkv"][:AW]))),
        "a_bv": rows(np.ascontiguousarray(a["a_bkv"][AW:])), "a_bo": rows(a["a_bo"]),
        "cos": cos, "sin": sin, "ident": np.eye(P, dtype=np.float32), "identb": np.eye(P).astype(ml_dtypes.bfloat16),
        "blkmask": np.repeat(np.repeat(np.eye(HPC, dtype=np.float32), FDH, axis=0), NS, axis=1),
        "masked": np.where(np.arange(P)[None, :] > np.arange(P)[:, None], MASKED, 0.0).astype(ml_dtypes.bfloat16),
    }
    nc = bacc.Bacc("TRN2", target_bir_lowering=False, num_devices=1)
    io = {k: nc.dram_tensor("in_" + k, v.shape, mybir.dt.from_np(v.dtype), kind="ExternalInput").ap() for k, v in arrays.items()}
    io["out"] = nc.dram_tensor("out_x", (B, S, D), F32, kind="ExternalOutput").ap()
    macaron_block(nc, io)
    r = run_bass_kernel_spmd(nc, [{"in_" + k: v for k, v in arrays.items()}], core_ids=[0])
    return r.results[0]["out_x"]
```

```python
from contextlib import ExitStack

import numpy as np

import concourse.bass as bass
from concourse import mybir

F32 = mybir.dt.float32
F32R = mybir.dt.float32r
BF16 = mybir.dt.bfloat16
ALU = mybir.AluOpType
ACT = mybir.ActivationFunctionType
AX = mybir.AxisListType

P = 128
B, S, D = 16, 512, 256
TT = S // P
DC = D // P
FH, FDH = 16, 16
NS = 16
HS = FH * NS
HPC = P // FDH
NE, F = 16, 1024
FK = F // P
AH, ADH = 16, 64
AW = AH * ADH
PAIRS = AH // 2
QUAD = 32
EPS = 1e-5
MASKED = -3.0e38


class Count:

    def __init__(self, sem, per, credit=0):
        self.sem, self.per, self.credit = sem, per, credit

    def at(self, j, n):
        assert n + self.credit >= 1 or not isinstance(j, int) or j * self.per + n + self.credit >= 1
        return j * self.per + (n + self.credit)


def hold(g, eng, sem, value):
    eng.wait_ge(sem, value)
    eng.sem_inc(g.held, 1)


def bcast(ap, axis, n):
    shape = list(ap.shape)
    return ap.unsqueeze(axis).broadcast_to(shape[:axis] + [n] + shape[axis:])


def setup_phase(nc, io, g, sem):
    loaded = sem("setup_loaded")
    q_mm, q_done, blk_done, g_mm, g_done, zeroed, scaled = (
        sem(f"setup_{n}") for n in ("q_mm", "q_done", "blk_done", "g_mm", "g_done", "zeroed", "scaled"))
    LOADS = 12 + 4
    with ExitStack() as s:
        sb = lambda n, sh: s.enter_context(nc.sbuf_tensor(n, sh, F32))
        wq, wkT = sb("su_wq", [P, DC, D]), sb("su_wkT", [P, DC, D])
        sqT, bq, bk = sb("su_sqT", [P, DC, NS]), sb("su_bq", [P, DC]), sb("su_bk", [P, DC])
        qT, qblk = sb("su_qT", [P, DC, NS]), sb("su_qblk", [P, DC, HPC, NS])
        ps_q = s.enter_context(nc.psum_tensor("su_psq", [P, DC, NS], F32))
        ps_g = s.enter_context(nc.psum_tensor("su_psg", [P, DC, HS], F32))
        ps_c = s.enter_context(nc.psum_tensor("su_psc", [P, DC, 2], F32))
        block = s.enter_context(nc.Block())

        @block.sync
        def _(sp):
            sp.wait_ge(zeroed, 2)
            for dst, src in (
                (g.ident[:], io["ident"]), (g.blkmask[:], io["blkmask"]),
                (wq[:], io["d_Wq"].rearrange("(c p) n -> p c n", p=P)),
                (wkT[:], io["d_WkT"].rearrange("(c p) n -> p c n", p=P)),
                (sqT[:], io["sqT"]), (bq[:], io["d_bq"]), (bk[:], io["d_bk"]),
                *((g.wv_pad[:, c, :, 0:FDH], io["d_Wv"].rearrange("(c p) (h e) -> c p h e", p=P, e=FDH)[c]) for c in range(DC)),
                (g.bv_pad[:], io["d_bv_pad"]),
                (g.cwqT[:], io["c_WqT"].rearrange("(c p) n -> p c n", p=P)),
                (g.cwo[:], io["c_Wo"].rearrange("(c p) n -> p c n", p=P)),
            ):
                sp.dma_start(dst, src).then_inc(loaded, 16)
            for q in range(4):
                sp.dma_start(g.wo_pad[q * QUAD:q * QUAD + FDH, :, :],
                             io["d_Wo"].rearrange("(t q e) n -> q e t n", q=4, e=FDH)[q]).then_inc(loaded, 16)

        @block.vector
        def _(dve):
            nc.vector.memset(g.wv_pad[:], 0.0).then_inc(zeroed, 1)
            nc.vector.memset(g.wo_pad[:], 0.0).then_inc(zeroed, 1)
            dve.wait_ge(q_mm, 1)
            for c in range(DC):
                nc.vector.tensor_scalar(qT[:, c, :], ps_q[:, c, :], bq[:, c:c + 1], FDH ** -0.5,
                                        ALU.add, ALU.mult).then_inc(q_done, 1)
            dve.wait_ge(q_done, DC)
            for c in range(DC):
                nc.vector.tensor_tensor(qblk[:, c], g.blkmask[:].rearrange("p (h s) -> p h s", s=NS),
                                        bcast(qT[:, c, :], 1, HPC), ALU.mult).then_inc(blk_done, 1)
            dve.wait_ge(g_mm, 1)
            nc.vector.tensor_copy(g.G[:], ps_g[:]).then_inc(g_done, 1)
            nc.vector.tensor_copy(g.cb[:], ps_c[:, :, 0]).then_inc(g_done, 1)

        @block.tensor
        def _(pe):
            pe.wait_ge(loaded, 16 * LOADS)
            for m in range(DC):
                for c in range(DC):
                    last = nc.tensor.matmul(ps_q[:, m, :], wq[:, c, m * P:(m + 1) * P], sqT[:, c, :],
                                            start=(c == 0), stop=(c == DC - 1))
            last.then_inc(q_mm, 1)
            pe.wait_ge(blk_done, DC)
            for m in range(DC):
                for c in range(DC):
                    nc.tensor.matmul(ps_g[:, m, c * P:(c + 1) * P], wkT[:, c, m * P:(m + 1) * P],
                                     qblk[:, c].rearrange("p h s -> p (h s)"), start=True, stop=True)
            for c in range(DC):
                last = nc.tensor.matmul(ps_c[:, c, 0:1], qblk[:, c].rearrange("p h s -> p (h s)"),
                                        bk[:, c:c + 1], start=True, stop=True)
            last.then_inc(g_mm, 1)


def layernorm_stats(nc, g, dve, x, stats, mv, tiles, stats_sem, mom_sem, j):
    for i in range(tiles):
        nc.vector.bn_stats(stats[:, i, :], x[:, i, :]).then_inc(stats_sem.sem, 1)
    hold(g, dve, stats_sem.sem, stats_sem.at(j, tiles))
    for i in range(tiles):
        nc.vector.bn_aggr(mv[:, i, :], stats[:, i, :]).then_inc(mom_sem.sem, 1)


def layernorm_rstd(nc, g, pool, mv, veps, rstd, tiles, mom_sem, veps_sem, rstd_sem, j):
    hold(g, pool, mom_sem.sem, mom_sem.at(j, tiles))
    nc.gpsimd.tensor_scalar(veps[:, 0:tiles], mv[:, 0:tiles, 1], EPS, None, ALU.add).then_inc(veps_sem.sem, 1)
    pool.wait_ge(veps_sem.sem, veps_sem.at(j, 1))
    nc.gpsimd.tensor_tensor(rstd[:, 0:tiles], veps[:, 0:tiles], g.mhalf[:, 0:tiles], ALU.pow).then_inc(rstd_sem.sem, 1)


def dispatch_phase(nc, g, sem, f, x_dram, at_all):
    n = lambda x: f"dis_{x}"
    name = lambda x: f"dis{f}_{x}"
    x_in = [sem(n(f"x_in{i}")) for i in range(2)]
    c = lambda x, per: Count(sem(n(x)), per)
    stats_s, mom_s, veps_s, rstd_s, xn_s = c("stats", TT), c("moments", TT), c("veps", 1), c("rstd", 1), c("xn", TT)
    xt_mm, xt_s = c("xt_mm", DC), c("xt", DC)
    score_mm, max_s, bias_s, exp_s, recip_s, p_s = (
        c("score_mm", DC), c("max", DC), c("bias", DC), c("exp", DC), c("recip", 1), c("p", DC))
    pt_mm, pt_s, at_mm, at_s = c("pt_mm", 2), c("pt", 2), c("at_mm", 1), c("at", 1)
    with ExitStack() as s:
        sb = lambda nm, sh: s.enter_context(nc.sbuf_tensor(name(nm), sh, F32))
        pb = lambda nm, sh: s.enter_context(nc.psum_tensor(name(nm), sh, F32))
        xin, xn = sb("b_x", [P, 2, TT, D]), sb("b_xn", [P, 2, TT, D])
        stats, mv = sb("b_stats", [P, TT, 6]), sb("b_mv", [P, TT, 2])
        veps, rstd = sb("b_veps", [P, TT]), sb("b_rstd", [P, TT])
        xnT = sb("b_xnT", [P, DC, S])
        nmax, ebias, sums, rinv = (sb(x, [P, DC]) for x in ("b_nmax", "b_ebias", "b_sums", "b_rinv"))
        prob, probT = sb("b_prob", [P, 2, DC, S]), sb("b_probT", [P, TT, HS])
        ps_xt, ps_s = pb("ps_xt", [P, DC, S]), pb("ps_s", [P, DC, S])
        ps_pt, ps_at = pb("ps_pt", [P, TT, HS]), pb("ps_at", [P, DC, HS])
        block = s.enter_context(nc.Block())

        @block.sync
        def _(sp):
            def load(j, par):
                sp.dma_start(xin[:, par], x_dram[j].rearrange("(i p) d -> p i d", p=P)).then_inc(x_in[par], 16)

            load(0, 0)
            load(1, 1)
            with sp.Fori(0, B // 2 - 1) as k:
                for par in range(2):
                    hold(g, sp, xn_s.sem, xn_s.at(2 * k + par, TT))
                    load(2 * k + 2 + par, par)

        @block.vector
        def _(dve):
            def moments(j, h, par, first=False):
                dve.wait_ge(x_in[par], (h + 1) * 16)
                if not first:
                    dve.wait_ge(xn_s.sem, xn_s.at(j, 0))
                layernorm_stats(nc, g, dve, xin[:, par], stats, mv, TT, stats_s, mom_s, j)

            def normalise(j, par, first=False):
                dve.wait_ge(rstd_s.sem, rstd_s.at(j, 1))
                if not first:
                    dve.wait_ge(at_mm.sem, at_mm.at(j, -1))
                for i in range(TT):
                    nc.vector.tensor_scalar(xn[:, par, i, :], xin[:, par, i, :], mv[:, i, 0:1], rstd[:, i:i + 1],
                                            ALU.subtract, ALU.mult).then_inc(xn_s.sem, 1)

            def shift(j):
                for m in range(DC):
                    dve.wait_ge(score_mm.sem, score_mm.at(j, m + 1))
                    nc.vector.tensor_reduce(nmax[:, m:m + 1], ps_s[:, m, :], AX.X, ALU.max, negate=True)\
                        .then_inc(max_s.sem, 1)
                    dve.wait_ge(max_s.sem, max_s.at(j, m + 1))
                    nc.vector.scalar_tensor_tensor(ebias[:, m:m + 1], nmax[:, m:m + 1], g.cb[:, m:m + 1],
                                                   g.cb[:, m:m + 1], ALU.subtract, ALU.add).then_inc(bias_s.sem, 1)

            def scale(j, par):
                dve.wait_ge(exp_s.sem, exp_s.at(j, DC))
                nc.vector.reciprocal(rinv[:], sums[:]).then_inc(recip_s.sem, 1)
                dve.wait_ge(recip_s.sem, recip_s.at(j, 1))
                for m in range(DC):
                    nc.vector.tensor_scalar(prob[:, par, m, :], prob[:, par, m, :], rinv[:, m:m + 1], None,
                                            ALU.mult).then_inc(p_s.sem, 1)

            def keep(j):
                dve.wait_ge(at_mm.sem, at_mm.at(j, 1))
                nc.vector.tensor_copy(at_all[:, :, :, j], ps_at[:]).then_inc(at_s.sem, 1)

            def step(j, h, par, first=False, last=False):
                if not last:
                    moments(j + 1, h + par, 1 - par)
                shift(j)
                scale(j, par)
                if not first:
                    keep(j - 1)
                if not last:
                    normalise(j + 1, 1 - par, first)

            moments(0, 0, 0, True)
            normalise(0, 0, True)
            step(0, 0, 0, first=True)
            with dve.Fori(0, B // 2 - 1) as k:
                step(2 * k + 1, k, 1)
                step(2 * k + 2, k + 1, 0)
            step(B - 1, B // 2 - 1, 1, last=True)
            keep(B - 1)

        @block.gpsimd
        def _(pool):
            layernorm_rstd(nc, g, pool, mv, veps, rstd, TT, mom_s, veps_s, rstd_s, 0)
            with pool.Fori(1, B) as j:
                pool.wait_ge(xn_s.sem, xn_s.at(j, 0))
                layernorm_rstd(nc, g, pool, mv, veps, rstd, TT, mom_s, veps_s, rstd_s, j)

        @block.tensor
        def _(pe):
            def transpose_x(j, par, first=False):
                pe.wait_ge(xn_s.sem, xn_s.at(j, TT))
                if not first:
                    pe.wait_ge(xt_s.sem, xt_s.at(j, 0))
                for c in range(DC):
                    for i in range(TT):
                        last = nc.tensor.transpose(ps_xt[:, c, i * P:(i + 1) * P],
                                                   xn[:, par, i, c * P:(c + 1) * P], g.ident[:])
                    last.then_inc(xt_mm.sem, 1)

            def scores(j, first):
                pe.wait_ge(xt_s.sem, xt_s.at(j, DC))
                if not first:
                    pe.wait_ge(exp_s.sem, exp_s.at(j, 0))
                for m in range(DC):
                    for c in range(DC):
                        last = nc.tensor.matmul(ps_s[:, m, :], g.G[:, c, m * P:(m + 1) * P], xnT[:, c, :],
                                                start=(c == 0), stop=(c == DC - 1))
                    last.then_inc(score_mm.sem, 1)

            def transpose_p(j, par, first=False):
                pe.wait_ge(p_s.sem, p_s.at(j, DC))
                if not first:
                    pe.wait_ge(pt_s.sem, pt_s.at(j, 0))
                for half in range(2):
                    for i in range(2 * half, 2 * half + 2):
                        for m in range(DC):
                            last = nc.tensor.transpose(ps_pt[:, i, m * P:(m + 1) * P],
                                                       prob[:, par, m, i * P:(i + 1) * P], g.ident[:])
                    last.then_inc(pt_mm.sem, 1)

            def gather(j, par, first=False):
                pe.wait_ge(pt_s.sem, pt_s.at(j, 2))
                if not first:
                    pe.wait_ge(at_s.sem, at_s.at(j, 0))
                for c in range(DC):
                    for i in range(TT):
                        last = nc.tensor.matmul(ps_at[:, c, :], xn[:, par, i, c * P:(c + 1) * P], probT[:, i, :],
                                                start=(i == 0), stop=(i == TT - 1))
                last.then_inc(at_mm.sem, 1)

            def step(j, par, first=False, second=False, last=False):
                if not first:
                    transpose_p(j - 1, 1 - par, second)
                scores(j, first)
                if not first:
                    gather(j - 1, 1 - par, second)
                if not last:
                    transpose_x(j + 1, 1 - par)

            transpose_x(0, 0, True)
            step(0, 0, first=True)
            step(1, 1, second=True)
            step(2, 0)
            with pe.Fori(1, B // 2 - 1) as k:
                step(2 * k + 1, 1)
                step(2 * k + 2, 0)
            step(B - 1, 1, last=True)
            transpose_p(B - 1, 1)
            gather(B - 1, 1)

        @block.scalar
        def _(act):
            def copy_x(j, first=False):
                if not first:
                    act.wait_ge(score_mm.sem, score_mm.at(j, 0))
                for c in range(DC):
                    act.wait_ge(xt_mm.sem, xt_mm.at(j, c + 1))
                    nc.scalar.copy(xnT[:, c, :], ps_xt[:, c, :]).then_inc(xt_s.sem, 1)

            def exps(j, par, early=False):
                if not early:
                    act.wait_ge(pt_mm.sem, pt_mm.at(j, -2))
                for m in range(DC):
                    act.wait_ge(bias_s.sem, bias_s.at(j, m + 1))
                    nc.scalar.activation(prob[:, par, m, :], ps_s[:, m, :], ACT.Exp, bias=ebias[:, m:m + 1],
                                         accum_out=sums[:, m:m + 1]).then_inc(exp_s.sem, 1)

            def copy_p(j, first=False):
                if not first:
                    act.wait_ge(at_mm.sem, at_mm.at(j, 0))
                for half in range(2):
                    act.wait_ge(pt_mm.sem, pt_mm.at(j, half + 1))
                    nc.scalar.copy(probT[:, 2 * half:2 * half + 2, :], ps_pt[:, 2 * half:2 * half + 2, :])\
                        .then_inc(pt_s.sem, 1)

            def step(j, par, first=False, second=False, last=False):
                if not first:
                    copy_p(j - 1, second)
                exps(j, par, first or second)
                if not last:
                    copy_x(j + 1)

            copy_x(0, True)
            step(0, 0, first=True)
            step(1, 1, second=True)
            step(2, 0)
            with act.Fori(1, B // 2 - 1) as k:
                step(2 * k + 1, 1)
                step(2 * k + 2, 0)
            step(B - 1, 1, last=True)
            copy_p(B - 1)


def expert_phase(nc, io, g, sem, f, at_all, kT, vT):
    n = lambda x: f"ex_{x}"
    name = lambda x: f"ex{f}_{x}"
    one = lambda x: sem(n(x))
    c = lambda x, per: Count(sem(n(x)), per)
    NP = NE // 2
    R = 2 * QUAD
    tab_in, padded, rows_s, v_mm, v_s, o_mm, o_s = (one(x) for x in ("tab", "pad", "rows", "v_mm", "v", "o_mm", "o"))
    stats_s, mom_s, veps_s, rstd_s = c("stats", 2), c("moments", 2), c("veps", 1), c("rstd", 1)
    h0_s, hT_mm, hg_s, hb_s, oT_s = one("h0"), one("hT_mm"), one("hg"), one("hb"), one("oT")
    w_in = [[one(f"{w}_in{i}") for i in range(2)] for w in ("w1", "wg", "w2")]
    stage_s, up_mm, pre_s, silu_s, ug_s = c("stage", 1), c("up_mm", 2), c("pre", 2), c("silu", 2), c("ug", 1)
    ugT_mm, ugT_s, y_mm, y_s, yT_mm, on_s = c("ugT_mm", 1), c("ugT", 1), c("y_mm", 1), c("y", 1), c("yT_mm", 1), c("on", 1)
    kv_mm, kv_s, bk_s = one("kv_mm"), one("kv"), one("bk")
    with ExitStack() as s:
        sb = lambda nm, sh: s.enter_context(nc.sbuf_tensor(name(nm), sh, F32))
        pb = lambda nm, sh: s.enter_context(nc.psum_tensor(name(nm), sh, F32))
        sq, bo = sb("t_sq", [P, 2, D]), sb("t_bo", [P, D])
        gT, bT, b2T = (sb(x, [P, DC, NE]) for x in ("t_gT", "t_bT", "t_b2T"))
        cwk, cwv = sb("t_cwk", [P, DC, D]), sb("t_cwv", [P, DC, D])
        bk, bv, bk4 = sb("t_bk", [P, DC]), sb("t_bv", [P, DC]), sb("t_bk4", [P, DC])
        attnT = sb("t_attnT", [P, 4, HS])
        o, h0 = sb("t_o", [P, 2, D]), sb("t_h0", [P, 2, D])
        stats, mv, veps, rstd = sb("t_st", [P, 2, 6]), sb("t_mv", [P, 2, 2]), sb("t_ve", [P, 2]), sb("t_rs", [P, 2])
        hg = sb("t_hg", [P, DC, NE, B])
        hP = sb("t_hP", [P, DC, NE, QUAD])
        oT, onT = sb("t_oT", [P, DC, NE, B]), sb("t_onT", [P, DC, NE, B])
        w1, wg = sb("t_w1", [P, 2, 2, DC, F]), sb("t_wg", [P, 2, 2, DC, F])
        w2 = sb("t_w2", [P, 2, 2, FK, D])
        b1, bg = sb("t_b1", [R, 2, F]), sb("t_bg", [R, 2, F])
        stage = sb("t_stage", [P, 2, DC, 2, QUAD])
        ub, gb = sb("t_ub", [R, F]), sb("t_gb", [R, F])
        ugT, y = sb("t_ugT", [P, FK, R]), sb("t_y", [R, D])
        ps_u, ps_g = pb("ps_u", [P, F]), pb("ps_g", [P, F])
        ps_ugT, ps_y, ps_yT, ps_kv = pb("ps_ugT", [P, FK, R]), pb("ps_y", [P, 512]), pb("ps_yT", [P, DC, R]), pb("ps_kv", [P, 2, 256])
        ps_v = ps_u[:].rearrange("p (t r) -> p t r", t=4)
        ps_o = ps_g[:, 0:2 * D].rearrange("p (m d) -> p m d", m=2)
        ps_hT = ps_ugT[:].rearrange("p k r -> p (k r)").rearrange("p (c r) -> p c r", c=DC)
        ps_oT = ps_y[:].rearrange("p (c r) -> p c r", c=DC)
        TABS = 9
        block = s.enter_context(nc.Block())

        @block.sync
        def _(sp):
            def load(pr, par):
                for (w, src, bias, bsrc), at in zip((
                        (w1, io["e_W1"], b1, io["e_b1"]), (wg, io["e_Wg"], bg, io["e_bg"])), w_in):
                    for e in range(2):
                        sp.dma_start(w[:, par, e], src[2 * pr + e].rearrange("(c p) f -> p c f", p=P)).then_inc(at[par], 16)
                    sp.dma_start(bias[:, par, :], bsrc[pr]).then_inc(at[par], 16)
                for e in range(2):
                    sp.dma_start(w2[:, par, e], io["e_W2"][2 * pr + e].rearrange("(p k) d -> p k d", k=FK))\
                        .then_inc(w_in[2][par], 16)

            for dst, src in ((sq[:], io["sq_rows"].rearrange("(m p) d -> p m d", p=P)), (bo[:], io["d_bo"]),
                             (gT[:], io["e_gT"]), (bT[:], io["e_bT"]), (b2T[:], io["e_b2T"]),
                             (cwk[:], io["c_Wk"].rearrange("(c p) n -> p c n", p=P)),
                             (cwv[:], io["c_Wv"].rearrange("(c p) n -> p c n", p=P)),
                             (bk[:], io["c_bk"]), (bv[:], io["c_bv"])):
                sp.dma_start(dst, src).then_inc(tab_in, 16)
            load(0, 0)
            load(1, 1)
            with sp.Fori(0, NP // 2 - 1) as k:
                for par in range(2):
                    hold(g, sp, pre_s.sem, pre_s.at(2 * k + par, 2))
                    hold(g, sp, y_mm.sem, y_mm.at(2 * k + par, 1))
                    load(2 * k + 2 + par, par)

        @block.vector
        def _(dve):
            nc.vector.memset(hP[:], 0.0).then_inc(padded, 1)
            dve.wait_ge(tab_in, 16 * TABS)
            nc.vector.tensor_scalar(bk4[:], bk[:], FDH ** -0.5, None, ALU.mult).then_inc(bk_s, 1)
            for m in range(2):
                nc.vector.tensor_tensor(sq[:, m, :], sq[:, m, :], bo[:], ALU.add).then_inc(rows_s, 1)
            dve.wait_ge(o_mm, 1)
            dve.wait_ge(rows_s, 2)
            nc.vector.tensor_tensor(o[:], ps_o, sq[:], ALU.add).then_inc(o_s, 1)
            dve.wait_ge(o_s, 1)
            layernorm_stats(nc, g, dve, o, stats, mv, 2, stats_s, mom_s, 0)
            dve.wait_ge(rstd_s.sem, rstd_s.at(0, 1))
            for m in range(2):
                nc.vector.tensor_scalar(h0[:, m, :], o[:, m, :], mv[:, m, 0:1], rstd[:, m:m + 1],
                                        ALU.subtract, ALU.mult).then_inc(h0_s, 1)
            dve.wait_ge(hT_mm, 2)
            for ch in range(DC):
                nc.vector.tensor_tensor(hg[:, ch], ps_hT[:, ch].rearrange("p (e b) -> p e b", b=B),
                                        bcast(gT[:, ch, :], 2, B), ALU.mult).then_inc(hg_s, 1)
                nc.vector.tensor_tensor(oT[:, ch], ps_oT[:, ch].rearrange("p (e b) -> p e b", b=B),
                                        bcast(b2T[:, ch, :], 2, B), ALU.add).then_inc(oT_s, 1)
            dve.wait_ge(hg_s, DC)
            dve.wait_ge(padded, 1)
            for ch in range(DC):
                nc.vector.tensor_tensor(hP[:, ch, :, 0:B], hg[:, ch], bcast(bT[:, ch, :], 2, B), ALU.add).then_inc(hb_s, 1)
            dve.wait_ge(hb_s, DC)
            dve.wait_ge(oT_s, DC)

            def hidden(pr, par, first=False):
                if not first:
                    dve.wait_ge(up_mm.sem, up_mm.at(pr, -2))
                nc.vector.tensor_copy(stage[:, par], hP[:, :, bass.ds(2 * pr, 2), :]).then_inc(stage_s.sem, 1)

            def step(pr, par, h, first=False, second=False, last=False):
                if not last:
                    hidden(pr + 1, 1 - par, first)
                for i, (bias, ps, pre) in enumerate(((b1, ps_u, ub), (bg, ps_g, gb))):
                    dve.wait_ge(up_mm.sem, up_mm.at(pr, i + 1))
                    if not first and i == 0:
                        dve.wait_ge(ugT_mm.sem, ugT_mm.at(pr, 0))
                    nc.vector.tensor_tensor(pre[:], ps[0:R, :], bias[:, par, :], ALU.add).then_inc(pre_s.sem, 1)
                dve.wait_ge(silu_s.sem, silu_s.at(pr, 2))
                nc.vector.tensor_tensor(ub[:], ub[:], gb[:], ALU.mult).then_inc(ug_s.sem, 1)
                dve.wait_ge(yT_mm.sem, yT_mm.at(pr, 1))
                nc.vector.tensor_tensor(onT[:, :, bass.ds(2 * pr, 2), :],
                                        ps_yT[:].rearrange("p c (e r) -> p c e r", e=2)[:, :, :, 0:B],
                                        oT[:, :, bass.ds(2 * pr, 2), :], ALU.add).then_inc(on_s.sem, 1)

            hidden(0, 0, True)
            step(0, 0, 0, first=True)
            with dve.Fori(0, NP // 2 - 1) as k:
                step(2 * k + 1, 1, k)
                step(2 * k + 2, 0, k + 1)
            step(NP - 1, 1, NP // 2 - 1, last=True)

        @block.gpsimd
        def _(pool):
            layernorm_rstd(nc, g, pool, mv, veps, rstd, 2, mom_s, veps_s, rstd_s, 0)

        @block.tensor
        def _(pe):
            for t in range(4):
                for ch in range(DC):
                    for q in range(4):
                        h = 4 * t + q
                        last = nc.tensor.matmul(
                            ps_v[q * QUAD:(q + 1) * QUAD, t, :], g.wv_pad[:, ch, h, :],
                            at_all[:, ch, h * NS:(h + 1) * NS, :].rearrange("p s b -> p (s b)"),
                            start=(ch == 0), stop=(ch == DC - 1))
            last.then_inc(v_mm, 1)
            pe.wait_ge(v_s, 4)
            for m in range(2):
                for t in range(4):
                    last = nc.tensor.matmul(ps_o[:, m, :], attnT[:, t, m * P:(m + 1) * P], g.wo_pad[:, t, :],
                                            start=(t == 0), stop=(t == 3))
            last.then_inc(o_mm, 1)
            pe.wait_ge(h0_s, 2)
            for src, dst in ((h0, ps_hT), (o, ps_oT)):
                for ch in range(DC):
                    for m in range(2):
                        last = nc.tensor.transpose(dst[:, ch, m * P:(m + 1) * P], src[:, m, ch * P:(ch + 1) * P], g.ident[:])
                last.then_inc(hT_mm, 1)

            def up(pr, par, h, first=False):
                pe.wait_ge(stage_s.sem, stage_s.at(pr, 1))
                for i, (w, ps) in enumerate(((w1, ps_u), (wg, ps_g))):
                    pe.wait_ge(w_in[i][par], (h + 1) * 48)
                    if not first:
                        pe.wait_ge(pre_s.sem, pre_s.at(pr, i - 1))
                    for half in range(2):
                        for ch in range(DC):
                            for e in range(2):
                                last = nc.tensor.matmul(ps[e * QUAD:(e + 1) * QUAD, half * 512:(half + 1) * 512],
                                                        stage[:, par, ch, e, :], w[:, par, e, ch, half * 512:(half + 1) * 512],
                                                        start=(ch == 0), stop=(ch == DC - 1))
                    last.then_inc(up_mm.sem, 1)

            def down(pr, par, h, first=False):
                pe.wait_ge(ug_s.sem, ug_s.at(pr, 1))
                if not first:
                    hold(g, pe, ugT_s.sem, ugT_s.at(pr, 0))
                for k in range(FK):
                    last = nc.tensor.transpose(ps_ugT[:, k, :], ub[:].rearrange("r (p k) -> r k p", k=FK)[:, k, :],
                                               g.ident[0:R, 0:R])
                last.then_inc(ugT_mm.sem, 1)
                pe.wait_ge(ugT_s.sem, ugT_s.at(pr, 1))
                pe.wait_ge(w_in[2][par], (h + 1) * 32)
                if not first:
                    pe.wait_ge(y_s.sem, y_s.at(pr, 0))
                for k in range(FK):
                    for e in range(2):
                        last = nc.tensor.matmul(ps_y[e * QUAD:(e + 1) * QUAD, 0:D], ugT[:, k, e * QUAD:(e + 1) * QUAD],
                                                w2[:, par, e, k, :], start=(k == 0), stop=(k == FK - 1))
                last.then_inc(y_mm.sem, 1)
                pe.wait_ge(y_s.sem, y_s.at(pr, 1))
                if not first:
                    hold(g, pe, on_s.sem, on_s.at(pr, 0))
                for ch in range(DC):
                    last = nc.tensor.transpose(ps_yT[:, ch, :], y[:, ch * P:(ch + 1) * P], g.ident[0:R, 0:R])
                last.then_inc(yT_mm.sem, 1)

            up(0, 0, 0, True)
            down(0, 0, 0, True)
            with pe.Fori(0, NP // 2 - 1) as k:
                for par in range(2):
                    up(2 * k + 1 + par, 1 - par, k + par)
                    down(2 * k + 1 + par, 1 - par, k + par)
            up(NP - 1, 1, NP // 2 - 1)
            down(NP - 1, 1, NP // 2 - 1)
            pe.wait_ge(on_s.sem, on_s.at(NP - 1, 1))
            for i, (w, ps) in enumerate(((cwk, ps_kv), (cwv, ps_o))):
                for m in range(2):
                    for ch in range(DC):
                        last = nc.tensor.matmul(ps[:, m, :], w[:, ch, m * P:(m + 1) * P],
                                                onT[:, ch].rearrange("p e b -> p (e b)"),
                                                start=(ch == 0), stop=(ch == DC - 1))
                last.then_inc(kv_mm, 1)

        @block.scalar
        def _(act):
            act.wait_ge(v_mm, 1)
            for t in range(4):
                nc.scalar.activation(attnT[:, t, :], ps_v[:, t, :], ACT.Identity, bias=g.bv_pad[:, t:t + 1]).then_inc(v_s, 1)

            def step(pr, first=False):
                for i, pre in enumerate((ub, gb)):
                    act.wait_ge(pre_s.sem, pre_s.at(pr, i + 1))
                    nc.scalar.activation(pre[:], pre[:], ACT.Silu).then_inc(silu_s.sem, 1)
                act.wait_ge(ugT_mm.sem, ugT_mm.at(pr, 1))
                if not first:
                    act.wait_ge(y_mm.sem, y_mm.at(pr, 0))
                nc.scalar.copy(ugT[:], ps_ugT[:]).then_inc(ugT_s.sem, 1)
                act.wait_ge(y_mm.sem, y_mm.at(pr, 1))
                if not first:
                    act.wait_ge(yT_mm.sem, yT_mm.at(pr, 0))
                nc.scalar.copy(y[:], ps_y[0:R, 0:D]).then_inc(y_s.sem, 1)

            step(0, True)
            with act.Fori(1, NP) as pr:
                step(pr)
            act.wait_ge(bk_s, 1)
            act.wait_ge(kv_mm, 1)
            for m in range(DC):
                nc.scalar.activation(kT[:, m].rearrange("p s b -> p (s b)"), ps_kv[:, m, :], ACT.Identity,
                                     bias=bk4[:, m:m + 1], scale=FDH ** -0.5).then_inc(kv_s, 1)
            act.wait_ge(kv_mm, 2)
            for m in range(DC):
                nc.scalar.activation(vT[:, m].rearrange("p s b -> p (s b)"), ps_o[:, m, :], ACT.Identity,
                                     bias=bv[:, m:m + 1]).then_inc(kv_s, 1)


def combine_phase(nc, io, g, sem, f, x_dram, out_dram, kT, vT):
    n = lambda x: f"com_{x}"
    name = lambda x: f"com{f}_{x}"
    c = lambda x, per, credit=0: Count(sem(n(x)), per, credit)
    W, NB = 2, 4
    NK = 2 * B // NB
    tab_in, half_s = sem(n("tab")), sem(n("half"))
    x_in = [sem(n(f"x_in{i}")) for i in range(NB)]
    out_s = [c(f"out{i}", 16, 16) for i in range(2)]
    stats_s, mom_s, veps_s, rstd_s, xn_s = c("stats", W), c("moments", W), c("veps", 1), c("rstd", 1), c("xn", W, W)
    blk_s, gu_mm, g_s, cb_mm, cb_s = c("blk", 4), c("gu_mm", 2, 2), c("gu", 2, 2), c("cb_mm", 1, 1), c("cb", 1, 1)
    xt_mm, xt_s, s_mm, s1_s, o_mm, pt_s = (c(x, 1, 1) for x in ("xt_mm", "xt", "s_mm", "s1", "o_mm", "pt"))
    max_s, sub_s, exp_s, sum_s, rec_s, p_s, xb_s = (c(x, 1) for x in ("max", "sub", "exp", "sum", "rec", "p", "xb"))
    pt_mm, o_s = c("pt_mm", 1, 2), c("o", 1, NB)

    class Unit:

        def __init__(self, k, i):
            k, i = k + i // NB, i % NB
            self.k, self.u, self.j, self.p, self.jp, self.buf = k, k * NB + i, k * 2 + i // 2, i % 2, i // 2, i

    with ExitStack() as s:
        sb = lambda nm, sh: s.enter_context(nc.sbuf_tensor(name(nm), sh, F32))
        pb = lambda nm, sh: s.enter_context(nc.psum_tensor(name(nm), sh, F32))
        bq, bo, boh = sb("t_bq", [P, DC, P]), sb("t_bo", [P, W, D]), sb("t_boh", [P, W, D])
        xin, xb, xo = sb("b_x", [P, NB, W, D]), sb("b_xb", [P, NB, W, D]), sb("b_xo", [P, 2, W, D])
        stats, mv, veps, rstd = sb("b_st", [P, W, 6]), sb("b_mv", [P, W, 2]), sb("b_ve", [P, W]), sb("b_rs", [P, W])
        xn, xnT = sb("b_xn", [P, W, D]), sb("b_xnT", [P, DC, W * P])
        kblk, vblk = sb("b_kblk", [P, DC, HPC, NS]), sb("b_vblk", [P, DC, HPC, NS])
        G, U, cb = sb("b_G", [P, 2, DC, HS]), sb("b_U", [P, 2, DC, D]), sb("b_cb", [P, 2, HS])
        s1, prob = sb("b_s1", [P, W, HS]), sb("b_prob", [P, 2, W, HS])
        mx, sm, rc = (sb(x, [P, W * FH]) for x in ("b_mx", "b_sm", "b_rc"))
        pT = sb("b_pT", [P, DC, W * P])
        ps_xt, ps_g, ps_u, ps_c = pb("ps_xt", [P, DC, W * P]), pb("ps_g", [P, DC, HS]), pb("ps_u", [P, DC, D]), pb("ps_c", [P, 512])
        ps_s, ps_pt, ps_o = pb("ps_s", [P, W, HS]), pb("ps_pt", [P, DC, W * P]), pb("ps_o", [P, 2, W, D])
        heads = lambda ap: ap.rearrange("p w (h s) -> p (w h) s", s=NS)
        block = s.enter_context(nc.Block())

        def bodies(eng, body):
            body(0, first=True)
            with eng.Fori(1, NK - 1) as k:
                body(k)
            body(NK - 1, last=True)

        @block.sync
        def _(sp):
            sp.dma_start(bq[:], io["c_bq"]).then_inc(tab_in, 16)
            sp.dma_start(bo[:], io["c_bo"]).then_inc(tab_in, 16)
            for i in range(2):
                sp.sem_inc(out_s[i].sem, 16)

            def rows(dram, v):
                return dram[v.j].rearrange("(u i p) d -> u p i d", u=2, p=P)[v.p]

            def load(v):
                sp.dma_start(xin[:, v.buf], rows(x_dram, v)).then_inc(x_in[v.buf], 16)

            def store(v):
                hold(g, sp, o_s.sem, o_s.at(v.u, 1))
                sp.dma_start(rows(out_dram, v), xo[:, v.p]).then_inc(out_s[v.p].sem, 16)

            def body(k, first=False, last=False):
                for i in range(NB):
                    v = Unit(k, i)
                    if not last:
                        hold(g, sp, xn_s.sem, xn_s.at(v.u, W))
                        hold(g, sp, xb_s.sem, xb_s.at(v.u, 1))
                        load(Unit(k, i + NB))
                    if not first or i >= 3:
                        store(Unit(k, i - 3))

            for i in range(NB):
                load(Unit(0, i))
            bodies(sp, body)
            for i in range(1, NB):
                store(Unit(NK - 1, i))
            for p in range(2):
                sp.wait_ge(out_s[p].sem, out_s[p].at(B, 0))

        @block.vector
        def _(dve):
            dve.sem_inc(xn_s.sem, W)
            dve.sem_inc(s1_s.sem, 1)
            dve.sem_inc(o_s.sem, NB)
            dve.wait_ge(tab_in, 32)
            nc.vector.tensor_scalar(boh[:], bo[:], 0.5, None, ALU.mult).then_inc(half_s, 1)

            def moments(v):
                dve.wait_ge(x_in[v.buf], (v.k + 1) * 16)
                dve.wait_ge(xn_s.sem, xn_s.at(v.u, 0))
                layernorm_stats(nc, g, dve, xin[:, v.buf], stats, mv, W, stats_s, mom_s, v.u)

            def normalise(v):
                dve.wait_ge(rstd_s.sem, rstd_s.at(v.u, 1))
                dve.wait_ge(xt_mm.sem, xt_mm.at(v.u, 0))
                for i in range(W):
                    nc.vector.tensor_scalar(xn[:, i, :], xin[:, v.buf, i, :], mv[:, i, 0:1], rstd[:, i:i + 1],
                                            ALU.subtract, ALU.mult).then_inc(xn_s.sem, 1)

            def shift(v):
                dve.wait_ge(cb_s.sem, cb_s.at(v.j, 1))
                dve.wait_ge(s_mm.sem, s_mm.at(v.u, 1))
                nc.vector.tensor_tensor(s1[:], ps_s[:], bcast(cb[:, v.jp, :], 1, W), ALU.add).then_inc(s1_s.sem, 1)
                dve.wait_ge(s1_s.sem, s1_s.at(v.u, 1))
                nc.vector.tensor_reduce(mx[:], heads(s1[:]), AX.X, ALU.max).then_inc(max_s.sem, 1)
                dve.wait_ge(max_s.sem, max_s.at(v.u, 1))
                nc.vector.tensor_tensor(heads(s1[:]), heads(s1[:]), bcast(mx[:], 2, NS), ALU.subtract).then_inc(sub_s.sem, 1)

            def scale(v):
                dve.wait_ge(exp_s.sem, exp_s.at(v.u, 1))
                pr = heads(prob[:, v.p])
                nc.vector.tensor_reduce(sm[:], pr, AX.X, ALU.add).then_inc(sum_s.sem, 1)
                dve.wait_ge(sum_s.sem, sum_s.at(v.u, 1))
                nc.vector.reciprocal(rc[:], sm[:]).then_inc(rec_s.sem, 1)
                dve.wait_ge(rec_s.sem, rec_s.at(v.u, 1))
                nc.vector.tensor_tensor(pr, pr, bcast(rc[:], 2, NS), ALU.mult).then_inc(p_s.sem, 1)

            def result(v):
                dve.wait_ge(o_mm.sem, o_mm.at(v.u, 1))
                dve.wait_ge(xb_s.sem, xb_s.at(v.u, 1))
                dve.wait_ge(out_s[v.p].sem, out_s[v.p].at(v.j, 0))
                nc.vector.scalar_tensor_tensor(xo[:, v.p], ps_o[:, v.p], 0.5, xb[:, v.buf], ALU.mult, ALU.add)\
                    .then_inc(o_s.sem, 1)

            def body(k, first=False, last=False):
                for i in range(NB):
                    if not first or i >= 1:
                        scale(Unit(k, i - 1))
                    if not last or i + 1 < NB:
                        normalise(Unit(k, i + 1))
                    shift(Unit(k, i))
                    if not last or i + 2 < NB:
                        moments(Unit(k, i + 2))
                    if not first or i >= 2:
                        result(Unit(k, i - 2))

            moments(Unit(0, 0))
            normalise(Unit(0, 0))
            moments(Unit(0, 1))
            bodies(dve, body)
            scale(Unit(NK - 1, NB - 1))
            for i in (NB - 2, NB - 1):
                result(Unit(NK - 1, i))

        @block.gpsimd
        def _(pool):
            pool.wait_ge(half_s, 1)

            def blocks(v):
                for src, dst, used in ((kT, kblk, cb_mm), (vT, vblk, gu_mm)):
                    pool.wait_ge(used.sem, used.at(v.j, 0))
                    for ch in range(DC):
                        nc.gpsimd.tensor_tensor(dst[:, ch], g.blkmask[:].rearrange("p (h s) -> p h s", s=NS),
                                                bcast(src[:, ch, :, v.j], 1, HPC), ALU.mult).then_inc(blk_s.sem, 1)

            def unit(v):
                layernorm_rstd(nc, g, pool, mv, veps, rstd, W, mom_s, veps_s, rstd_s, v.u)
                pool.wait_ge(o_s.sem, o_s.at(v.u, 1 - NB))
                nc.gpsimd.tensor_tensor(xb[:, v.buf], xin[:, v.buf], boh[:], ALU.add).then_inc(xb_s.sem, 1)

            def body(k, first=False, last=False):
                for i in range(NB):
                    if i % 2 == 0 and (not last or i + 2 < NB):
                        blocks(Unit(k, i + 2))
                    if not last or i + 2 < NB:
                        unit(Unit(k, i + 2))

            blocks(Unit(0, 0))
            for i in range(2):
                unit(Unit(0, i))
            bodies(pool, body)

        @block.tensor
        def _(pe):
            for at, credit in ((gu_mm, 2), (cb_mm, 1), (xt_mm, 1), (s_mm, 1), (o_mm, 1), (pt_mm, 2)):
                pe.sem_inc(at.sem, credit)

            def fold_keys(v):
                pe.wait_ge(blk_s.sem, blk_s.at(v.j, 2))
                pe.wait_ge(g_s.sem, g_s.at(v.j, -1))
                pe.wait_ge(cb_s.sem, cb_s.at(v.j, 0))
                for m in range(DC):
                    for ch in range(DC):
                        last = nc.tensor.matmul(ps_g[:, m, ch * P:(ch + 1) * P], g.cwqT[:, ch, m * P:(m + 1) * P],
                                                kblk[:, ch].rearrange("p h s -> p (h s)"), start=True, stop=True)
                last.then_inc(gu_mm.sem, 1)
                for ch in range(DC):
                    last = nc.tensor.matmul(ps_c[:, ch * P:(ch + 1) * P], bq[:, ch, :],
                                            kblk[:, ch].rearrange("p h s -> p (h s)"), start=True, stop=True)
                last.then_inc(cb_mm.sem, 1)

            def fold_values(v):
                pe.wait_ge(blk_s.sem, blk_s.at(v.j, 4))
                pe.wait_ge(g_s.sem, g_s.at(v.j, 0))
                for ch in range(DC):
                    last = nc.tensor.matmul(ps_u[:, ch, :], vblk[:, ch].rearrange("p h s -> p (h s)"), g.cwo[:, ch, :],
                                            start=True, stop=True)
                last.then_inc(gu_mm.sem, 1)

            def transpose_x(v):
                pe.wait_ge(xn_s.sem, xn_s.at(v.u, W))
                pe.wait_ge(xt_s.sem, xt_s.at(v.u, 0))
                for ch in range(DC):
                    for i in range(W):
                        last = nc.tensor.transpose(ps_xt[:, ch, i * P:(i + 1) * P], xn[:, i, ch * P:(ch + 1) * P], g.ident[:])
                last.then_inc(xt_mm.sem, 1)

            def scores(v):
                pe.wait_ge(xt_s.sem, xt_s.at(v.u, 1))
                pe.wait_ge(g_s.sem, g_s.at(v.j, 1))
                pe.wait_ge(s1_s.sem, s1_s.at(v.u, 0))
                for i in range(W):
                    for ch in range(DC):
                        last = nc.tensor.matmul(ps_s[:, i, :], xnT[:, ch, i * P:(i + 1) * P], G[:, v.jp, ch, :],
                                                start=(ch == 0), stop=(ch == DC - 1))
                last.then_inc(s_mm.sem, 1)

            def transpose_p(v):
                pe.wait_ge(p_s.sem, p_s.at(v.u, 1))
                pe.wait_ge(pt_s.sem, pt_s.at(v.u, 0))
                for ch in range(DC):
                    for i in range(W):
                        last = nc.tensor.transpose(ps_pt[:, ch, i * P:(i + 1) * P], prob[:, v.p, i, ch * P:(ch + 1) * P], g.ident[:])
                last.then_inc(pt_mm.sem, 1)

            def mix(v):
                pe.wait_ge(pt_s.sem, pt_s.at(v.u, 1))
                pe.wait_ge(g_s.sem, g_s.at(v.j, 2))
                pe.wait_ge(o_s.sem, o_s.at(v.u, -1))
                for i in range(W):
                    for ch in range(DC):
                        last = nc.tensor.matmul(ps_o[:, v.p, i, :], pT[:, ch, i * P:(i + 1) * P], U[:, v.jp, ch, :],
                                                start=(ch == 0), stop=(ch == DC - 1))
                last.then_inc(o_mm.sem, 1)

            def body(k, first=False, last=False):
                for i in range(NB):
                    before, following = not first or i >= 1, not last or i + 1 < NB
                    scores(Unit(k, i))
                    if before:
                        transpose_p(Unit(k, i - 1))
                    if following:
                        transpose_x(Unit(k, i + 1))
                    if i % 2 == 0:
                        fold_values(Unit(k, i))
                    elif following:
                        fold_keys(Unit(k, i + 1))
                    if before:
                        mix(Unit(k, i - 1))

            fold_keys(Unit(0, 0))
            transpose_x(Unit(0, 0))
            bodies(pe, body)
            transpose_p(Unit(NK - 1, NB - 1))
            mix(Unit(NK - 1, NB - 1))

        @block.scalar
        def _(act):
            for at, credit in ((g_s, 2), (cb_s, 1), (xt_s, 1), (pt_s, 1)):
                act.sem_inc(at.sem, credit)

            def keys(v):
                act.wait_ge(gu_mm.sem, gu_mm.at(v.j, 1))
                nc.scalar.copy(G[:, v.jp], ps_g[:]).then_inc(g_s.sem, 1)

            def values(v):
                act.wait_ge(gu_mm.sem, gu_mm.at(v.j, 2))
                nc.scalar.copy(U[:, v.jp], ps_u[:]).then_inc(g_s.sem, 1)

            def biases(v):
                act.wait_ge(cb_mm.sem, cb_mm.at(v.j, 1))
                nc.scalar.copy(cb[:, v.jp, :], ps_c[:, 0:HS]).then_inc(cb_s.sem, 1)

            def copy_x(v):
                act.wait_ge(xt_mm.sem, xt_mm.at(v.u, 1))
                act.wait_ge(s_mm.sem, s_mm.at(v.u, 0))
                nc.scalar.copy(xnT[:], ps_xt[:]).then_inc(xt_s.sem, 1)

            def exps(v):
                act.wait_ge(sub_s.sem, sub_s.at(v.u, 1))
                act.wait_ge(pt_mm.sem, pt_mm.at(v.u, -1))
                nc.scalar.activation(prob[:, v.p], s1[:], ACT.Exp).then_inc(exp_s.sem, 1)

            def copy_p(v):
                act.wait_ge(pt_mm.sem, pt_mm.at(v.u, 1))
                act.wait_ge(o_mm.sem, o_mm.at(v.u, 0))
                nc.scalar.copy(pT[:], ps_pt[:]).then_inc(pt_s.sem, 1)

            def body(k, first=False, last=False):
                for i in range(NB):
                    following = not last or i + 1 < NB
                    if not first or i >= 1:
                        copy_p(Unit(k, i - 1))
                    if following:
                        copy_x(Unit(k, i + 1))
                    if i % 2 == 1 and following:
                        keys(Unit(k, i + 1))
                    exps(Unit(k, i))
                    if i % 2 == 0:
                        values(Unit(k, i))
                    elif following:
                        biases(Unit(k, i + 1))

            keys(Unit(0, 0))
            biases(Unit(0, 0))
            copy_x(Unit(0, 0))
            bodies(act, body)
            copy_p(Unit(NK - 1, NB - 1))


def attention_phase(nc, io, g, sem, x_dram, out_dram):
    n = lambda x: f"att_{x}"
    c = lambda x, per, credit=0: Count(sem(n(x)), per, credit)
    one = lambda x: sem(n(x))
    tab_in, w_in, w_hi, w_lo, zero_s, bqs_s = (one(x) for x in ("tab", "w_in", "w_hi", "w_lo", "zero", "bqs"))
    x_in, xres_in, out_s = c("x_in", 16), c("xres_in", 16), c("out", 16, 16)
    stats_s, mom_s, veps_s, rstd_s, xn_s = c("stats", TT), c("moments", TT), c("veps", 1), c("rstd", 1), c("xn", TT, TT)
    xt_mm, xhi_s, xlo_s = c("xt_mm", DC, DC), c("xhi", DC), c("xlo", DC)
    v_mm, v_s = c("v_mm", 2 * TT), c("v", 2 * TT)
    z_mm, z_s, shuf_s, cos_s, sin_s = (c(x, 2 * PAIRS, 2 * PAIRS) for x in ("z_mm", "z", "shuf", "cos", "sin"))
    rq_s, rk_s = c("rq", 2 * PAIRS, 2), c("rk", PAIRS, 1)
    s_mm, max_s, exp_s, rec_s, p_s = (
        c("s_mm", 4 * AH, 9), c("max", 4 * AH), c("exp", 4 * AH, 4), c("rec", AH), c("p", 4 * AH))
    pt_mm, pt_s, pv_mm, ohi_s, olo_s = (
        c("pt_mm", 4 * AH, 4 * AH), c("pt", 4 * AH, 4), c("pv_mm", PAIRS, 1), c("ohi", PAIRS), c("olo", PAIRS, 1))
    wo_mm, xb_s, xo_s = c("wo_mm", 2, 2), c("xb", 1), c("xo", 2, 2)
    V_SLOT, X_SLOT = 3, AH - 3
    OFF = [0, 512, 896, 1152]
    WIDTH = [S - kb * P for kb in range(TT)]
    PLACE = [slice(o, o + (qt + 1) * P) for qt, o in enumerate((0, 128, 384, 768))]
    with ExitStack() as s:
        sb = lambda nm, sh, dt=F32: s.enter_context(nc.sbuf_tensor(n(nm), sh, dt))
        pb = lambda nm, sh: s.enter_context(nc.psum_tensor(n(nm), sh, F32))
        w_parts = {w: [sb(f"w{w}_{x}", [P, 2048], F32R) for x in ("hi", "lo")] for w in ("q", "k", "v", "o")}
        split = lambda w: [t[:].rearrange("p (c n) -> p c n", c=(PAIRS if w == "o" else DC)) for t in w_parts[w]]
        wq, wk, wv, wo = (split(w) for w in ("q", "k", "v", "o"))
        cos, sin = sb("cos", [P, S]), sb("sin", [P, S])
        bq, bqs, bk = sb("bq", [P, PAIRS]), sb("bqs", [P, PAIRS]), sb("bk", [P, PAIRS])
        bv, bo = sb("bv", [P, AW]), sb("bo", [P, D])
        identb, masked = sb("identb", [P, P], BF16), sb("masked", [P, P], BF16)
        xin, xn, xres = (sb(x, [P, TT, D]) for x in ("x", "xn", "xres"))
        stats, mv, veps, rstd = sb("st", [P, TT, 6]), sb("mv", [P, TT, 2]), sb("ve", [P, TT]), sb("rs", [P, TT])
        xT = [sb(f"xT_{x}", [P, DC, S], F32R) for x in ("hi", "lo")]
        v = sb("v_sb", [P, TT, AW])
        z, zs = sb("z_sb", [P, 2, S]), sb("zs", [P, 2, S])
        qz = sb("qz", [P, 2, 2, S])
        kT = sb("kT", [P, 2, S])
        prob = sb("prob", [P, 4, OFF[3] + WIDTH[3]])
        nmax, sums, rinv = (sb(x, [P, 2, TT]) for x in ("nmax", "sums", "rinv"))
        probT = sb("probT", [P, 2, OFF[3] + WIDTH[3]])
        oT = [sb(f"oT_{x}", [P, PAIRS, S], F32R) for x in ("hi", "lo")]
        ps_s = [pb(f"ps_s{i}", [P, S]) for i in range(TT)]
        ps_z = [pb(f"ps_z{i}", [P, S]) for i in range(2)]
        ps_pt, ps_pv = pb("ps_pt", [P, S]), pb("ps_pv", [P, S])
        w_stage = [t[:].rearrange("p h n -> p (h n)")[:, 0:2048] for t in (prob, probT)]
        block = s.enter_context(nc.Block())

        def products(ps, lhs, rhs):
            terms = [(a, b, ch) for a, b in ((0, 0), (0, 1), (1, 0)) for ch in range(len(lhs[0]))]
            for i, (a, b, ch) in enumerate(terms):
                last = nc.tensor.matmul(ps, lhs[a][ch], rhs[b][ch], start=(i == 0), stop=(i == len(terms) - 1))
            return last

        @block.sync
        def _(sp):
            tiles = lambda dram, j: dram[j].rearrange("(i p) d -> p i d", p=P)
            for dst, src in ((cos[:], io["cos"]), (sin[:], io["sin"]), (bq[:], io["a_bq"]), (bk[:], io["a_bk"]),
                             (bv[:], io["a_bv"]), (bo[:], io["a_bo"]), (identb[:], io["identb"]), (masked[:], io["masked"])):
                sp.dma_start(dst, src).then_inc(tab_in, 16)
            sp.dma_start(xin[:], tiles(x_dram, 0)).then_inc(x_in.sem, 16)
            for i, (w, pitch) in enumerate((("q", 2), ("k", 2), ("v", 2), ("o", 8))):
                if i >= 2:
                    sp.wait_ge(w_lo, i - 1)
                sp.dma_start(w_stage[i % 2].rearrange("p (c n) -> p c n", c=pitch),
                             io["a_W" + w].rearrange("(c p) n -> p c n", p=P)).then_inc(w_in, 16)
                sp.wait_ge(w_in, 16 * (i + 1))

            def body(j, last=False):
                if not last:
                    hold(g, sp, xn_s.sem, xn_s.at(j, TT))
                    sp.dma_start(xin[:], tiles(x_dram, j + 1)).then_inc(x_in.sem, 16)
                hold(g, sp, out_s.sem, out_s.at(j, 0))
                sp.dma_start(xres[:], tiles(x_dram, j)).then_inc(xres_in.sem, 16)
                hold(g, sp, xo_s.sem, xo_s.at(j, 2))
                sp.dma_start(tiles(out_dram, j), xres[:]).then_inc(out_s.sem, 16)

            with sp.Fori(0, B - 1) as j:
                body(j)
            body(B - 1, last=True)
            sp.wait_ge(out_s.sem, out_s.at(B - 1, 16))

        @block.gpsimd
        def _(pool):
            nc.gpsimd.memset(qz[:], 0.0).then_inc(zero_s, 1)
            pool.sem_inc(cos_s.sem, 2 * PAIRS)
            pool.sem_inc(sin_s.sem, 2 * PAIRS)
            pool.sem_inc(rk_s.sem, 1)
            pool.wait_ge(tab_in, 16 * 8)

            def rotate(j, p):
                for i in range(2):
                    m = 2 * p + i + 1
                    pool.wait_ge(shuf_s.sem, shuf_s.at(j, m))
                    nc.gpsimd.tensor_tensor(z[:, i, :], z[:, i, :], cos[:], ALU.mult).then_inc(cos_s.sem, 1)
                    nc.gpsimd.tensor_tensor(zs[:, i, :], zs[:, i, :], sin[:], ALU.mult).then_inc(sin_s.sem, 1)
                pool.wait_ge(sin_s.sem, sin_s.at(j, 2 * p + 2))
                pool.wait_ge(s_mm.sem, s_mm.at(j, 8 * (p - 1)))
                nc.gpsimd.tensor_tensor(kT[:, p % 2, :], z[:, 1, :], zs[:, 1, :], ALU.add).then_inc(rk_s.sem, 1)

            def residual(j):
                pool.wait_ge(xres_in.sem, xres_in.at(j, 16))
                for i in range(TT):
                    last = nc.gpsimd.tensor_tensor(xres[:, i, :], xres[:, i, :], bo[:], ALU.add)
                last.then_inc(xb_s.sem, 1)

            def slots(j, heads, last=False):
                for h in heads:
                    if h % 2 == 0 and h // 2 + 1 < PAIRS:
                        rotate(j, h // 2 + 1)
                    if h == 6:
                        residual(j)
                    if not last and h == 8:
                        layernorm_rstd(nc, g, pool, mv, veps, rstd, TT, mom_s, veps_s, rstd_s, j + 1)
                    if not last and h == AH - 2:
                        rotate(j + 1, 0)

            layernorm_rstd(nc, g, pool, mv, veps, rstd, TT, mom_s, veps_s, rstd_s, 0)
            rotate(0, 0)
            slots(0, range(4))
            with pool.Fori(0, B - 1) as j:
                slots(j, range(4, AH))
                slots(j + 1, range(4))
            slots(B - 1, range(4, AH), last=True)

        @block.vector
        def _(dve):
            dve.sem_inc(xn_s.sem, TT)
            dve.sem_inc(shuf_s.sem, 2 * PAIRS)
            dve.sem_inc(rq_s.sem, 2)
            dve.sem_inc(olo_s.sem, 1)
            dve.sem_inc(xo_s.sem, 2)
            dve.wait_ge(tab_in, 16 * 8)
            nc.vector.tensor_scalar(bqs[:], bq[:], ADH ** -0.5, None, ALU.mult).then_inc(bqs_s, 1)
            for i, w in enumerate("qkvo"):
                dve.wait_ge(w_hi, i + 1)
                hi, lo = w_parts[w]
                nc.vector.tensor_tensor(lo[:], w_stage[i % 2], hi[:].bitcast(F32), ALU.subtract).then_inc(w_lo, 1)
            dve.wait_ge(zero_s, 1)

            def moments(j):
                dve.wait_ge(x_in.sem, x_in.at(j, 16))
                dve.wait_ge(xn_s.sem, xn_s.at(j, 0))
                layernorm_stats(nc, g, dve, xin, stats, mv, TT, stats_s, mom_s, j)

            def normalise(j):
                dve.wait_ge(rstd_s.sem, rstd_s.at(j, 1))
                dve.wait_ge(xt_mm.sem, xt_mm.at(j, 0))
                for i in range(TT):
                    nc.vector.tensor_scalar(xn[:, i, :], xin[:, i, :], mv[:, i, 0:1], rstd[:, i:i + 1],
                                            ALU.subtract, ALU.mult).then_inc(xn_s.sem, 1)

            def x_low(j):
                for ch in range(DC):
                    dve.wait_ge(xhi_s.sem, xhi_s.at(j, ch + 1))
                    nc.vector.tensor_tensor(xT[1][:, ch, :], ps_z[ch][:], xT[0][:, ch, :].bitcast(F32), ALU.subtract)\
                        .then_inc(xlo_s.sem, 1)

            def values(j, ms):
                for m in ms:
                    if m == 0:
                        dve.wait_ge(pv_mm.sem, pv_mm.at(j, 0))
                    dve.wait_ge(v_mm.sem, v_mm.at(j, m + 1))
                    i, half = m // 2, m % 2
                    nc.vector.tensor_tensor(v[:, i, half * 512:(half + 1) * 512], ps_z[m % 2][:],
                                            bv[:, half * 512:(half + 1) * 512], ALU.add).then_inc(v_s.sem, 1)

            def result(j, i):
                dve.wait_ge(xb_s.sem, xb_s.at(j, 1))
                dve.wait_ge(wo_mm.sem, wo_mm.at(j, i + 1))
                t = xres[:, 2 * i:2 * i + 2, :]
                nc.vector.tensor_tensor(t, ps_z[i][:].rearrange("p (i d) -> p i d", i=2), t, ALU.add).then_inc(xo_s.sem, 1)

            def swap(j, p, i):
                hold(g, dve, z_s.sem, z_s.at(j, 2 * p + i + 1))
                nc.vector.stream_shuffle(zs[:, i, :], z[:, i, :], mask=[k ^ 16 for k in range(32)]).then_inc(shuf_s.sem, 1)

            def rotate(j, p):
                dve.wait_ge(s_mm.sem, s_mm.at(j, 8 * (p - 1)))
                dve.wait_ge(sin_s.sem, sin_s.at(j, 2 * p + 1))
                for hh in range(2):
                    at = slice(hh * ADH, (hh + 1) * ADH)
                    nc.vector.tensor_tensor(qz[at, p % 2, hh, :], z[at, 0, :], zs[at, 0, :], ALU.add).then_inc(rq_s.sem, 1)

            def largest(j, h, i):
                qt = TT - 1 - i
                dve.wait_ge(s_mm.sem, s_mm.at(j, 4 * h + i + 1))
                nc.vector.tensor_reduce(nmax[:, h % 2, qt:qt + 1], ps_s[qt][:, 0:(qt + 1) * P], AX.X, ALU.max, negate=True)\
                    .then_inc(max_s.sem, 1)

            def scale(j, h):
                dve.wait_ge(exp_s.sem, exp_s.at(j, 4 * h + 4))
                nc.vector.reciprocal(rinv[:, h % 2, :], sums[:, h % 2, :]).then_inc(rec_s.sem, 1)
                dve.wait_ge(rec_s.sem, rec_s.at(j, h + 1))
                for qt in range(TT):
                    t = prob[:, h % 4, PLACE[qt]]
                    nc.vector.tensor_scalar(t, t, rinv[:, h % 2, qt:qt + 1], None, ALU.mult).then_inc(p_s.sem, 1)

            def low_part(j, p):
                dve.wait_ge(ohi_s.sem, ohi_s.at(j, p + 1))
                nc.vector.tensor_tensor(oT[1][:, p, :], ps_pv[:], oT[0][:, p, :].bitcast(F32), ALU.subtract).then_inc(olo_s.sem, 1)

            def slots(j, heads, first=False, last=False):
                for h in heads:
                    p = h // 2
                    more = p + 1 < PAIRS or not last
                    nxt = (j, p + 1) if p + 1 < PAIRS else (j + 1, 0)
                    if h % 2 == 0:
                        if h > 0:
                            scale(j, h - 1)
                        elif not first:
                            scale(j - 1, AH - 1)
                        if h >= 4:
                            low_part(j, p - 2)
                        elif not first:
                            low_part(j - 1, PAIRS - 2 + p)
                        if more:
                            swap(*nxt, 0)
                        largest(j, h, 0)
                        if more:
                            swap(*nxt, 1)
                        for i in range(1, TT):
                            largest(j, h, i)
                    else:
                        if h == X_SLOT and not last:
                            x_low(j + 1)
                        if more:
                            rotate(*nxt)
                        for i in range(TT):
                            if h == V_SLOT and i < 2:
                                values(j, range(4 * i, 4 * i + 4))
                            if h == V_SLOT and i >= 2 and not first:
                                result(j - 1, i - 2)
                            largest(j, h, i)
                        scale(j, h - 1)
                        if h == 9 and not last:
                            moments(j + 1)
                        if h == 11 and not last:
                            normalise(j + 1)

            moments(0)
            normalise(0)
            x_low(0)
            for i in range(2):
                swap(0, 0, i)
            rotate(0, 0)
            slots(0, range(4), first=True)
            with dve.Fori(0, B - 1) as j:
                slots(j, range(4, AH))
                slots(j + 1, range(4))
            slots(B - 1, range(4, AH), last=True)
            scale(B - 1, AH - 1)
            for p in (PAIRS - 2, PAIRS - 1):
                low_part(B - 1, p)
            for i in range(2):
                result(B - 1, i)

        @block.scalar
        def _(act):
            act.sem_inc(exp_s.sem, 4)
            act.sem_inc(out_s.sem, 16)
            act.sem_inc(pt_s.sem, 4)
            act.sem_inc(z_s.sem, 2 * PAIRS)
            for i, w in enumerate("qkvo"):
                act.wait_ge(w_in, 16 * (i + 1))
                nc.scalar.copy(w_parts[w][0][:], w_stage[i % 2]).then_inc(w_hi, 1)
            act.wait_ge(bqs_s, 1)

            def x_high(j):
                for ch in range(DC):
                    act.wait_ge(xt_mm.sem, xt_mm.at(j, ch + 1))
                    nc.scalar.copy(xT[0][:, ch, :], ps_z[ch][:]).then_inc(xhi_s.sem, 1)

            def project(j, p, i):
                act.wait_ge(z_mm.sem, z_mm.at(j, 2 * p + i + 1))
                act.wait_ge((rq_s, rk_s)[i].sem, (rq_s.at(j, 2 * p), rk_s.at(j, p))[i])
                nc.scalar.activation(z[:, i, :], ps_z[i][:], ACT.Identity, bias=(bqs, bk)[i][:, p:p + 1],
                                     scale=(ADH ** -0.5, 1.0)[i]).then_inc(z_s.sem, 1)

            def exps(j, h, i):
                qt = TT - 1 - i
                act.wait_ge(max_s.sem, max_s.at(j, 4 * h + i + 1))
                act.wait_ge(pt_mm.sem, pt_mm.at(j, 4 * (h - 3)))
                nc.scalar.activation(prob[:, h % 4, PLACE[qt]], ps_s[qt][:, 0:(qt + 1) * P], ACT.Exp,
                                     bias=nmax[:, h % 2, qt:qt + 1], accum_out=sums[:, h % 2, qt:qt + 1]).then_inc(exp_s.sem, 1)

            def copy_pt(j, h, kb):
                act.wait_ge(pv_mm.sem, pv_mm.at(j, h // 2))
                act.wait_ge(pt_mm.sem, pt_mm.at(j, 4 * h + kb + 1))
                nc.scalar.copy(probT[:, h % 2, OFF[kb]:OFF[kb] + WIDTH[kb]], ps_pt[:, 0:WIDTH[kb]]).then_inc(pt_s.sem, 1)

            def high_part(j, p):
                act.wait_ge(pv_mm.sem, pv_mm.at(j, p + 1))
                act.wait_ge(wo_mm.sem, wo_mm.at(j, 0))
                nc.scalar.copy(oT[0][:, p, :], ps_pv[:]).then_inc(ohi_s.sem, 1)

            def slots(j, heads, first=False, last=False):
                for h in heads:
                    p = h // 2
                    more = p + 1 < PAIRS or not last
                    nxt = (j, p + 1) if p + 1 < PAIRS else (j + 1, 0)
                    before = (j, h - 1) if h else (j - 1, AH - 1)
                    turned = (j, h - 2) if h >= 2 else (j - 1, AH + h - 2)
                    exps_before, turns = h > 0 or not first, h >= 2 or not first
                    if h % 2 == 0:
                        if exps_before:
                            for i in (2, 3):
                                exps(*before, i)
                        if h >= 4:
                            high_part(j, p - 2)
                        elif not first:
                            high_part(j - 1, PAIRS - 2 + p)
                        if more:
                            project(*nxt, 0)
                        if turns:
                            copy_pt(*turned, 0)
                        exps(j, h, 0)
                        if turns:
                            copy_pt(*turned, 1)
                        if more:
                            project(*nxt, 1)
                    else:
                        if h == X_SLOT and not last:
                            x_high(j + 1)
                        if turns:
                            copy_pt(*turned, 0)
                        for i in (2, 3):
                            exps(*before, i)
                        if turns:
                            copy_pt(*turned, 1)
                        exps(j, h, 0)
                    if turns:
                        copy_pt(*turned, 2)
                        copy_pt(*turned, 3)
                    exps(j, h, 1)

            x_high(0)
            for i in range(2):
                project(0, 0, i)
            slots(0, range(4), first=True)
            with act.Fori(0, B - 1) as j:
                slots(j, range(4, AH))
                slots(j + 1, range(4))
            slots(B - 1, range(4, AH), last=True)
            for i in (2, 3):
                exps(B - 1, AH - 1, i)
            high_part(B - 1, PAIRS - 2)
            for h in (AH - 2, AH - 1):
                for kb in range(TT):
                    copy_pt(B - 1, h, kb)
            high_part(B - 1, PAIRS - 1)

        @block.tensor
        def _(pe):
            pe.sem_inc(xt_mm.sem, DC)
            pe.sem_inc(z_mm.sem, 2 * PAIRS)
            pe.sem_inc(s_mm.sem, 9)
            pe.sem_inc(pt_mm.sem, 4 * AH)
            pe.sem_inc(pv_mm.sem, 1)
            pe.sem_inc(wo_mm.sem, 2)
            pe.wait_ge(w_lo, 4)
            pe.wait_ge(tab_in, 16 * 8)

            def transpose_x(j, ch):
                pe.wait_ge(xn_s.sem, xn_s.at(j, TT))
                pe.wait_ge(z_s.sem, z_s.at(j, ch - 1))
                for i in range(TT):
                    last = nc.tensor.transpose(ps_z[ch][:, i * P:(i + 1) * P], xn[:, i, ch * P:(ch + 1) * P], g.ident[:])
                last.then_inc(xt_mm.sem, 1)

            def project(j, p, i):
                if p == 0:
                    pe.wait_ge(xlo_s.sem, xlo_s.at(j, DC))
                elif p == 3:
                    pe.wait_ge(v_s.sem, v_s.at(j, 2 * TT - 1 + i))
                    pe.wait_ge(xo_s.sem, xo_s.at(j, i - 1))
                else:
                    pe.wait_ge(z_s.sem, z_s.at(j, 2 * p - 1 + i))
                w = (wq, wk)[i]
                products(ps_z[i][:], [[part[:, ch, p * P:(p + 1) * P] for ch in range(DC)] for part in w],
                         [[part[:, ch, :] for ch in range(DC)] for part in xT]).then_inc(z_mm.sem, 1)

            def values(j, ms):
                for m in ms:
                    i, half = m // 2, m % 2
                    if m < 2:
                        pe.wait_ge(z_s.sem, z_s.at(j, 5 + m))
                    else:
                        pe.wait_ge(v_s.sem, v_s.at(j, m - 1))
                    products(ps_z[m % 2][:], [[part[:, ch, i * P:(i + 1) * P] for ch in range(DC)] for part in xT],
                             [[part[:, ch, half * 512:(half + 1) * 512] for ch in range(DC)] for part in wv]).then_inc(v_mm.sem, 1)

            def scores(j, h, i):
                qt, par, width = TT - 1 - i, (h // 2) % 2, (TT - i) * P
                if i == 0 and h % 2 == 0:
                    pe.wait_ge(rq_s.sem, rq_s.at(j, 2 * (h // 2) + 2))
                    pe.wait_ge(rk_s.sem, rk_s.at(j, h // 2 + 1))
                pe.wait_ge(exp_s.sem, exp_s.at(j, 4 * (h - 1) + i + 1))
                nc.tensor.matmul(ps_s[qt][:, 0:width], qz[:, par, h % 2, qt * P:(qt + 1) * P], kT[:, par, 0:width],
                                 start=True, stop=False)
                nc.tensor.matmul(ps_s[qt][:, qt * P:width], identb[:], masked[:], start=False, stop=True).then_inc(s_mm.sem, 1)

            def transposes(j, h, kb):
                if kb == 0:
                    pe.wait_ge(p_s.sem, p_s.at(j, 4 * h + 4))
                pe.wait_ge(pt_s.sem, pt_s.at(j, 4 * h + kb))
                for qt in range(kb, TT):
                    last = nc.tensor.transpose(ps_pt[:, (qt - kb) * P:(qt - kb + 1) * P],
                                               prob[:, h % 4, PLACE[qt]][:, kb * P:(kb + 1) * P], g.ident[:])
                last.then_inc(pt_mm.sem, 1)

            def mix(j, p):
                pe.wait_ge(pt_s.sem, pt_s.at(j, 8 * p + 8))
                pe.wait_ge(olo_s.sem, olo_s.at(j, p))
                if p == 0:
                    pe.wait_ge(v_s.sem, v_s.at(j, 2 * TT))
                for kb in range(TT):
                    for hh in range(2):
                        h = 2 * p + hh
                        last = nc.tensor.matmul(ps_pv[hh * ADH:(hh + 1) * ADH, kb * P:S], v[:, kb, h * ADH:(h + 1) * ADH],
                                                probT[:, hh, OFF[kb]:OFF[kb] + WIDTH[kb]], start=(kb == 0), stop=(kb == TT - 1))
                last.then_inc(pv_mm.sem, 1)

            def output(j, i, last=False):
                pe.wait_ge(olo_s.sem, olo_s.at(j, PAIRS))
                if last:
                    pe.wait_ge(z_s.sem, z_s.at(j, 2 * PAIRS - 1 + i))
                else:
                    pe.wait_ge(v_s.sem, v_s.at(j + 1, 2 * TT - 1 + i))
                for t in range(2):
                    at = slice((2 * i + t) * P, (2 * i + t + 1) * P)
                    out = products(ps_z[i][:, t * D:(t + 1) * D], [[part[:, p, at] for p in range(PAIRS)] for part in oT],
                                   [[part[:, p, :] for p in range(PAIRS)] for part in wo])
                out.then_inc(wo_mm.sem, 1)

            def slots(j, heads, first=False, last=False):
                for h in heads:
                    p = h // 2
                    more = h % 2 == 0 and (p + 1 < PAIRS or not last)
                    nxt = (j, p + 1) if p + 1 < PAIRS else (j + 1, 0)
                    turned = (j, h - 2) if h >= 2 else (j - 1, AH + h - 2)
                    if h % 2 == 0:
                        if h >= 4:
                            mix(j, p - 2)
                        elif not first:
                            mix(j - 1, PAIRS - 2 + p)
                    if h == X_SLOT and not last:
                        for ch in range(DC):
                            transpose_x(j + 1, ch)
                    for i in range(TT):
                        if more and i < 2:
                            project(*nxt, i)
                        if h == V_SLOT and i < 2:
                            values(j, range(4 * i, 4 * i + 4))
                        if h == V_SLOT and i >= 2 and not first:
                            output(j - 1, i - 2)
                        if h >= 2 or not first:
                            transposes(*turned, i)
                        scores(j, h, i)

            for ch in range(DC):
                transpose_x(0, ch)
            for i in range(2):
                project(0, 0, i)
            slots(0, range(4), first=True)
            with pe.Fori(0, B - 1) as j:
                slots(j, range(4, AH))
                slots(j + 1, range(4))
            slots(B - 1, range(4, AH), last=True)
            mix(B - 1, PAIRS - 2)
            for h in (AH - 2, AH - 1):
                for kb in range(TT):
                    transposes(B - 1, h, kb)
            mix(B - 1, PAIRS - 1)
            for i in range(2):
                output(B - 1, i, last=True)


class Shared:
    pass


def macaron_block(nc, io):
    sems = ExitStack()
    with sems, ExitStack() as s:
        made = {}

        def sem(name):
            if name not in made:
                made[name] = sems.enter_context(nc.semaphore(name))
            return made[name]

        sb = lambda nm, sh: s.enter_context(nc.sbuf_tensor("sh_" + nm, sh, F32))
        g = Shared()
        g.ident, g.blkmask = sb("ident", [P, P]), sb("blkmask", [P, P])
        g.mhalf = sb("mhalf", [P, TT])
        g.G, g.cb = sb("G", [P, DC, HS]), sb("cb", [P, DC])
        g.wv_pad, g.bv_pad = sb("wv_pad", [P, DC, FH, QUAD]), sb("bv_pad", [P, 4])
        g.wo_pad = sb("wo_pad", [P, 4, D])
        g.cwqT, g.cwo = sb("cwqT", [P, DC, D]), sb("cwo", [P, DC, D])
        x1 = nc.dram_tensor("x_after_ffn", (B, S, D), F32, kind="Internal").ap()
        x2 = nc.dram_tensor("x_after_attention", (B, S, D), F32, kind="Internal").ap()
        mhalf_s = sem("mhalf")
        g.held = sem("held")
        with nc.Block() as block:
            @block.gpsimd
            def _(pool):
                nc.gpsimd.memset(g.mhalf[:], -0.5).then_inc(mhalf_s, 1)
                pool.wait_ge(mhalf_s, 1)
        setup_phase(nc, io, g, sem)

        def ffn(f, src, dst):
            with ExitStack() as t:
                kT = t.enter_context(nc.sbuf_tensor(f"ffn{f}_kT", [P, DC, NS, B], F32))
                vT = t.enter_context(nc.sbuf_tensor(f"ffn{f}_vT", [P, DC, NS, B], F32))
                with ExitStack() as u:
                    at_all = u.enter_context(nc.sbuf_tensor(f"ffn{f}_at", [P, DC, HS, B], F32))
                    dispatch_phase(nc, g, sem, f, src, at_all)
                    expert_phase(nc, io, g, sem, f, at_all, kT, vT)
                combine_phase(nc, io, g, sem, f, src, dst, kT, vT)

        ffn(0, io["x"], x1)
        ffn_sems = [h for k, h in made.items() if k.startswith(("dis_", "ex_", "com_"))]
        attention_phase(nc, io, g, sem, x1, x2)
        with nc.Block() as block:
            @block.sync
            def _(sp):
                for h in ffn_sems:
                    sp.sem_clear(h)
        ffn(1, x2, io["out"])



def _rotary_order():
    half = ADH // 2
    return np.concatenate([np.arange(0, 16), half + np.arange(0, 16), np.arange(16, 32), half + np.arange(16, 32)])


def _rotary_tables():
    inv = (np.float32(1.0) / np.float32(10000.0) ** (np.arange(0, ADH, 2, dtype=np.float32) / np.float32(ADH))).astype(np.float32)
    ang = np.arange(S, dtype=np.float32)[:, None] * inv[None, :]
    order = _rotary_order()
    freq, sign = order % (ADH // 2), np.where(order < ADH // 2, -1.0, 1.0).astype(np.float32)
    cos, sin = np.cos(ang)[:, freq].T, np.sin(ang)[:, freq].T * sign[:, None]
    return (np.ascontiguousarray(np.tile(t, (2, 1)).astype(np.float32)) for t in (cos, sin))


def kernel(**inputs):
    import concourse.bacc as bacc
    from concourse.bass_utils import run_bass_kernel_spmd
    import ml_dtypes

    a = {k.replace("L0_attn_", "a_").replace("L0_ffn_", ""): np.ascontiguousarray(v) for k, v in inputs.items()}
    cols = lambda v: np.ascontiguousarray(v.reshape(-1, P).T)
    rows = lambda v: np.ascontiguousarray(np.broadcast_to(v, (P,) + v.shape))
    byexp = lambda v: np.ascontiguousarray(v.reshape(NE, DC, P).transpose(2, 1, 0))
    pairs = lambda v: np.ascontiguousarray(np.broadcast_to(v[:, None, :], (NE, QUAD, F)).reshape(NE // 2, 2 * QUAD, F))
    order = _rotary_order()
    perm = lambda v: np.ascontiguousarray(v.reshape(-1, AH, ADH)[:, :, order].reshape(v.shape))
    cos, sin = _rotary_tables()
    bv_pad = np.zeros((4, 4, QUAD), np.float32)
    bv_pad[:, :, :FDH] = a["d_bv"].reshape(4, 4, FDH)
    wk, wv = a["a_Wkv"][:, :AW], a["a_Wkv"][:, AW:]
    arrays = {
        "x": a["a_x"], "sqT": np.ascontiguousarray(a["slot_query"].reshape(NS, DC, P).transpose(2, 1, 0)),
        "sq_rows": np.repeat(a["slot_query"][0], B, axis=0),
        "d_Wq": a["d_Wq"], "d_WkT": np.ascontiguousarray(a["d_Wk"].T), "d_Wv": a["d_Wv"], "d_Wo": a["d_Wo"],
        "d_bq": cols(a["d_bq"]), "d_bk": cols(a["d_bk"]), "d_bv_pad": np.ascontiguousarray(bv_pad.reshape(4, P).T),
        "d_bo": rows(a["d_bo"]),
        "c_WqT": np.ascontiguousarray(a["c_Wq"].T), "c_Wk": a["c_Wk"], "c_Wv": a["c_Wv"], "c_Wo": a["c_Wo"],
        "c_bq": np.ascontiguousarray(np.repeat(cols(a["c_bq"])[:, :, None], P, axis=2)),
        "c_bk": cols(a["c_bk"]), "c_bv": cols(a["c_bv"]),
        "c_bo": np.ascontiguousarray(np.broadcast_to(a["c_bo"], (P, 2, D))),
        "e_gT": byexp(a["e_ln_g"]), "e_bT": byexp(a["e_ln_b"]), "e_b2T": byexp(a["e_b2"]),
        "e_W1": a["e_W1"], "e_Wg": a["e_Wg"], "e_W2": a["e_W2"], "e_b1": pairs(a["e_b1"]), "e_bg": pairs(a["e_bg"]),
        "a_Wq": perm(a["a_Wq"]), "a_Wk": perm(np.ascontiguousarray(wk)), "a_Wv": np.ascontiguousarray(wv), "a_Wo": a["a_Wo"],
        "a_bq": cols(perm(a["a_bq"])), "a_bk": cols(perm(np.ascontiguousarray(a["a_bkv"][:AW]))),
        "a_bv": rows(np.ascontiguousarray(a["a_bkv"][AW:])), "a_bo": rows(a["a_bo"]),
        "cos": cos, "sin": sin, "ident": np.eye(P, dtype=np.float32), "identb": np.eye(P).astype(ml_dtypes.bfloat16),
        "blkmask": np.repeat(np.repeat(np.eye(HPC, dtype=np.float32), FDH, axis=0), NS, axis=1),
        "masked": np.where(np.arange(P)[None, :] > np.arange(P)[:, None], MASKED, 0.0).astype(ml_dtypes.bfloat16),
    }
    nc = bacc.Bacc("TRN2", target_bir_lowering=False, num_devices=1)
    io = {k: nc.dram_tensor("in_" + k, v.shape, mybir.dt.from_np(v.dtype), kind="ExternalInput").ap() for k, v in arrays.items()}
    io["out"] = nc.dram_tensor("out_x", (B, S, D), F32, kind="ExternalOutput").ap()
    macaron_block(nc, io)
    r = run_bass_kernel_spmd(nc, [{"in_" + k: v for k, v in arrays.items()}], core_ids=[0])
    return r.results[0]["out_x"]
```

```python
from contextlib import ExitStack

import numpy as np

import concourse.bass as bass
from concourse import mybir

F32 = mybir.dt.float32
F32R = mybir.dt.float32r
BF16 = mybir.dt.bfloat16
ALU = mybir.AluOpType
ACT = mybir.ActivationFunctionType
AX = mybir.AxisListType

P = 128
B, S, D = 16, 512, 256
TT = S // P
DC = D // P
FH, FDH = 16, 16
NS = 16
HS = FH * NS
HPC = P // FDH
NE, F = 16, 1024
FK = F // P
AH, ADH = 16, 64
AW = AH * ADH
PAIRS = AH // 2
QUAD = 32
EPS = 1e-5
MASKED = -3.0e38


class Count:

    def __init__(self, sem, per, credit=0):
        self.sem, self.per, self.credit = sem, per, credit

    def at(self, j, n):
        assert n + self.credit >= 1 or not isinstance(j, int) or j * self.per + n + self.credit >= 1
        return j * self.per + (n + self.credit)


def hold(g, eng, sem, value):
    eng.wait_ge(sem, value)
    eng.sem_inc(g.held, 1)


def bcast(ap, axis, n):
    shape = list(ap.shape)
    return ap.unsqueeze(axis).broadcast_to(shape[:axis] + [n] + shape[axis:])


def setup_phase(nc, io, g, sem):
    loaded = sem("setup_loaded")
    q_mm, q_done, blk_done, g_mm, g_done, zeroed, scaled = (
        sem(f"setup_{n}") for n in ("q_mm", "q_done", "blk_done", "g_mm", "g_done", "zeroed", "scaled"))
    LOADS = 12 + 4
    with ExitStack() as s:
        sb = lambda n, sh: s.enter_context(nc.sbuf_tensor(n, sh, F32))
        wq, wkT = sb("su_wq", [P, DC, D]), sb("su_wkT", [P, DC, D])
        sqT, bq, bk = sb("su_sqT", [P, DC, NS]), sb("su_bq", [P, DC]), sb("su_bk", [P, DC])
        qT, qblk = sb("su_qT", [P, DC, NS]), sb("su_qblk", [P, DC, HPC, NS])
        ps_q = s.enter_context(nc.psum_tensor("su_psq", [P, DC, NS], F32))
        ps_g = s.enter_context(nc.psum_tensor("su_psg", [P, DC, HS], F32))
        ps_c = s.enter_context(nc.psum_tensor("su_psc", [P, DC, 2], F32))
        block = s.enter_context(nc.Block())

        @block.sync
        def _(sp):
            sp.wait_ge(zeroed, 2)
            for dst, src in (
                (g.ident[:], io["ident"]), (g.blkmask[:], io["blkmask"]),
                (wq[:], io["d_Wq"].rearrange("(c p) n -> p c n", p=P)),
                (wkT[:], io["d_WkT"].rearrange("(c p) n -> p c n", p=P)),
                (sqT[:], io["sqT"]), (bq[:], io["d_bq"]), (bk[:], io["d_bk"]),
                *((g.wv_pad[:, c, :, 0:FDH], io["d_Wv"].rearrange("(c p) (h e) -> c p h e", p=P, e=FDH)[c]) for c in range(DC)),
                (g.bv_pad[:], io["d_bv_pad"]),
                (g.cwqT[:], io["c_WqT"].rearrange("(c p) n -> p c n", p=P)),
                (g.cwo[:], io["c_Wo"].rearrange("(c p) n -> p c n", p=P)),
            ):
                sp.dma_start(dst, src).then_inc(loaded, 16)
            for q in range(4):
                sp.dma_start(g.wo_pad[q * QUAD:q * QUAD + FDH, :, :],
                             io["d_Wo"].rearrange("(t q e) n -> q e t n", q=4, e=FDH)[q]).then_inc(loaded, 16)

        @block.vector
        def _(dve):
            nc.vector.memset(g.wv_pad[:], 0.0).then_inc(zeroed, 1)
            nc.vector.memset(g.wo_pad[:], 0.0).then_inc(zeroed, 1)
            dve.wait_ge(q_mm, 1)
            for c in range(DC):
                nc.vector.tensor_scalar(qT[:, c, :], ps_q[:, c, :], bq[:, c:c + 1], FDH ** -0.5,
                                        ALU.add, ALU.mult).then_inc(q_done, 1)
            dve.wait_ge(q_done, DC)
            for c in range(DC):
                nc.vector.tensor_tensor(qblk[:, c], g.blkmask[:].rearrange("p (h s) -> p h s", s=NS),
                                        bcast(qT[:, c, :], 1, HPC), ALU.mult).then_inc(blk_done, 1)
            dve.wait_ge(g_mm, 1)
            nc.vector.tensor_copy(g.G[:], ps_g[:]).then_inc(g_done, 1)
            nc.vector.tensor_copy(g.cb[:], ps_c[:, :, 0]).then_inc(g_done, 1)

        @block.tensor
        def _(pe):
            pe.wait_ge(loaded, 16 * LOADS)
            for m in range(DC):
                for c in range(DC):
                    last = nc.tensor.matmul(ps_q[:, m, :], wq[:, c, m * P:(m + 1) * P], sqT[:, c, :],
                                            start=(c == 0), stop=(c == DC - 1))
            last.then_inc(q_mm, 1)
            pe.wait_ge(blk_done, DC)
            for m in range(DC):
                for c in range(DC):
                    nc.tensor.matmul(ps_g[:, m, c * P:(c + 1) * P], wkT[:, c, m * P:(m + 1) * P],
                                     qblk[:, c].rearrange("p h s -> p (h s)"), start=True, stop=True)
            for c in range(DC):
                last = nc.tensor.matmul(ps_c[:, c, 0:1], qblk[:, c].rearrange("p h s -> p (h s)"),
                                        bk[:, c:c + 1], start=True, stop=True)
            last.then_inc(g_mm, 1)


def layernorm_stats(nc, g, dve, x, stats, mv, tiles, stats_sem, mom_sem, j):
    for i in range(tiles):
        nc.vector.bn_stats(stats[:, i, :], x[:, i, :]).then_inc(stats_sem.sem, 1)
    hold(g, dve, stats_sem.sem, stats_sem.at(j, tiles))
    for i in range(tiles):
        nc.vector.bn_aggr(mv[:, i, :], stats[:, i, :]).then_inc(mom_sem.sem, 1)


def layernorm_rstd(nc, g, pool, mv, veps, rstd, tiles, mom_sem, veps_sem, rstd_sem, j):
    hold(g, pool, mom_sem.sem, mom_sem.at(j, tiles))
    nc.gpsimd.tensor_scalar(veps[:, 0:tiles], mv[:, 0:tiles, 1], EPS, None, ALU.add).then_inc(veps_sem.sem, 1)
    pool.wait_ge(veps_sem.sem, veps_sem.at(j, 1))
    nc.gpsimd.tensor_tensor(rstd[:, 0:tiles], veps[:, 0:tiles], g.mhalf[:, 0:tiles], ALU.pow).then_inc(rstd_sem.sem, 1)


class Unit:

    def __init__(self, n, k, i):
        self.k, self.i = k + i // n, i % n
        self.u, self.par = self.k * n + self.i, self.i % 2


def bodies(eng, n, body):
    body(0, first=True)
    with eng.Fori(1, n - 1) as k:
        body(k)
    body(n - 1, last=True)


def expert_loads(io, ring, w_in, pr, par):
    loads = []
    for w, src, bias, bsrc, at in ((ring.w1, io["e_W1"], ring.b1, io["e_b1"], w_in[0]), (ring.wg, io["e_Wg"], ring.bg, io["e_bg"], w_in[1])):
        loads += [(w[:, par, e], src[2 * pr + e].rearrange("(c p) f -> p c f", p=P), at[par]) for e in range(2)]
        loads.append((bias[:, par, :], bsrc[pr], at[par]))
    loads += [(ring.w2[:, par, e], io["e_W2"][2 * pr + e].rearrange("(p k) d -> p k d", k=FK), w_in[2][par]) for e in range(2)]
    return loads


def dispatch_phase(nc, io, g, sem, f, x_dram, at_all, ring, w_in):
    n = lambda x: f"dis_{x}"
    name = lambda x: f"dis{f}_{x}"
    x_in = [sem(n(f"x_in{i}")) for i in range(2)]
    c = lambda x, per, credit=0: Count(sem(n(x)), per, credit)
    NB = 4
    unit = lambda k, i: Unit(NB, k, i)
    stats_s, mom_s, veps_s, rstd_s, xn_s = c("stats", TT), c("moments", TT), c("veps", 1), c("rstd", 1), c("xn", TT, TT)
    xt_mm, xt_s = c("xt_mm", DC), c("xt", DC, DC)
    score_mm, max_s, bias_s, exp_s, recip_s, p_s = (
        c("score_mm", DC, DC), c("max", DC), c("bias", DC), c("exp", DC, DC), c("recip", 1), c("p", DC))
    pt_mm, pt_s, at_mm, at_s = c("pt_mm", 2, 4), c("pt", 2, 2), c("at_mm", 1, NB), c("at", 1, 2)
    with ExitStack() as s:
        sb = lambda nm, sh: s.enter_context(nc.sbuf_tensor(name(nm), sh, F32))
        pb = lambda nm, sh: s.enter_context(nc.psum_tensor(name(nm), sh, F32))
        xin, xn = sb("b_x", [P, 2, TT, D]), sb("b_xn", [P, NB, TT, D])
        stats, mv = sb("b_stats", [P, TT, 6]), sb("b_mv", [P, TT, 2])
        veps, rstd = sb("b_veps", [P, TT]), sb("b_rstd", [P, TT])
        xnT = sb("b_xnT", [P, DC, S])
        nmax, ebias, sums, rinv = (sb(x, [P, DC]) for x in ("b_nmax", "b_ebias", "b_sums", "b_rinv"))
        prob, probT = sb("b_prob", [P, 2, DC, S]), sb("b_probT", [P, TT, HS])
        ps_xt, ps_s = pb("ps_xt", [P, DC, S]), pb("ps_s", [P, DC, S])
        ps_pt, ps_at = pb("ps_pt", [P, TT, HS]), pb("ps_at", [P, 2, DC, HS])
        block = s.enter_context(nc.Block())

        @block.sync
        def _(sp):
            def load(v):
                sp.dma_start(xin[:, v.par], x_dram[v.u].rearrange("(i p) d -> p i d", p=P)).then_inc(x_in[v.par], 16)

            def experts(pair, i):
                for dst, src, at in expert_loads(io, ring, w_in, pair, pair)[2 * i:2 * i + 2]:
                    sp.dma_start(dst, src).then_inc(at, 16)

            def body(k, first=False, last=False):
                for i in range(NB):
                    v = unit(k, i)
                    if not last or i + 2 < NB:
                        hold(g, sp, xn_s.sem, xn_s.at(v.u, TT))
                        load(unit(k, i + 2))
                    if first or last:
                        experts(0 if first else 1, i)

            for i in range(2):
                load(unit(0, i))
            bodies(sp, B // NB, body)

        @block.vector
        def _(dve):
            dve.sem_inc(xn_s.sem, TT)
            dve.sem_inc(at_s.sem, 2)

            def moments(v):
                dve.wait_ge(x_in[v.par], (v.k * (NB // 2) + (v.i // 2 + 1)) * 16)
                dve.wait_ge(xn_s.sem, xn_s.at(v.u, 0))
                layernorm_stats(nc, g, dve, xin[:, v.par], stats, mv, TT, stats_s, mom_s, v.u)

            def normalise(v):
                dve.wait_ge(rstd_s.sem, rstd_s.at(v.u, 1))
                dve.wait_ge(at_mm.sem, at_mm.at(v.u, 1 - NB))
                for i in range(TT):
                    nc.vector.tensor_scalar(xn[:, v.i, i, :], xin[:, v.par, i, :], mv[:, i, 0:1], rstd[:, i:i + 1],
                                            ALU.subtract, ALU.mult).then_inc(xn_s.sem, 1)

            def shift(v, m):
                dve.wait_ge(score_mm.sem, score_mm.at(v.u, m + 1))
                nc.vector.tensor_reduce(nmax[:, m:m + 1], ps_s[:, m, :], AX.X, ALU.max, negate=True)\
                    .then_inc(max_s.sem, 1)
                dve.wait_ge(max_s.sem, max_s.at(v.u, m + 1))
                nc.vector.scalar_tensor_tensor(ebias[:, m:m + 1], nmax[:, m:m + 1], g.cb[:, m:m + 1],
                                               g.cb[:, m:m + 1], ALU.subtract, ALU.add).then_inc(bias_s.sem, 1)

            def scale(v):
                dve.wait_ge(exp_s.sem, exp_s.at(v.u, DC))
                nc.vector.reciprocal(rinv[:], sums[:]).then_inc(recip_s.sem, 1)
                dve.wait_ge(recip_s.sem, recip_s.at(v.u, 1))
                for m in range(DC):
                    nc.vector.tensor_scalar(prob[:, v.par, m, :], prob[:, v.par, m, :], rinv[:, m:m + 1], None,
                                            ALU.mult).then_inc(p_s.sem, 1)

            def keep(v):
                dve.wait_ge(at_mm.sem, at_mm.at(v.u, 1))
                nc.vector.tensor_copy(at_all[:, :, :, v.u], ps_at[:, v.par]).then_inc(at_s.sem, 1)

            def body(k, first=False, last=False):
                for i in range(NB):
                    if not first or i >= 2:
                        keep(unit(k, i - 2))
                    if not last or i + 1 < NB:
                        normalise(unit(k, i + 1))
                    for m in range(DC):
                        shift(unit(k, i), m)
                    if not last or i + 2 < NB:
                        moments(unit(k, i + 2))
                    scale(unit(k, i))

            moments(unit(0, 0))
            normalise(unit(0, 0))
            moments(unit(0, 1))
            bodies(dve, B // NB, body)
            for i in (NB - 2, NB - 1):
                keep(unit(B // NB - 1, i))

        @block.gpsimd
        def _(pool):
            layernorm_rstd(nc, g, pool, mv, veps, rstd, TT, mom_s, veps_s, rstd_s, 0)
            with pool.Fori(1, B) as j:
                layernorm_rstd(nc, g, pool, mv, veps, rstd, TT, mom_s, veps_s, rstd_s, j)

        @block.tensor
        def _(pe):
            for at, credit in ((score_mm, DC), (pt_mm, 4), (at_mm, NB)):
                pe.sem_inc(at.sem, credit)

            def transpose_x(v):
                pe.wait_ge(xn_s.sem, xn_s.at(v.u, TT))
                pe.wait_ge(xt_s.sem, xt_s.at(v.u, 0))
                for c in range(DC):
                    for i in range(TT):
                        last = nc.tensor.transpose(ps_xt[:, c, i * P:(i + 1) * P],
                                                   xn[:, v.i, i, c * P:(c + 1) * P], g.ident[:])
                    last.then_inc(xt_mm.sem, 1)

            def scores(v):
                pe.wait_ge(xt_s.sem, xt_s.at(v.u, DC))
                pe.wait_ge(exp_s.sem, exp_s.at(v.u, 0))
                for m in range(DC):
                    for c in range(DC):
                        last = nc.tensor.matmul(ps_s[:, m, :], g.G[:, c, m * P:(m + 1) * P], xnT[:, c, :],
                                                start=(c == 0), stop=(c == DC - 1))
                    last.then_inc(score_mm.sem, 1)

            def transpose_p(v):
                pe.wait_ge(p_s.sem, p_s.at(v.u, DC))
                pe.wait_ge(pt_s.sem, pt_s.at(v.u, 0))
                for half in range(2):
                    for i in range(2 * half, 2 * half + 2):
                        for m in range(DC):
                            last = nc.tensor.transpose(ps_pt[:, i, m * P:(m + 1) * P],
                                                       prob[:, v.par, m, i * P:(i + 1) * P], g.ident[:])
                    last.then_inc(pt_mm.sem, 1)

            def gather(v):
                pe.wait_ge(pt_s.sem, pt_s.at(v.u, 2))
                pe.wait_ge(at_s.sem, at_s.at(v.u, -1))
                for c in range(DC):
                    for i in range(TT):
                        last = nc.tensor.matmul(ps_at[:, v.par, c, :], xn[:, v.i, i, c * P:(c + 1) * P], probT[:, i, :],
                                                start=(i == 0), stop=(i == TT - 1))
                last.then_inc(at_mm.sem, 1)

            def body(k, first=False, last=False):
                for i in range(NB):
                    before = not first or i >= 1
                    scores(unit(k, i))
                    if before:
                        transpose_p(unit(k, i - 1))
                    if not last or i + 1 < NB:
                        transpose_x(unit(k, i + 1))
                    if before:
                        gather(unit(k, i - 1))

            transpose_x(unit(0, 0))
            bodies(pe, B // NB, body)
            transpose_p(unit(B // NB - 1, NB - 1))
            gather(unit(B // NB - 1, NB - 1))

        @block.scalar
        def _(act):
            for at, credit in ((xt_s, DC), (exp_s, DC), (pt_s, 2)):
                act.sem_inc(at.sem, credit)

            def copy_x(v):
                act.wait_ge(score_mm.sem, score_mm.at(v.u, 0))
                for c in range(DC):
                    act.wait_ge(xt_mm.sem, xt_mm.at(v.u, c + 1))
                    nc.scalar.copy(xnT[:, c, :], ps_xt[:, c, :]).then_inc(xt_s.sem, 1)

            def exps(v, m):
                act.wait_ge(pt_mm.sem, pt_mm.at(v.u, -2))
                act.wait_ge(bias_s.sem, bias_s.at(v.u, m + 1))
                nc.scalar.activation(prob[:, v.par, m, :], ps_s[:, m, :], ACT.Exp, bias=ebias[:, m:m + 1],
                                     accum_out=sums[:, m:m + 1]).then_inc(exp_s.sem, 1)

            def copy_p(v):
                act.wait_ge(at_mm.sem, at_mm.at(v.u, 0))
                for half in range(2):
                    act.wait_ge(pt_mm.sem, pt_mm.at(v.u, half + 1))
                    nc.scalar.copy(probT[:, 2 * half:2 * half + 2, :], ps_pt[:, 2 * half:2 * half + 2, :])\
                        .then_inc(pt_s.sem, 1)

            def body(k, first=False, last=False):
                for i in range(NB):
                    exps(unit(k, i), 0)
                    if not first or i >= 1:
                        copy_p(unit(k, i - 1))
                    exps(unit(k, i), 1)
                    if not last or i + 1 < NB:
                        copy_x(unit(k, i + 1))

            copy_x(unit(0, 0))
            bodies(act, B // NB, body)
            copy_p(unit(B // NB - 1, NB - 1))


def expert_phase(nc, io, g, sem, f, at_all, kT, vT, ring, w_in):
    n = lambda x: f"ex_{x}"
    name = lambda x: f"ex{f}_{x}"
    one = lambda x: sem(n(x))
    c = lambda x, per: Count(sem(n(x)), per)
    NP = NE // 2
    R = 2 * QUAD
    tab_in, padded, rows_s, v_mm, v_s, o_mm, o_s = (one(x) for x in ("tab", "pad", "rows", "v_mm", "v", "o_mm", "o"))
    stats_s, mom_s, veps_s, rstd_s = c("stats", 2), c("moments", 2), c("veps", 1), c("rstd", 1)
    h0_s, hT_mm, hg_s, hb_s, oT_s = one("h0"), one("hT_mm"), one("hg"), one("hb"), one("oT")
    stage_s, up_mm, pre_s, silu_s, ug_s = c("stage", 1), c("up_mm", 2), c("pre", 2), c("silu", 2), c("ug", 1)
    ugT_mm, ugT_s, y_mm, y_s, yT_mm, on_s = c("ugT_mm", 1), c("ugT", 1), c("y_mm", 1), c("y", 1), c("yT_mm", 1), c("on", 1)
    kv_mm, kv_s, bk_s = one("kv_mm"), one("kv"), one("bk")
    with ExitStack() as s:
        sb = lambda nm, sh: s.enter_context(nc.sbuf_tensor(name(nm), sh, F32))
        pb = lambda nm, sh: s.enter_context(nc.psum_tensor(name(nm), sh, F32))
        sq, bo = sb("t_sq", [P, 2, D]), sb("t_bo", [P, D])
        gT, bT, b2T = (sb(x, [P, DC, NE]) for x in ("t_gT", "t_bT", "t_b2T"))
        cwk, cwv = sb("t_cwk", [P, DC, D]), sb("t_cwv", [P, DC, D])
        bk, bv, bk4 = sb("t_bk", [P, DC]), sb("t_bv", [P, DC]), sb("t_bk4", [P, DC])
        attnT = sb("t_attnT", [P, 4, HS])
        o, h0 = sb("t_o", [P, 2, D]), sb("t_h0", [P, 2, D])
        stats, mv, veps, rstd = sb("t_st", [P, 2, 6]), sb("t_mv", [P, 2, 2]), sb("t_ve", [P, 2]), sb("t_rs", [P, 2])
        hg = sb("t_hg", [P, DC, NE, B])
        hP = sb("t_hP", [P, DC, NE, QUAD])
        oT, onT = sb("t_oT", [P, DC, NE, B]), sb("t_onT", [P, DC, NE, B])
        w1, wg, w2, b1, bg = ring.w1, ring.wg, ring.w2, ring.b1, ring.bg
        stage = sb("t_stage", [P, 2, DC, 2, QUAD])
        ub, gb = sb("t_ub", [R, F]), sb("t_gb", [R, F])
        ugT, y = sb("t_ugT", [P, FK, R]), sb("t_y", [R, D])
        ps_u, ps_g = pb("ps_u", [P, F]), pb("ps_g", [P, F])
        ps_ugT, ps_y, ps_yT, ps_kv = pb("ps_ugT", [P, FK, R]), pb("ps_y", [P, 512]), pb("ps_yT", [P, DC, R]), pb("ps_kv", [P, 2, 256])
        ps_v = ps_u[:].rearrange("p (t r) -> p t r", t=4)
        ps_o = ps_g[:, 0:2 * D].rearrange("p (m d) -> p m d", m=2)
        ps_hT = ps_ugT[:].rearrange("p k r -> p (k r)").rearrange("p (c r) -> p c r", c=DC)
        ps_oT = ps_y[:].rearrange("p (c r) -> p c r", c=DC)
        TABS = 9
        block = s.enter_context(nc.Block())

        @block.sync
        def _(sp):
            def load_up(pr, par):
                loads = expert_loads(io, ring, w_in, pr, par)
                for i in range(2):
                    hold(g, sp, pre_s.sem, pre_s.at(pr - 2, i + 1))
                    for dst, src, at in loads[3 * i:3 * i + 3]:
                        sp.dma_start(dst, src).then_inc(at, 16)

            def load_down(pr, par):
                hold(g, sp, y_mm.sem, y_mm.at(pr - 2, 1))
                for dst, src, at in expert_loads(io, ring, w_in, pr, par)[-2:]:
                    sp.dma_start(dst, src).then_inc(at, 16)

            for dst, src in ((sq[:], io["sq_rows"].rearrange("(m p) d -> p m d", p=P)), (bo[:], io["d_bo"]),
                             (gT[:], io["e_gT"]), (bT[:], io["e_bT"]), (b2T[:], io["e_b2T"]),
                             (cwk[:], io["c_Wk"].rearrange("(c p) n -> p c n", p=P)),
                             (cwv[:], io["c_Wv"].rearrange("(c p) n -> p c n", p=P)),
                             (bk[:], io["c_bk"]), (bv[:], io["c_bv"])):
                sp.dma_start(dst, src).then_inc(tab_in, 16)
            load_up(2, 0)
            with sp.Fori(1, NP // 2 - 1) as k:
                for par in range(2):
                    load_up(2 * k + 1 + par, 1 - par)
                    load_down(2 * k + par, par)
            load_up(NP - 1, 1)
            load_down(NP - 2, 0)
            load_down(NP - 1, 1)

        @block.vector
        def _(dve):
            nc.vector.memset(hP[:], 0.0).then_inc(padded, 1)
            dve.wait_ge(tab_in, 16 * TABS)
            nc.vector.tensor_scalar(bk4[:], bk[:], FDH ** -0.5, None, ALU.mult).then_inc(bk_s, 1)
            for m in range(2):
                nc.vector.tensor_tensor(sq[:, m, :], sq[:, m, :], bo[:], ALU.add).then_inc(rows_s, 1)
            dve.wait_ge(o_mm, 1)
            dve.wait_ge(rows_s, 2)
            nc.vector.tensor_tensor(o[:], ps_o, sq[:], ALU.add).then_inc(o_s, 1)
            dve.wait_ge(o_s, 1)
            layernorm_stats(nc, g, dve, o, stats, mv, 2, stats_s, mom_s, 0)
            dve.wait_ge(rstd_s.sem, rstd_s.at(0, 1))
            for m in range(2):
                nc.vector.tensor_scalar(h0[:, m, :], o[:, m, :], mv[:, m, 0:1], rstd[:, m:m + 1],
                                        ALU.subtract, ALU.mult).then_inc(h0_s, 1)
            dve.wait_ge(hT_mm, 2)
            for ch in range(DC):
                nc.vector.tensor_tensor(hg[:, ch], ps_hT[:, ch].rearrange("p (e b) -> p e b", b=B),
                                        bcast(gT[:, ch, :], 2, B), ALU.mult).then_inc(hg_s, 1)
                nc.vector.tensor_tensor(oT[:, ch], ps_oT[:, ch].rearrange("p (e b) -> p e b", b=B),
                                        bcast(b2T[:, ch, :], 2, B), ALU.add).then_inc(oT_s, 1)
            dve.wait_ge(hg_s, DC)
            dve.wait_ge(padded, 1)
            for ch in range(DC):
                nc.vector.tensor_tensor(hP[:, ch, :, 0:B], hg[:, ch], bcast(bT[:, ch, :], 2, B), ALU.add).then_inc(hb_s, 1)
            dve.wait_ge(hb_s, DC)
            dve.wait_ge(oT_s, DC)

            def hidden(pr, par, first=False):
                if not first:
                    dve.wait_ge(up_mm.sem, up_mm.at(pr, -2))
                nc.vector.tensor_copy(stage[:, par], hP[:, :, bass.ds(2 * pr, 2), :]).then_inc(stage_s.sem, 1)

            def step(pr, par, h, first=False, second=False, last=False):
                if not last:
                    hidden(pr + 1, 1 - par, first)
                for i, (bias, ps, pre) in enumerate(((b1, ps_u, ub), (bg, ps_g, gb))):
                    dve.wait_ge(up_mm.sem, up_mm.at(pr, i + 1))
                    if not first and i == 0:
                        dve.wait_ge(ugT_mm.sem, ugT_mm.at(pr, 0))
                    nc.vector.tensor_tensor(pre[:], ps[0:R, :], bias[:, par, :], ALU.add).then_inc(pre_s.sem, 1)
                dve.wait_ge(silu_s.sem, silu_s.at(pr, 2))
                nc.vector.tensor_tensor(ub[:], ub[:], gb[:], ALU.mult).then_inc(ug_s.sem, 1)
                if not first:
                    finish(pr - 1)

            def finish(pr):
                dve.wait_ge(yT_mm.sem, yT_mm.at(pr, 1))
                nc.vector.tensor_tensor(onT[:, :, bass.ds(2 * pr, 2), :],
                                        ps_yT[:].rearrange("p c (e r) -> p c e r", e=2)[:, :, :, 0:B],
                                        oT[:, :, bass.ds(2 * pr, 2), :], ALU.add).then_inc(on_s.sem, 1)

            hidden(0, 0, True)
            step(0, 0, 0, first=True)
            with dve.Fori(0, NP // 2 - 1) as k:
                step(2 * k + 1, 1, k)
                step(2 * k + 2, 0, k + 1)
            step(NP - 1, 1, NP // 2 - 1, last=True)
            finish(NP - 1)

        @block.gpsimd
        def _(pool):
            layernorm_rstd(nc, g, pool, mv, veps, rstd, 2, mom_s, veps_s, rstd_s, 0)

        @block.tensor
        def _(pe):
            for t in range(4):
                for ch in range(DC):
                    for q in range(4):
                        h = 4 * t + q
                        last = nc.tensor.matmul(
                            ps_v[q * QUAD:(q + 1) * QUAD, t, :], g.wv_pad[:, ch, h, :],
                            at_all[:, ch, h * NS:(h + 1) * NS, :].rearrange("p s b -> p (s b)"),
                            start=(ch == 0), stop=(ch == DC - 1))
            last.then_inc(v_mm, 1)
            pe.wait_ge(v_s, 4)
            for m in range(2):
                for t in range(4):
                    last = nc.tensor.matmul(ps_o[:, m, :], attnT[:, t, m * P:(m + 1) * P], g.wo_pad[:, t, :],
                                            start=(t == 0), stop=(t == 3))
            last.then_inc(o_mm, 1)
            pe.wait_ge(h0_s, 2)
            for src, dst in ((h0, ps_hT), (o, ps_oT)):
                for ch in range(DC):
                    for m in range(2):
                        last = nc.tensor.transpose(dst[:, ch, m * P:(m + 1) * P], src[:, m, ch * P:(ch + 1) * P], g.ident[:])
                last.then_inc(hT_mm, 1)

            def up(pr, par, h, first=False):
                pe.wait_ge(stage_s.sem, stage_s.at(pr, 1))
                for i, (w, ps) in enumerate(((w1, ps_u), (wg, ps_g))):
                    pe.wait_ge(w_in[i][par], (h + 1) * 48)
                    if not first:
                        pe.wait_ge(pre_s.sem, pre_s.at(pr, i - 1))
                    for half in range(2):
                        for ch in range(DC):
                            for e in range(2):
                                last = nc.tensor.matmul(ps[e * QUAD:(e + 1) * QUAD, half * 512:(half + 1) * 512],
                                                        stage[:, par, ch, e, :], w[:, par, e, ch, half * 512:(half + 1) * 512],
                                                        start=(ch == 0), stop=(ch == DC - 1))
                    last.then_inc(up_mm.sem, 1)

            def down(pr, par, h, first=False):
                pe.wait_ge(ug_s.sem, ug_s.at(pr, 1))
                if not first:
                    hold(g, pe, ugT_s.sem, ugT_s.at(pr, 0))
                for k in range(FK):
                    last = nc.tensor.transpose(ps_ugT[:, k, :], ub[:].rearrange("r (p k) -> r k p", k=FK)[:, k, :],
                                               g.ident[0:R, 0:R])
                last.then_inc(ugT_mm.sem, 1)
                pe.wait_ge(ugT_s.sem, ugT_s.at(pr, 1))
                pe.wait_ge(w_in[2][par], (h + 1) * 32)
                if not first:
                    pe.wait_ge(y_s.sem, y_s.at(pr, 0))
                for k in range(FK):
                    for e in range(2):
                        last = nc.tensor.matmul(ps_y[e * QUAD:(e + 1) * QUAD, 0:D], ugT[:, k, e * QUAD:(e + 1) * QUAD],
                                                w2[:, par, e, k, :], start=(k == 0), stop=(k == FK - 1))
                last.then_inc(y_mm.sem, 1)
                pe.wait_ge(y_s.sem, y_s.at(pr, 1))
                if not first:
                    hold(g, pe, on_s.sem, on_s.at(pr, 0))
                for ch in range(DC):
                    last = nc.tensor.transpose(ps_yT[:, ch, :], y[:, ch * P:(ch + 1) * P], g.ident[0:R, 0:R])
                last.then_inc(yT_mm.sem, 1)

            up(0, 0, 0, True)
            up(1, 1, 0)
            down(0, 0, 0, True)
            with pe.Fori(1, NP // 2) as k:
                up(2 * k, 0, k)
                down(2 * k - 1, 1, k - 1)
                up(2 * k + 1, 1, k)
                down(2 * k, 0, k)
            down(NP - 1, 1, NP // 2 - 1)
            pe.wait_ge(on_s.sem, on_s.at(NP - 1, 1))
            for i, (w, ps) in enumerate(((cwk, ps_kv), (cwv, ps_o))):
                for m in range(2):
                    for ch in range(DC):
                        last = nc.tensor.matmul(ps[:, m, :], w[:, ch, m * P:(m + 1) * P],
                                                onT[:, ch].rearrange("p e b -> p (e b)"),
                                                start=(ch == 0), stop=(ch == DC - 1))
                last.then_inc(kv_mm, 1)

        @block.scalar
        def _(act):
            act.wait_ge(v_mm, 1)
            for t in range(4):
                nc.scalar.activation(attnT[:, t, :], ps_v[:, t, :], ACT.Identity, bias=g.bv_pad[:, t:t + 1]).then_inc(v_s, 1)

            def silu(pr):
                for i, pre in enumerate((ub, gb)):
                    act.wait_ge(pre_s.sem, pre_s.at(pr, i + 1))
                    nc.scalar.activation(pre[:], pre[:], ACT.Silu).then_inc(silu_s.sem, 1)

            def copy_hidden(pr, first=False):
                act.wait_ge(ugT_mm.sem, ugT_mm.at(pr, 1))
                if not first:
                    act.wait_ge(y_mm.sem, y_mm.at(pr, 0))
                nc.scalar.copy(ugT[:], ps_ugT[:]).then_inc(ugT_s.sem, 1)

            def copy_y(pr, first=False):
                act.wait_ge(y_mm.sem, y_mm.at(pr, 1))
                if not first:
                    act.wait_ge(yT_mm.sem, yT_mm.at(pr, 0))
                nc.scalar.copy(y[:], ps_y[0:R, 0:D]).then_inc(y_s.sem, 1)

            def step(pr, first=False):
                copy_hidden(pr - 1, first)
                silu(pr)
                copy_y(pr - 1, first)

            silu(0)
            step(1, True)
            with act.Fori(2, NP) as pr:
                step(pr)
            copy_hidden(NP - 1)
            copy_y(NP - 1)
            act.wait_ge(bk_s, 1)
            act.wait_ge(kv_mm, 1)
            for m in range(DC):
                nc.scalar.activation(kT[:, m].rearrange("p s b -> p (s b)"), ps_kv[:, m, :], ACT.Identity,
                                     bias=bk4[:, m:m + 1], scale=FDH ** -0.5).then_inc(kv_s, 1)
            act.wait_ge(kv_mm, 2)
            for m in range(DC):
                nc.scalar.activation(vT[:, m].rearrange("p s b -> p (s b)"), ps_o[:, m, :], ACT.Identity,
                                     bias=bv[:, m:m + 1]).then_inc(kv_s, 1)


def combine_phase(nc, io, g, sem, f, x_dram, out_dram, kT, vT):
    n = lambda x: f"com_{x}"
    name = lambda x: f"com{f}_{x}"
    c = lambda x, per, credit=0: Count(sem(n(x)), per, credit)
    W, NB = 2, 4
    NK = 2 * B // NB
    tab_in, half_s = sem(n("tab")), sem(n("half"))
    x_in = [sem(n(f"x_in{i}")) for i in range(NB)]
    out_s = [c(f"out{i}", 16, 16) for i in range(2)]
    stats_s, mom_s, veps_s, rstd_s, xn_s = c("stats", W), c("moments", W), c("veps", 1), c("rstd", 1), c("xn", W, W)
    blk_s, gu_mm, g_s, cb_mm, cb_s = c("blk", 4), c("gu_mm", 2, 2), c("gu", 2, 2), c("cb_mm", 1, 1), c("cb", 1, 1)
    xt_mm, xt_s, s_mm, s1_s, o_mm, pt_s = (c(x, 1, 1) for x in ("xt_mm", "xt", "s_mm", "s1", "o_mm", "pt"))
    nm_s, nmr_s = c("nm", 1), c("nmr", 1)
    max_s, sub_s, exp_s, sum_s, rec_s, p_s, xb_s = (c(x, 1) for x in ("max", "sub", "exp", "sum", "rec", "p", "xb"))
    pt_mm, o_s = c("pt_mm", 1, 2), c("o", 1, NB)

    def unit(k, i):
        v = Unit(NB, k, i)
        v.j, v.jp, v.p = v.k * 2 + v.i // 2, v.i // 2, v.par
        return v

    with ExitStack() as s:
        sb = lambda nm, sh: s.enter_context(nc.sbuf_tensor(name(nm), sh, F32))
        pb = lambda nm, sh: s.enter_context(nc.psum_tensor(name(nm), sh, F32))
        bq, bo, boh = sb("t_bq", [P, DC, P]), sb("t_bo", [P, W, D]), sb("t_boh", [P, W, D])
        xin, xb, xo = sb("b_x", [P, NB, W, D]), sb("b_xb", [P, NB, W, D]), sb("b_xo", [P, 2, W, D])
        stats, mv, veps, rstd = sb("b_st", [P, W, 6]), sb("b_mv", [P, W, 2]), sb("b_ve", [P, W]), sb("b_rs", [P, W])
        nmr = sb("b_nmr", [P, W])
        xn, xnT = sb("b_xn", [P, W, D]), sb("b_xnT", [P, DC, W * P])
        kblk, vblk = sb("b_kblk", [P, DC, HPC, NS]), sb("b_vblk", [P, DC, HPC, NS])
        G, U, cb = sb("b_G", [P, 2, DC, HS]), sb("b_U", [P, 2, DC, D]), sb("b_cb", [P, 2, HS])
        s1, prob = sb("b_s1", [P, W, HS]), sb("b_prob", [P, 2, W, HS])
        mx, sm, rc = (sb(x, [P, W * FH]) for x in ("b_mx", "b_sm", "b_rc"))
        pT = sb("b_pT", [P, DC, W * P])
        ps_xt, ps_g, ps_u, ps_c = pb("ps_xt", [P, DC, W * P]), pb("ps_g", [P, DC, HS]), pb("ps_u", [P, DC, D]), pb("ps_c", [P, 512])
        ps_s, ps_pt, ps_o = pb("ps_s", [P, W, HS]), pb("ps_pt", [P, DC, W * P]), pb("ps_o", [P, 2, W, D])
        heads = lambda ap: ap.rearrange("p w (h s) -> p (w h) s", s=NS)
        block = s.enter_context(nc.Block())

        @block.sync
        def _(sp):
            sp.dma_start(bq[:], io["c_bq"]).then_inc(tab_in, 16)
            sp.dma_start(bo[:], io["c_bo"]).then_inc(tab_in, 16)
            for i in range(2):
                sp.sem_inc(out_s[i].sem, 16)

            def rows(dram, v):
                return dram[v.j].rearrange("(u i p) d -> u p i d", u=2, p=P)[v.p]

            def load(v):
                sp.dma_start(xin[:, v.i], rows(x_dram, v)).then_inc(x_in[v.i], 16)

            def store(v):
                hold(g, sp, o_s.sem, o_s.at(v.u, 1))
                sp.dma_start(rows(out_dram, v), xo[:, v.p]).then_inc(out_s[v.p].sem, 16)

            def body(k, first=False, last=False):
                for i in range(NB):
                    v = unit(k, i)
                    if not last:
                        hold(g, sp, xn_s.sem, xn_s.at(v.u, W))
                        hold(g, sp, xb_s.sem, xb_s.at(v.u, 1))
                        load(unit(k, i + NB))
                    if not first or i >= 3:
                        store(unit(k, i - 3))

            for i in range(NB):
                load(unit(0, i))
            bodies(sp, NK, body)
            for i in range(1, NB):
                store(unit(NK - 1, i))
            for p in range(2):
                sp.wait_ge(out_s[p].sem, out_s[p].at(B, 0))

        @block.vector
        def _(dve):
            dve.sem_inc(s1_s.sem, 1)
            dve.sem_inc(o_s.sem, NB)
            dve.wait_ge(tab_in, 32)
            nc.vector.tensor_scalar(boh[:], bo[:], 0.5, None, ALU.mult).then_inc(half_s, 1)

            def moments(v):
                dve.wait_ge(x_in[v.i], (v.k + 1) * 16)
                dve.wait_ge(xn_s.sem, xn_s.at(v.u, 0))
                layernorm_stats(nc, g, dve, xin[:, v.i], stats, mv, W, stats_s, mom_s, v.u)

            def shift(v):
                dve.wait_ge(cb_s.sem, cb_s.at(v.j, 1))
                dve.wait_ge(s_mm.sem, s_mm.at(v.u, 1))
                nc.vector.tensor_tensor(s1[:], ps_s[:], bcast(cb[:, v.jp, :], 1, W), ALU.add).then_inc(s1_s.sem, 1)
                dve.wait_ge(s1_s.sem, s1_s.at(v.u, 1))
                nc.vector.tensor_reduce(mx[:], heads(s1[:]), AX.X, ALU.max).then_inc(max_s.sem, 1)
                dve.wait_ge(max_s.sem, max_s.at(v.u, 1))
                nc.vector.tensor_tensor(heads(s1[:]), heads(s1[:]), bcast(mx[:], 2, NS), ALU.subtract).then_inc(sub_s.sem, 1)

            def scale(v):
                dve.wait_ge(exp_s.sem, exp_s.at(v.u, 1))
                pr = heads(prob[:, v.p])
                nc.vector.tensor_reduce(sm[:], pr, AX.X, ALU.add).then_inc(sum_s.sem, 1)
                dve.wait_ge(sum_s.sem, sum_s.at(v.u, 1))
                nc.vector.reciprocal(rc[:], sm[:]).then_inc(rec_s.sem, 1)
                dve.wait_ge(rec_s.sem, rec_s.at(v.u, 1))
                nc.vector.tensor_tensor(pr, pr, bcast(rc[:], 2, NS), ALU.mult).then_inc(p_s.sem, 1)

            def result(v):
                dve.wait_ge(o_mm.sem, o_mm.at(v.u, 1))
                dve.wait_ge(xb_s.sem, xb_s.at(v.u, 1))
                dve.wait_ge(out_s[v.p].sem, out_s[v.p].at(v.j, 0))
                nc.vector.scalar_tensor_tensor(xo[:, v.p], ps_o[:, v.p], 0.5, xb[:, v.i], ALU.mult, ALU.add)\
                    .then_inc(o_s.sem, 1)

            def body(k, first=False, last=False):
                for i in range(NB):
                    if not first or i >= 1:
                        scale(unit(k, i - 1))
                    shift(unit(k, i))
                    if not last or i + 2 < NB:
                        moments(unit(k, i + 2))
                    if not first or i >= 2:
                        result(unit(k, i - 2))

            for i in range(2):
                moments(unit(0, i))
            bodies(dve, NK, body)
            scale(unit(NK - 1, NB - 1))
            for i in (NB - 2, NB - 1):
                result(unit(NK - 1, i))

        @block.gpsimd
        def _(pool):
            pool.wait_ge(half_s, 1)

            def blocks(v):
                for src, dst, used in ((kT, kblk, -1), (vT, vblk, 0)):
                    pool.wait_ge(gu_mm.sem, gu_mm.at(v.j, used))
                    for ch in range(DC):
                        nc.gpsimd.tensor_tensor(dst[:, ch], g.blkmask[:].rearrange("p (h s) -> p h s", s=NS),
                                                bcast(src[:, ch, :, v.j], 1, HPC), ALU.mult).then_inc(blk_s.sem, 1)

            def residual(v):
                layernorm_rstd(nc, g, pool, mv, veps, rstd, W, mom_s, veps_s, rstd_s, v.u)
                nc.gpsimd.tensor_scalar(nmr[:], mv[:, :, 0], -1.0, None, ALU.mult).then_inc(nm_s.sem, 1)
                pool.wait_ge(nm_s.sem, nm_s.at(v.u, 1))
                nc.gpsimd.tensor_tensor(nmr[:], nmr[:], rstd[:], ALU.mult).then_inc(nmr_s.sem, 1)
                pool.wait_ge(o_s.sem, o_s.at(v.u, 1 - NB))
                nc.gpsimd.tensor_tensor(xb[:, v.i], xin[:, v.i], boh[:], ALU.add).then_inc(xb_s.sem, 1)

            def body(k, first=False, last=False):
                for i in range(NB):
                    if i % 2 == 0 and (not last or i + 2 < NB):
                        blocks(unit(k, i + 2))
                    if not last or i + 2 < NB:
                        residual(unit(k, i + 2))

            blocks(unit(0, 0))
            for i in range(2):
                residual(unit(0, i))
            bodies(pool, NK, body)

        @block.tensor
        def _(pe):
            for at, credit in ((gu_mm, 2), (cb_mm, 1), (xt_mm, 1), (s_mm, 1), (o_mm, 1), (pt_mm, 2)):
                pe.sem_inc(at.sem, credit)

            def fold_biases(v):
                pe.wait_ge(blk_s.sem, blk_s.at(v.j, 2))
                pe.wait_ge(cb_s.sem, cb_s.at(v.j, 0))
                for ch in range(DC):
                    last = nc.tensor.matmul(ps_c[:, ch * P:(ch + 1) * P], bq[:, ch, :],
                                            kblk[:, ch].rearrange("p h s -> p (h s)"), start=True, stop=True)
                last.then_inc(cb_mm.sem, 1)

            def fold_keys(v):
                pe.wait_ge(g_s.sem, g_s.at(v.j, -1))
                for m in range(DC):
                    for ch in range(DC):
                        last = nc.tensor.matmul(ps_g[:, m, ch * P:(ch + 1) * P], g.cwqT[:, ch, m * P:(m + 1) * P],
                                                kblk[:, ch].rearrange("p h s -> p (h s)"), start=True, stop=True)
                last.then_inc(gu_mm.sem, 1)

            def fold_values(v):
                pe.wait_ge(blk_s.sem, blk_s.at(v.j, 4))
                pe.wait_ge(g_s.sem, g_s.at(v.j, 0))
                for ch in range(DC):
                    last = nc.tensor.matmul(ps_u[:, ch, :], vblk[:, ch].rearrange("p h s -> p (h s)"), g.cwo[:, ch, :],
                                            start=True, stop=True)
                last.then_inc(gu_mm.sem, 1)

            def transpose_x(v):
                pe.wait_ge(xn_s.sem, xn_s.at(v.u, W))
                pe.wait_ge(xt_s.sem, xt_s.at(v.u, 0))
                for ch in range(DC):
                    for i in range(W):
                        last = nc.tensor.transpose(ps_xt[:, ch, i * P:(i + 1) * P], xn[:, i, ch * P:(ch + 1) * P], g.ident[:])
                last.then_inc(xt_mm.sem, 1)

            def scores(v):
                pe.wait_ge(xt_s.sem, xt_s.at(v.u, 1))
                pe.wait_ge(g_s.sem, g_s.at(v.j, 1))
                pe.wait_ge(s1_s.sem, s1_s.at(v.u, 0))
                for i in range(W):
                    for ch in range(DC):
                        last = nc.tensor.matmul(ps_s[:, i, :], xnT[:, ch, i * P:(i + 1) * P], G[:, v.jp, ch, :],
                                                start=(ch == 0), stop=(ch == DC - 1))
                last.then_inc(s_mm.sem, 1)

            def transpose_p(v):
                pe.wait_ge(p_s.sem, p_s.at(v.u, 1))
                pe.wait_ge(pt_s.sem, pt_s.at(v.u, 0))
                for ch in range(DC):
                    for i in range(W):
                        last = nc.tensor.transpose(ps_pt[:, ch, i * P:(i + 1) * P], prob[:, v.p, i, ch * P:(ch + 1) * P], g.ident[:])
                last.then_inc(pt_mm.sem, 1)

            def mix(v):
                pe.wait_ge(pt_s.sem, pt_s.at(v.u, 1))
                pe.wait_ge(g_s.sem, g_s.at(v.j, 2))
                pe.wait_ge(o_s.sem, o_s.at(v.u, -1))
                for i in range(W):
                    for ch in range(DC):
                        last = nc.tensor.matmul(ps_o[:, v.p, i, :], pT[:, ch, i * P:(i + 1) * P], U[:, v.jp, ch, :],
                                                start=(ch == 0), stop=(ch == DC - 1))
                last.then_inc(o_mm.sem, 1)

            def body(k, first=False, last=False):
                for i in range(NB):
                    before, following = not first or i >= 1, not last or i + 1 < NB
                    scores(unit(k, i))
                    if i % 2 == 0:
                        if before:
                            transpose_p(unit(k, i - 1))
                        transpose_x(unit(k, i + 1))
                        fold_values(unit(k, i))
                    else:
                        if following:
                            fold_biases(unit(k, i + 1))
                            transpose_x(unit(k, i + 1))
                        transpose_p(unit(k, i - 1))
                        if following:
                            fold_keys(unit(k, i + 1))
                    if before:
                        mix(unit(k, i - 1))

            fold_biases(unit(0, 0))
            fold_keys(unit(0, 0))
            transpose_x(unit(0, 0))
            bodies(pe, NK, body)
            transpose_p(unit(NK - 1, NB - 1))
            mix(unit(NK - 1, NB - 1))

        @block.scalar
        def _(act):
            for at, credit in ((g_s, 2), (cb_s, 1), (xt_s, 1), (pt_s, 1), (xn_s, W)):
                act.sem_inc(at.sem, credit)

            def normalise(v):
                act.wait_ge(nmr_s.sem, nmr_s.at(v.u, 1))
                act.wait_ge(xt_mm.sem, xt_mm.at(v.u, 0))
                for i in range(W):
                    nc.scalar.activation(xn[:, i, :], xin[:, v.i, i, :], ACT.Identity, bias=nmr[:, i:i + 1],
                                         scale=rstd[:, i:i + 1]).then_inc(xn_s.sem, 1)

            def keys(v):
                act.wait_ge(gu_mm.sem, gu_mm.at(v.j, 1))
                nc.scalar.copy(G[:, v.jp], ps_g[:]).then_inc(g_s.sem, 1)

            def values(v):
                act.wait_ge(gu_mm.sem, gu_mm.at(v.j, 2))
                nc.scalar.copy(U[:, v.jp], ps_u[:]).then_inc(g_s.sem, 1)

            def biases(v):
                act.wait_ge(cb_mm.sem, cb_mm.at(v.j, 1))
                nc.scalar.copy(cb[:, v.jp, :], ps_c[:, 0:HS]).then_inc(cb_s.sem, 1)

            def copy_x(v):
                act.wait_ge(xt_mm.sem, xt_mm.at(v.u, 1))
                act.wait_ge(s_mm.sem, s_mm.at(v.u, 0))
                nc.scalar.copy(xnT[:], ps_xt[:]).then_inc(xt_s.sem, 1)

            def exps(v):
                act.wait_ge(sub_s.sem, sub_s.at(v.u, 1))
                act.wait_ge(pt_mm.sem, pt_mm.at(v.u, -1))
                nc.scalar.activation(prob[:, v.p], s1[:], ACT.Exp).then_inc(exp_s.sem, 1)

            def copy_p(v):
                act.wait_ge(pt_mm.sem, pt_mm.at(v.u, 1))
                act.wait_ge(o_mm.sem, o_mm.at(v.u, 0))
                nc.scalar.copy(pT[:], ps_pt[:]).then_inc(pt_s.sem, 1)

            def body(k, first=False, last=False):
                for i in range(NB):
                    following = not last or i + 1 < NB
                    if following:
                        normalise(unit(k, i + 1))
                    if i % 2 == 0:
                        if not first or i >= 1:
                            copy_p(unit(k, i - 1))
                        copy_x(unit(k, i + 1))
                        exps(unit(k, i))
                        values(unit(k, i))
                    else:
                        if following:
                            copy_x(unit(k, i + 1))
                        copy_p(unit(k, i - 1))
                        if following:
                            biases(unit(k, i + 1))
                        exps(unit(k, i))
                        if following:
                            keys(unit(k, i + 1))

            normalise(unit(0, 0))
            keys(unit(0, 0))
            biases(unit(0, 0))
            copy_x(unit(0, 0))
            bodies(act, NK, body)
            copy_p(unit(NK - 1, NB - 1))


def attention_phase(nc, io, g, sem, x_dram, out_dram, ffn_sems):
    WIDTH = [S - kb * P for kb in range(TT)]
    TURNS = ((0,), (2,), (1, 3))
    NT = len(TURNS)
    OFF = [0, 768, 512, 1152]
    FULL = sum(WIDTH)
    n = lambda x: f"att_{x}"
    c = lambda x, per, credit=0: Count(sem(n(x)), per, credit)
    one = lambda x: sem(n(x))
    tab_in, w_hi, w_lo, zero_s, bqs_s = (one(x) for x in ("tab", "w_hi", "w_lo", "zero", "bqs"))
    w_in = [one(f"w{w}_in") for w in "qkvo"]
    x_in, xres_in, out_s = c("x_in", 16), c("xres_in", 16), c("out", 16, 16)
    stats_s, mom_s, veps_s, rstd_s, xn_s = c("stats", TT), c("moments", TT), c("veps", 1), c("rstd", 1), c("xn", TT, TT)
    xt_mm, xhi_s, xlo_s = c("xt_mm", DC, DC), c("xhi", DC), c("xlo", DC)
    v_mm, v_s = c("v_mm", 2 * TT), c("v", 2 * TT)
    z_mm, z_s, shuf_s, cos_s, sin_s = (c(x, 2 * PAIRS, 2 * PAIRS) for x in ("z_mm", "z", "shuf", "cos", "sin"))
    sum_s, qhi_s, khi_s = c("sum", 2 * PAIRS), c("qhi", 2 * PAIRS), c("khi", PAIRS)
    rq_s, rk_s = c("rq", 2 * PAIRS, 2), c("rk", PAIRS, 1)
    s_mm, max_s, exp_s, rec_s, p_s = (
        c("s_mm", 4 * AH, 9), c("max", 4 * AH), c("exp", 4 * AH, 4), c("rec", AH), c("p", 4 * AH))
    pt_mm, pt_s, pv_mm, ohi_s, olo_s = (
        c("pt_mm", NT * AH, NT * AH), c("pt", NT * AH, 1), c("pv_mm", PAIRS, 1), c("ohi", PAIRS), c("olo", PAIRS, 1))
    wo_mm, xb_s, xo_s = c("wo_mm", 2, 2), c("xb", TT), c("xo", 2, 2)
    V_SLOT, X_SLOT = 3, AH - 3
    PLACE = [slice(o, o + (qt + 1) * P) for qt, o in enumerate((0, 128, 384, 768))]
    with ExitStack() as s:
        sb = lambda nm, sh, dt=F32: s.enter_context(nc.sbuf_tensor(n(nm), sh, dt))
        pb = lambda nm, sh: s.enter_context(nc.psum_tensor(n(nm), sh, F32))
        w_parts = {w: [sb(f"w{w}_{x}", [P, 2048], F32R) for x in ("hi", "lo")] for w in ("q", "k", "v", "o")}
        split = lambda w: [t[:].rearrange("p (c n) -> p c n", c=(PAIRS if w == "o" else DC)) for t in w_parts[w]]
        wq, wk, wv, wo = (split(w) for w in ("q", "k", "v", "o"))
        cos, sin = sb("cos", [P, S]), sb("sin", [P, S])
        bq, bqs, bk = sb("bq", [P, PAIRS]), sb("bqs", [P, PAIRS]), sb("bk", [P, PAIRS])
        bv, bo = sb("bv", [P, AW]), sb("bo", [P, D])
        identb, masked = sb("identb", [P, P], BF16), sb("masked", [P, P], BF16)
        xin, xres = (sb(x, [P, TT, D]) for x in ("x", "xres"))
        stats, mv, veps, rstd = sb("st", [P, TT, 6]), sb("mv", [P, TT, 2]), sb("ve", [P, TT]), sb("rs", [P, TT])
        xT = [sb(f"xT_{x}", [P, DC, S], F32R) for x in ("hi", "lo")]
        v = sb("v_sb", [P, TT, AW])
        z, zs = sb("z_sb", [P, 2, S]), sb("zs", [P, 2, S])
        qz = [sb(f"qz_{x}", [P, 2, S], F32R) for x in ("hi", "lo")]
        kT = [sb(f"kT_{x}", [P, 2, S], F32R) for x in ("hi", "lo")]
        of_head = lambda hh: slice(hh * ADH, (hh + 1) * ADH)
        prob = sb("prob", [P, 4, FULL])
        nmax, sums, rinv = (sb(x, [P, 2, TT]) for x in ("nmax", "sums", "rinv"))
        probT = sb("probT", [P, 2, FULL])
        oT = [sb(f"oT_{x}", [P, PAIRS, S], F32R) for x in ("hi", "lo")]
        ps_s = [pb(f"ps_s{i}", [P, S]) for i in range(TT)]
        ps_z = [pb(f"ps_z{i}", [P, S]) for i in range(2)]
        ps_pt, ps_pv = pb("ps_pt", [P, S]), pb("ps_pv", [P, S])
        w_stage = [t[:].rearrange("p h n -> p (h n)")[:, at:at + 2048] for t in (prob, v) for at in (0, 2048)]
        block = s.enter_context(nc.Block())

        def products(ps, lhs, rhs):
            terms = [(a, b, ch) for a, b in ((0, 0), (0, 1), (1, 0)) for ch in range(len(lhs[0]))]
            for i, (a, b, ch) in enumerate(terms):
                last = nc.tensor.matmul(ps, lhs[a][ch], rhs[b][ch], start=(i == 0), stop=(i == len(terms) - 1))
            return last

        @block.sync
        def _(sp):
            tiles = lambda dram, j: dram[j].rearrange("(i p) d -> p i d", p=P)
            sp.dma_start(xin[:], tiles(x_dram, 0)).then_inc(x_in.sem, 16)

            def weights(i, w):
                sp.dma_start(w_stage[i].rearrange("p (c n) -> p c n", c=PAIRS if w == "o" else DC),
                             io["a_W" + w].rearrange("(c p) n -> p c n", p=P)).then_inc(w_in[i], 16)

            for i, w in enumerate("qk"):
                weights(i, w)
            for dst, src in ((bq[:], io["a_bq"]), (bk[:], io["a_bk"]), (cos[:], io["cos"]), (sin[:], io["sin"]),
                             (identb[:], io["identb"]), (masked[:], io["masked"]), (bv[:], io["a_bv"]), (bo[:], io["a_bo"])):
                sp.dma_start(dst, src).then_inc(tab_in, 16)
            for i, w in enumerate("vo"):
                weights(2 + i, w)
            for h in ffn_sems:
                sp.sem_clear(h)

            def body(j, last=False):
                if not last:
                    hold(g, sp, xt_mm.sem, xt_mm.at(j, DC))
                    sp.dma_start(xin[:], tiles(x_dram, j + 1)).then_inc(x_in.sem, 16)
                hold(g, sp, out_s.sem, out_s.at(j, 0))
                sp.dma_start(xres[:], tiles(x_dram, j)).then_inc(xres_in.sem, 16)
                hold(g, sp, xo_s.sem, xo_s.at(j, 2))
                sp.dma_start(tiles(out_dram, j), xres[:]).then_inc(out_s.sem, 16)

            with sp.Fori(0, B - 1) as j:
                body(j)
            body(B - 1, last=True)
            sp.wait_ge(out_s.sem, out_s.at(B - 1, 16))

        @block.gpsimd
        def _(pool):
            nc.gpsimd.memset(z[:, 0, :], 0.0).then_inc(zero_s, 1)
            pool.sem_inc(cos_s.sem, 2 * PAIRS)
            pool.sem_inc(sin_s.sem, 2 * PAIRS)
            pool.sem_inc(rk_s.sem, 1)
            pool.wait_ge(tab_in, 16 * 8)

            def rotate(j, p):
                for i in range(2):
                    m = 2 * p + i + 1
                    pool.wait_ge(shuf_s.sem, shuf_s.at(j, m))
                    nc.gpsimd.tensor_tensor(z[:, i, :], z[:, i, :], cos[:], ALU.mult).then_inc(cos_s.sem, 1)
                    nc.gpsimd.tensor_tensor(zs[:, i, :], zs[:, i, :], sin[:], ALU.mult).then_inc(sin_s.sem, 1)
                    pool.wait_ge(sin_s.sem, sin_s.at(j, m))
                    nc.gpsimd.tensor_tensor(z[:, i, :], z[:, i, :], zs[:, i, :], ALU.add).then_inc(sum_s.sem, 1)

            def key_low(j, p):
                pool.wait_ge(khi_s.sem, khi_s.at(j, p + 1))
                nc.gpsimd.tensor_tensor(kT[1][:, p % 2, :], z[:, 1, :], kT[0][:, p % 2, :].bitcast(F32), ALU.subtract)\
                    .then_inc(rk_s.sem, 1)

            def residual(j, i):
                pool.wait_ge(xres_in.sem, xres_in.at(j, 16))
                nc.gpsimd.tensor_tensor(xres[:, i, :], xres[:, i, :], bo[:], ALU.add).then_inc(xb_s.sem, 1)

            def slots(j, heads, last=False):
                for h in heads:
                    if h % 2 == 0:
                        key_low(j, h // 2)
                    if h in (6, 8, 12, 14):
                        residual(j, (6, 8, 12, 14).index(h))
                    if not last and h == 10:
                        layernorm_rstd(nc, g, pool, mv, veps, rstd, TT, mom_s, veps_s, rstd_s, j + 1)
                    if h % 2 == 0 and h // 2 + 1 < PAIRS:
                        rotate(j, h // 2 + 1)
                    if not last and h == AH - 2:
                        rotate(j + 1, 0)

            layernorm_rstd(nc, g, pool, mv, veps, rstd, TT, mom_s, veps_s, rstd_s, 0)
            rotate(0, 0)
            slots(0, range(4))
            with pool.Fori(0, B - 1) as j:
                slots(j, range(4, AH))
                slots(j + 1, range(4))
            slots(B - 1, range(4, AH), last=True)

        @block.vector
        def _(dve):
            dve.sem_inc(xn_s.sem, TT)
            dve.sem_inc(shuf_s.sem, 2 * PAIRS)
            dve.sem_inc(rq_s.sem, 2)
            dve.sem_inc(olo_s.sem, 1)
            dve.sem_inc(xo_s.sem, 2)

            def weight_low(i):
                dve.wait_ge(w_hi, i + 1)
                hi, lo = w_parts["qkvo"[i]]
                nc.vector.tensor_tensor(lo[:], w_stage[i], hi[:].bitcast(F32), ALU.subtract).then_inc(w_lo, 1)

            def statistics(j, i):
                if i == 0:
                    dve.wait_ge(x_in.sem, x_in.at(j, 16))
                    dve.wait_ge(xn_s.sem, xn_s.at(j, 0))
                nc.vector.bn_stats(stats[:, i, :], xin[:, i, :]).then_inc(stats_s.sem, 1)

            def moments(j):
                hold(g, dve, stats_s.sem, stats_s.at(j, TT))
                for i in range(TT):
                    nc.vector.bn_aggr(mv[:, i, :], stats[:, i, :]).then_inc(mom_s.sem, 1)

            def normalise(j, i):
                dve.wait_ge(rstd_s.sem, rstd_s.at(j, 1))
                dve.wait_ge(xt_mm.sem, xt_mm.at(j, 0))
                nc.vector.tensor_scalar(xin[:, i, :], xin[:, i, :], mv[:, i, 0:1], rstd[:, i:i + 1],
                                        ALU.subtract, ALU.mult).then_inc(xn_s.sem, 1)

            def x_low(j):
                for ch in range(DC):
                    dve.wait_ge(xhi_s.sem, xhi_s.at(j, ch + 1))
                    nc.vector.tensor_tensor(xT[1][:, ch, :], ps_z[ch][:], xT[0][:, ch, :].bitcast(F32), ALU.subtract)\
                        .then_inc(xlo_s.sem, 1)

            def values(j, ms):
                for m in ms:
                    if m == 0:
                        dve.wait_ge(pv_mm.sem, pv_mm.at(j, 0))
                    dve.wait_ge(v_mm.sem, v_mm.at(j, m + 1))
                    i, half = m // 2, m % 2
                    nc.vector.tensor_tensor(v[:, i, half * 512:(half + 1) * 512], ps_z[m % 2][:],
                                            bv[:, half * 512:(half + 1) * 512], ALU.add).then_inc(v_s.sem, 1)

            def result(j, i):
                dve.wait_ge(xb_s.sem, xb_s.at(j, TT))
                dve.wait_ge(wo_mm.sem, wo_mm.at(j, i + 1))
                t = xres[:, 2 * i:2 * i + 2, :]
                nc.vector.tensor_tensor(t, ps_z[i][:].rearrange("p (i d) -> p i d", i=2), t, ALU.add).then_inc(xo_s.sem, 1)

            def swap(j, p, i):
                hold(g, dve, z_s.sem, z_s.at(j, 2 * p + i + 1))
                nc.vector.stream_shuffle(zs[:, i, :], z[:, i, :], mask=[k ^ 16 for k in range(32)]).then_inc(shuf_s.sem, 1)

            def query_low(j, p, hh):
                dve.wait_ge(qhi_s.sem, qhi_s.at(j, 2 * p + hh + 1))
                at = of_head(hh)
                nc.vector.tensor_tensor(qz[1][at, hh, :], z[at, 0, :], qz[0][at, hh, :].bitcast(F32), ALU.subtract)\
                    .then_inc(rq_s.sem, 1)

            def largest(j, h, i):
                qt = TT - 1 - i
                dve.wait_ge(s_mm.sem, s_mm.at(j, 4 * h + i + 1))
                nc.vector.tensor_reduce(nmax[:, h % 2, qt:qt + 1], ps_s[qt][:, 0:(qt + 1) * P], AX.X, ALU.max, negate=True)\
                    .then_inc(max_s.sem, 1)

            def scale(j, h):
                dve.wait_ge(exp_s.sem, exp_s.at(j, 4 * h + 4))
                nc.vector.reciprocal(rinv[:, h % 2, :], sums[:, h % 2, :]).then_inc(rec_s.sem, 1)
                dve.wait_ge(rec_s.sem, rec_s.at(j, h + 1))
                for qt in range(TT):
                    t = prob[:, h % 4, PLACE[qt]]
                    nc.vector.tensor_scalar(t, t, rinv[:, h % 2, qt:qt + 1], None, ALU.mult).then_inc(p_s.sem, 1)

            def low_part(j, p):
                dve.wait_ge(ohi_s.sem, ohi_s.at(j, p + 1))
                nc.vector.tensor_tensor(oT[1][:, p, :], ps_pv[:], oT[0][:, p, :].bitcast(F32), ALU.subtract).then_inc(olo_s.sem, 1)

            def slots(j, heads, first=False, last=False):
                for h in heads:
                    p = h // 2
                    more = p + 1 < PAIRS or not last
                    nxt = (j, p + 1) if p + 1 < PAIRS else (j + 1, 0)
                    if h % 2 == 0:
                        if h > 0:
                            scale(j, h - 1)
                        elif not first:
                            scale(j - 1, AH - 1)
                        query_low(j, p, 1)
                        if h >= 4:
                            low_part(j, p - 2)
                        elif not first:
                            low_part(j - 1, PAIRS - 2 + p)
                        for i in range(TT):
                            largest(j, h, i)
                            if i < 2 and more:
                                swap(*nxt, i)
                    else:
                        for i in range(TT):
                            if h == V_SLOT and i < 2:
                                values(j, range(4 * i, 4 * i + 4))
                            if h == V_SLOT and i >= 2 and not first:
                                result(j - 1, i - 2)
                            largest(j, h, i)
                            if not last:
                                if h in (5, 7) and i < 2:
                                    statistics(j + 1, h - 5 + i)
                                if h == 9 and i == 0:
                                    moments(j + 1)
                                if h == 11:
                                    normalise(j + 1, i)
                                if h == X_SLOT and i == 0:
                                    x_low(j + 1)
                        scale(j, h - 1)
                        if more:
                            query_low(*nxt, 0)

            for i in range(TT):
                statistics(0, i)
            moments(0)
            for i in range(2):
                weight_low(i)
            for i in range(TT):
                normalise(0, i)
            dve.wait_ge(tab_in, 16 * 8)
            nc.vector.tensor_scalar(bqs[:], bq[:], ADH ** -0.5, None, ALU.mult).then_inc(bqs_s, 1)
            x_low(0)
            for i in range(2):
                swap(0, 0, i)
            query_low(0, 0, 0)
            for i in range(2, 4):
                weight_low(i)
            slots(0, range(4), first=True)
            with dve.Fori(0, B - 1) as j:
                slots(j, range(4, AH))
                slots(j + 1, range(4))
            slots(B - 1, range(4, AH), last=True)
            scale(B - 1, AH - 1)
            for p in (PAIRS - 2, PAIRS - 1):
                low_part(B - 1, p)
            for i in range(2):
                result(B - 1, i)

        @block.scalar
        def _(act):
            act.sem_inc(exp_s.sem, 4)
            act.sem_inc(out_s.sem, 16)
            act.sem_inc(pt_s.sem, 1)
            act.sem_inc(z_s.sem, 2 * PAIRS)

            def weight_high(i):
                act.wait_ge(w_in[i], 16)
                nc.scalar.copy(w_parts["qkvo"[i]][0][:], w_stage[i]).then_inc(w_hi, 1)

            def x_high(j):
                for ch in range(DC):
                    act.wait_ge(xt_mm.sem, xt_mm.at(j, ch + 1))
                    nc.scalar.copy(xT[0][:, ch, :], ps_z[ch][:]).then_inc(xhi_s.sem, 1)

            def project(j, p, i):
                act.wait_ge(z_mm.sem, z_mm.at(j, 2 * p + i + 1))
                act.wait_ge((rq_s, rk_s)[i].sem, (rq_s.at(j, 2 * p), rk_s.at(j, p))[i])
                nc.scalar.activation(z[:, i, :], ps_z[i][:], ACT.Identity, bias=(bqs, bk)[i][:, p:p + 1],
                                     scale=(ADH ** -0.5, 1.0)[i]).then_inc(z_s.sem, 1)

            def query_high(j, p, hh):
                act.wait_ge(sum_s.sem, sum_s.at(j, 2 * p + 1))
                act.wait_ge(s_mm.sem, s_mm.at(j, 8 * (p - 1) + 4 * (hh + 1)))
                nc.scalar.copy(qz[0][of_head(hh), hh, :], z[of_head(hh), 0, :]).then_inc(qhi_s.sem, 1)

            def key_high(j, p):
                act.wait_ge(sum_s.sem, sum_s.at(j, 2 * p + 2))
                act.wait_ge(s_mm.sem, s_mm.at(j, 8 * (p - 1)))
                nc.scalar.copy(kT[0][:, p % 2, :], z[:, 1, :]).then_inc(khi_s.sem, 1)

            def exps(j, h, i):
                qt = TT - 1 - i
                act.wait_ge(max_s.sem, max_s.at(j, 4 * h + i + 1))
                act.wait_ge(pt_mm.sem, pt_mm.at(j, NT * (h - 3)))
                nc.scalar.activation(prob[:, h % 4, PLACE[qt]], ps_s[qt][:, 0:(qt + 1) * P], ACT.Exp,
                                     bias=nmax[:, h % 2, qt:qt + 1], accum_out=sums[:, h % 2, qt:qt + 1]).then_inc(exp_s.sem, 1)

            def copy_pt(j, h, turn):
                width, at = sum(WIDTH[kb] for kb in TURNS[turn]), OFF[TURNS[turn][0]]
                act.wait_ge(pv_mm.sem, pv_mm.at(j, h // 2))
                act.wait_ge(pt_mm.sem, pt_mm.at(j, NT * h + turn + 1))
                nc.scalar.copy(probT[:, h % 2, at:at + width], ps_pt[:, 0:width]).then_inc(pt_s.sem, 1)

            def high_part(j, p):
                act.wait_ge(pv_mm.sem, pv_mm.at(j, p + 1))
                act.wait_ge(wo_mm.sem, wo_mm.at(j, 0))
                nc.scalar.copy(oT[0][:, p, :], ps_pv[:]).then_inc(ohi_s.sem, 1)

            def slots(j, heads, first=False, last=False):
                for h in heads:
                    p = h // 2
                    more = p + 1 < PAIRS or not last
                    nxt = (j, p + 1) if p + 1 < PAIRS else (j + 1, 0)
                    before = (j, h - 1) if h else (j - 1, AH - 1)
                    turned = (j, h - 2) if h >= 2 else (j - 1, AH + h - 2)
                    exps_before, turns = h > 0 or not first, h >= 2 or not first
                    if h % 2 == 0:
                        if exps_before:
                            for i in (2, 3):
                                exps(*before, i)
                        key_high(j, p)
                        query_high(j, p, 1)
                        if h >= 4:
                            high_part(j, p - 2)
                        elif not first:
                            high_part(j - 1, PAIRS - 2 + p)
                        if more:
                            project(*nxt, 0)
                        if turns:
                            copy_pt(*turned, 0)
                        exps(j, h, 0)
                        if turns:
                            copy_pt(*turned, 1)
                        if more:
                            project(*nxt, 1)
                    else:
                        if h == X_SLOT and not last:
                            x_high(j + 1)
                        if turns:
                            copy_pt(*turned, 0)
                        exps(*before, 2)
                        if turns:
                            copy_pt(*turned, 1)
                        exps(*before, 3)
                    if turns:
                        copy_pt(*turned, 2)
                    if h % 2 == 1:
                        exps(j, h, 0)
                    exps(j, h, 1)
                    if h % 2 == 1 and more:
                        query_high(*nxt, 0)

            act.wait_ge(zero_s, 1)
            for part in qz:
                for hh in range(2):
                    nc.scalar.copy(part[:, hh, :], z[:, 0, :])
            for i in range(2):
                weight_high(i)
            x_high(0)
            act.wait_ge(bqs_s, 1)
            for i in range(2):
                project(0, 0, i)
            query_high(0, 0, 0)
            for i in range(2, 4):
                weight_high(i)
            slots(0, range(4), first=True)
            with act.Fori(0, B - 1) as j:
                slots(j, range(4, AH))
                slots(j + 1, range(4))
            slots(B - 1, range(4, AH), last=True)
            for i in (2, 3):
                exps(B - 1, AH - 1, i)
            high_part(B - 1, PAIRS - 2)
            for h in (AH - 2, AH - 1):
                for turn in range(NT):
                    copy_pt(B - 1, h, turn)
            high_part(B - 1, PAIRS - 1)

        @block.tensor
        def _(pe):
            pe.sem_inc(xt_mm.sem, DC)
            pe.sem_inc(z_mm.sem, 2 * PAIRS)
            pe.sem_inc(s_mm.sem, 9)
            pe.sem_inc(pt_mm.sem, NT * AH)
            pe.sem_inc(pv_mm.sem, 1)
            pe.sem_inc(wo_mm.sem, 2)
            pe.wait_ge(tab_in, 16 * 8)

            def transpose_x(j, ch):
                pe.wait_ge(xn_s.sem, xn_s.at(j, TT))
                pe.wait_ge(z_s.sem, z_s.at(j, ch - 1))
                for i in range(TT):
                    last = nc.tensor.transpose(ps_z[ch][:, i * P:(i + 1) * P], xin[:, i, ch * P:(ch + 1) * P], g.ident[:])
                last.then_inc(xt_mm.sem, 1)

            def project(j, p, i):
                if p == 0:
                    pe.wait_ge(xlo_s.sem, xlo_s.at(j, DC))
                elif p == 3:
                    pe.wait_ge(v_s.sem, v_s.at(j, 2 * TT - 1 + i))
                    pe.wait_ge(xo_s.sem, xo_s.at(j, i - 1))
                else:
                    pe.wait_ge(z_s.sem, z_s.at(j, 2 * p - 1 + i))
                w = (wq, wk)[i]
                products(ps_z[i][:], [[part[:, ch, p * P:(p + 1) * P] for ch in range(DC)] for part in w],
                         [[part[:, ch, :] for ch in range(DC)] for part in xT]).then_inc(z_mm.sem, 1)

            def values(j, ms):
                for m in ms:
                    i, half = m // 2, m % 2
                    if m < 2:
                        pe.wait_ge(z_s.sem, z_s.at(j, 5 + m))
                    else:
                        pe.wait_ge(v_s.sem, v_s.at(j, m - 1))
                    products(ps_z[m % 2][:], [[part[:, ch, i * P:(i + 1) * P] for ch in range(DC)] for part in xT],
                             [[part[:, ch, half * 512:(half + 1) * 512] for ch in range(DC)] for part in wv]).then_inc(v_mm.sem, 1)

            def scores(j, h, i):
                p, hh = h // 2, h % 2
                qt, width = TT - 1 - i, (TT - i) * P
                if i == 0:
                    pe.wait_ge(rq_s.sem, rq_s.at(j, h + 1))
                    pe.wait_ge(rk_s.sem, rk_s.at(j, p + 1))
                pe.wait_ge(exp_s.sem, exp_s.at(j, 4 * (h - 1) + i + 1))
                wide = max(width, 2 * P)
                for n, (a, b) in enumerate(((0, 0), (0, 1), (1, 0))):
                    nc.tensor.matmul(ps_s[qt][:, 0:wide], qz[a][:, hh, qt * P:(qt + 1) * P], kT[b][:, p % 2, 0:wide],
                                     start=(n == 0), stop=False)
                nc.tensor.matmul(ps_s[qt][:, qt * P:width], identb[:], masked[:], start=False, stop=True).then_inc(s_mm.sem, 1)

            def transposes(j, h, turn):
                if turn == 0:
                    pe.wait_ge(p_s.sem, p_s.at(j, 4 * h + 4))
                pe.wait_ge(pt_s.sem, pt_s.at(j, NT * h + turn))
                for kb in TURNS[turn]:
                    for qt in range(kb, TT):
                        at = OFF[kb] - OFF[TURNS[turn][0]] + (qt - kb) * P
                        last = nc.tensor.transpose(ps_pt[:, at:at + P], prob[:, h % 4, PLACE[qt]][:, kb * P:(kb + 1) * P], g.ident[:])
                last.then_inc(pt_mm.sem, 1)

            def mix(j, p):
                pe.wait_ge(pt_s.sem, pt_s.at(j, 2 * NT * (p + 1)))
                pe.wait_ge(olo_s.sem, olo_s.at(j, p))
                if p == 0:
                    pe.wait_ge(v_s.sem, v_s.at(j, 2 * TT))
                for kb in range(TT):
                    for hh in range(2):
                        h = 2 * p + hh
                        last = nc.tensor.matmul(ps_pv[hh * ADH:(hh + 1) * ADH, kb * P:S], v[:, kb, h * ADH:(h + 1) * ADH],
                                                probT[:, hh, OFF[kb]:OFF[kb] + WIDTH[kb]], start=(kb == 0), stop=(kb == TT - 1))
                last.then_inc(pv_mm.sem, 1)

            def output(j, i, last=False):
                pe.wait_ge(olo_s.sem, olo_s.at(j, PAIRS))
                if last:
                    pe.wait_ge(z_s.sem, z_s.at(j, 2 * PAIRS - 1 + i))
                else:
                    pe.wait_ge(v_s.sem, v_s.at(j + 1, 2 * TT - 1 + i))
                for t in range(2):
                    at = slice((2 * i + t) * P, (2 * i + t + 1) * P)
                    out = products(ps_z[i][:, t * D:(t + 1) * D], [[part[:, p, at] for p in range(PAIRS)] for part in oT],
                                   [[part[:, p, :] for p in range(PAIRS)] for part in wo])
                out.then_inc(wo_mm.sem, 1)

            def slots(j, heads, first=False, last=False):
                for h in heads:
                    p = h // 2
                    more = h % 2 == 0 and (p + 1 < PAIRS or not last)
                    nxt = (j, p + 1) if p + 1 < PAIRS else (j + 1, 0)
                    turned = (j, h - 2) if h >= 2 else (j - 1, AH + h - 2)
                    if h % 2 == 0:
                        if h >= 4:
                            mix(j, p - 2)
                        elif not first:
                            mix(j - 1, PAIRS - 2 + p)
                    if h == X_SLOT and not last:
                        for ch in range(DC):
                            transpose_x(j + 1, ch)
                    for i in range(TT):
                        if more and i < 2:
                            project(*nxt, i)
                        if h == V_SLOT and i < 2:
                            values(j, range(4 * i, 4 * i + 4))
                        if h == V_SLOT and i >= 2 and not first:
                            output(j - 1, i - 2)
                        if i < NT and (h >= 2 or not first):
                            transposes(*turned, i)
                        scores(j, h, i)

            for ch in range(DC):
                transpose_x(0, ch)
            pe.wait_ge(w_lo, 2)
            for i in range(2):
                project(0, 0, i)
            slots(0, range(3), first=True)
            pe.wait_ge(w_lo, 4)
            slots(0, range(3, 4), first=True)
            with pe.Fori(0, B - 1) as j:
                slots(j, range(4, AH))
                slots(j + 1, range(4))
            slots(B - 1, range(4, AH), last=True)
            mix(B - 1, PAIRS - 2)
            for h in (AH - 2, AH - 1):
                for turn in range(NT):
                    transposes(B - 1, h, turn)
            mix(B - 1, PAIRS - 1)
            for i in range(2):
                output(B - 1, i, last=True)


class ExpertRing:

    def __init__(self, sb):
        self.w1, self.wg = sb("w1", [P, 2, 2, DC, F]), sb("wg", [P, 2, 2, DC, F])
        self.w2 = sb("w2", [P, 2, 2, FK, D])
        self.b1, self.bg = sb("b1", [2 * QUAD, 2, F]), sb("bg", [2 * QUAD, 2, F])


class Shared:
    pass


def macaron_block(nc, io):
    sems = ExitStack()
    with sems, ExitStack() as s:
        made = {}

        def sem(name):
            if name not in made:
                made[name] = sems.enter_context(nc.semaphore(name))
            return made[name]

        sb = lambda nm, sh: s.enter_context(nc.sbuf_tensor("sh_" + nm, sh, F32))
        g = Shared()
        g.ident, g.blkmask = sb("ident", [P, P]), sb("blkmask", [P, P])
        g.mhalf = sb("mhalf", [P, TT])
        g.G, g.cb = sb("G", [P, DC, HS]), sb("cb", [P, DC])
        g.wv_pad, g.bv_pad = sb("wv_pad", [P, DC, FH, QUAD]), sb("bv_pad", [P, 4])
        g.wo_pad = sb("wo_pad", [P, 4, D])
        g.cwqT, g.cwo = sb("cwqT", [P, DC, D]), sb("cwo", [P, DC, D])
        x1 = nc.dram_tensor("x_after_ffn", (B, S, D), F32, kind="Internal").ap()
        x2 = nc.dram_tensor("x_after_attention", (B, S, D), F32, kind="Internal").ap()
        mhalf_s = sem("mhalf")
        g.held = sem("held")
        with nc.Block() as block:
            @block.gpsimd
            def _(pool):
                nc.gpsimd.memset(g.mhalf[:], -0.5).then_inc(mhalf_s, 1)
                pool.wait_ge(mhalf_s, 1)
        setup_phase(nc, io, g, sem)

        def ffn(f, src, dst):
            with ExitStack() as t:
                kT = t.enter_context(nc.sbuf_tensor(f"ffn{f}_kT", [P, DC, NS, B], F32))
                vT = t.enter_context(nc.sbuf_tensor(f"ffn{f}_vT", [P, DC, NS, B], F32))
                with ExitStack() as u:
                    at_all = u.enter_context(nc.sbuf_tensor(f"ffn{f}_at", [P, DC, HS, B], F32))
                    ring = ExpertRing(lambda n, sh: u.enter_context(nc.sbuf_tensor(f"ffn{f}_{n}", sh, F32)))
                    w_in = [[sem(f"ex_{w}_in{i}") for i in range(2)] for w in ("w1", "wg", "w2")]
                    dispatch_phase(nc, io, g, sem, f, src, at_all, ring, w_in)
                    expert_phase(nc, io, g, sem, f, at_all, kT, vT, ring, w_in)
                combine_phase(nc, io, g, sem, f, src, dst, kT, vT)

        ffn(0, io["x"], x1)
        ffn_sems = [h for k, h in made.items() if k.startswith(("dis_", "ex_", "com_"))]
        attention_phase(nc, io, g, sem, x1, x2, ffn_sems)
        ffn(1, x2, io["out"])



def _rotary_order():
    half = ADH // 2
    return np.concatenate([np.arange(0, 16), half + np.arange(0, 16), np.arange(16, 32), half + np.arange(16, 32)])


def _rotary_tables():
    inv = (np.float32(1.0) / np.float32(10000.0) ** (np.arange(0, ADH, 2, dtype=np.float32) / np.float32(ADH))).astype(np.float32)
    ang = np.arange(S, dtype=np.float32)[:, None] * inv[None, :]
    order = _rotary_order()
    freq, sign = order % (ADH // 2), np.where(order < ADH // 2, -1.0, 1.0).astype(np.float32)
    cos, sin = np.cos(ang)[:, freq].T, np.sin(ang)[:, freq].T * sign[:, None]
    return (np.ascontiguousarray(np.tile(t, (2, 1)).astype(np.float32)) for t in (cos, sin))


def kernel(**inputs):
    import concourse.bacc as bacc
    from concourse.bass_utils import run_bass_kernel_spmd
    import ml_dtypes

    a = {k.replace("L0_attn_", "a_").replace("L0_ffn_", ""): np.ascontiguousarray(v) for k, v in inputs.items()}
    cols = lambda v: np.ascontiguousarray(v.reshape(-1, P).T)
    rows = lambda v: np.ascontiguousarray(np.broadcast_to(v, (P,) + v.shape))
    byexp = lambda v: np.ascontiguousarray(v.reshape(NE, DC, P).transpose(2, 1, 0))
    pairs = lambda v: np.ascontiguousarray(np.broadcast_to(v[:, None, :], (NE, QUAD, F)).reshape(NE // 2, 2 * QUAD, F))
    order = _rotary_order()
    perm = lambda v: np.ascontiguousarray(v.reshape(-1, AH, ADH)[:, :, order].reshape(v.shape))
    cos, sin = _rotary_tables()
    bv_pad = np.zeros((4, 4, QUAD), np.float32)
    bv_pad[:, :, :FDH] = a["d_bv"].reshape(4, 4, FDH)
    wk, wv = a["a_Wkv"][:, :AW], a["a_Wkv"][:, AW:]
    arrays = {
        "x": a["a_x"], "sqT": np.ascontiguousarray(a["slot_query"].reshape(NS, DC, P).transpose(2, 1, 0)),
        "sq_rows": np.repeat(a["slot_query"][0], B, axis=0),
        "d_Wq": a["d_Wq"], "d_WkT": np.ascontiguousarray(a["d_Wk"].T), "d_Wv": a["d_Wv"], "d_Wo": a["d_Wo"],
        "d_bq": cols(a["d_bq"]), "d_bk": cols(a["d_bk"]), "d_bv_pad": np.ascontiguousarray(bv_pad.reshape(4, P).T),
        "d_bo": rows(a["d_bo"]),
        "c_WqT": np.ascontiguousarray(a["c_Wq"].T), "c_Wk": a["c_Wk"], "c_Wv": a["c_Wv"], "c_Wo": a["c_Wo"],
        "c_bq": np.ascontiguousarray(np.repeat(cols(a["c_bq"])[:, :, None], P, axis=2)),
        "c_bk": cols(a["c_bk"]), "c_bv": cols(a["c_bv"]),
        "c_bo": np.ascontiguousarray(np.broadcast_to(a["c_bo"], (P, 2, D))),
        "e_gT": byexp(a["e_ln_g"]), "e_bT": byexp(a["e_ln_b"]), "e_b2T": byexp(a["e_b2"]),
        "e_W1": a["e_W1"], "e_Wg": a["e_Wg"], "e_W2": a["e_W2"], "e_b1": pairs(a["e_b1"]), "e_bg": pairs(a["e_bg"]),
        "a_Wq": perm(a["a_Wq"]), "a_Wk": perm(np.ascontiguousarray(wk)), "a_Wv": np.ascontiguousarray(wv), "a_Wo": a["a_Wo"],
        "a_bq": cols(perm(a["a_bq"])), "a_bk": cols(perm(np.ascontiguousarray(a["a_bkv"][:AW]))),
        "a_bv": rows(np.ascontiguousarray(a["a_bkv"][AW:])), "a_bo": rows(a["a_bo"]),
        "cos": cos, "sin": sin, "ident": np.eye(P, dtype=np.float32), "identb": np.eye(P).astype(ml_dtypes.bfloat16),
        "blkmask": np.repeat(np.repeat(np.eye(HPC, dtype=np.float32), FDH, axis=0), NS, axis=1),
        "masked": np.where(np.arange(P)[None, :] > np.arange(P)[:, None], MASKED, 0.0).astype(ml_dtypes.bfloat16),
    }
    nc = bacc.Bacc("TRN2", target_bir_lowering=False, num_devices=1)
    io = {k: nc.dram_tensor("in_" + k, v.shape, mybir.dt.from_np(v.dtype), kind="ExternalInput").ap() for k, v in arrays.items()}
    io["out"] = nc.dram_tensor("out_x", (B, S, D), F32, kind="ExternalOutput").ap()
    macaron_block(nc, io)
    r = run_bass_kernel_spmd(nc, [{"in_" + k: v for k, v in arrays.items()}], core_ids=[0])
    return r.results[0]["out_x"]
```
